# Optimizing a Trainium2 kernel written in Bass

```python
import numpy as np
import jax
import jax.numpy as jnp

def _softmax(x, axis=-1):
    return jax.nn.softmax(x, axis=axis)

def _gelu(x):
    return jax.nn.gelu(x, approximate=True)

def _silu(x):
    return jax.nn.silu(x)

def _sigmoid(x):
    return jax.nn.sigmoid(x)

def _layernorm(x, axis=-1, eps=1e-05):
    m = jnp.mean(x, axis=axis, keepdims=True)
    v = jnp.var(x, axis=axis, keepdims=True)
    return (x - m) / jnp.sqrt(v + eps)

def _scatter_add(tgt, idx, src, axis=0):
    return tgt.at[idx].add(src)

def _segment_sum(src, seg, n):
    return jax.ops.segment_sum(src, seg, n)
kernel_name = 'mk_flamingo_gated_d1_seqx_r4_a57a69'

def setup_inputs(seed: int=0):
    np.random.seed(seed)
    _w = jnp.asarray

    def _rec_inputs():
        import jax
        import jax.numpy as jnp
        _rk = jax.random.key(seed)
        x = -0.0002928 + 1 * jax.random.normal(jax.random.fold_in(_rk, 1), (1, 2048, 256), jnp.float32)
        _lenS = 2048 - jax.random.randint(jax.random.fold_in(_rk, 7), (1,), 0, max(1, 2048 // 4) + 1, jnp.int32)
        _lenS2 = 1601 - jax.random.randint(jax.random.fold_in(_rk, 8), (1,), 0, max(1, 1601 // 4) + 1, jnp.int32)
        _ctx_1024P = jax.random.normal(jax.random.fold_in(_rk, 11), (1, 16, 256), jnp.float32)
        _ctx_1024c = jax.random.dirichlet(jax.random.fold_in(_rk, 511), 0.3 * jnp.ones((16,), jnp.float32), (1, 1601))
        _ctx_1024t = jnp.einsum('bsk,bkd->bsd', _ctx_1024c, _ctx_1024P)
        _ctx_1024t = _ctx_1024t * jax.lax.rsqrt(jnp.mean(jnp.square(_ctx_1024t)) + 1e-12) * 0.953939
        ctx_1024 = -1.39393e-06 + 0.999914 * (_ctx_1024t + 0.3 * jax.random.normal(jax.random.fold_in(_rk, 611), (1, 1601, 256), jnp.float32))
        _validS = jnp.arange(2048)[None, :] < _lenS[:, None]
        _validS2 = jnp.arange(1601)[None, :] < _lenS2[:, None]
        _causal = jnp.tril(jnp.ones((2048, 2048), dtype=bool))
        mask_1x1xSxS2_bk0 = jnp.logical_not(jnp.broadcast_to(_validS2[0:1, None, None, :], (1, 1, 2048, 1601)))
        _g = jax.random.normal(jax.random.fold_in(_rk, 9001), (2, 1), jnp.float32)
        _g = jnp.sign(_g) * jnp.maximum(jnp.abs(_g), 1.0) + (_g == 0) * 1.0
        g_xattn = _g[0]
        g_ffn = _g[1]
        return (x, ctx_1024, mask_1x1xSxS2_bk0, g_xattn, g_ffn)
    x, ctx_1024, mask_1x1xSxS2_bk0, g_xattn, g_ffn = _rec_inputs()

    def _L0_xattn_setup():
        import jax, jax.numpy as jnp
        import numpy as np
        B, T, D = (2, 512, 256)
        H, HD = (16, 64)
        key = jax.random.key(seed)
        ks = jax.random.split(key, 6)
        scale = 1.0 / np.sqrt(D)
        inputs_q = jax.random.normal(ks[0], (B, T, D), dtype=jnp.float32)
        inputs_kv = jax.random.normal(ks[1], (B, T, D), dtype=jnp.float32)
        mask = jnp.tril(jnp.ones((T, T), dtype=bool))[None, None, :, :]
        Wq = jax.random.normal(ks[2], (D, H * HD), dtype=jnp.float32) * scale
        Wk = jax.random.normal(ks[3], (D, H * HD), dtype=jnp.float32) * scale
        Wv = jax.random.normal(ks[4], (D, H * HD), dtype=jnp.float32) * scale
        Wo = jax.random.normal(ks[5], (H * HD, D), dtype=jnp.float32) * scale
        return {'inputs_q': inputs_q, 'inputs_kv': inputs_kv, 'mask': mask, 'Wq': Wq, 'Wk': Wk, 'Wv': Wv, 'Wo': Wo}
    _L0_xattn_all = _L0_xattn_setup()
    _L0_xattn_in = {k: v for k, v in _L0_xattn_all.items() if k in ('Wq', 'Wk', 'Wv', 'Wo')}
    del _L0_xattn_all

    def _L0_ffn_setup():
        import jax, jax.numpy as jnp
        import numpy as np
        B, S, D = (4, 256, 256)
        E, K = (8, 2)
        H = 2 * D
        key = jax.random.key(seed)
        ks = jax.random.split(key, 5)
        x = jax.random.normal(ks[0], (B, S, D), dtype=jnp.float32)
        Wg = jax.random.normal(ks[1], (E, D), dtype=jnp.float32) * 0.02
        W1 = jax.random.normal(ks[2], (E, H, D), dtype=jnp.float32) * 0.02
        W2 = jax.random.normal(ks[3], (E, H, D), dtype=jnp.float32) * 0.02
        W3 = jax.random.normal(ks[4], (E, D, H), dtype=jnp.float32) * 0.02
        return {'x': x, 'Wg': Wg, 'W1': W1, 'W2': W2, 'W3': W3}
    _L0_ffn_all = _L0_ffn_setup()
    _L0_ffn_in = {k: v for k, v in _L0_ffn_all.items() if k in ('Wg', 'W1', 'W2', 'W3')}
    del _L0_ffn_all
    return {'x': x, 'ctx_1024': ctx_1024, 'mask_1x1xSxS2_bk0': mask_1x1xSxS2_bk0, 'g_xattn': g_xattn, 'g_ffn': g_ffn, 'L0_xattn_Wq': _L0_xattn_in['Wq'], 'L0_xattn_Wk': _L0_xattn_in['Wk'], 'L0_xattn_Wv': _L0_xattn_in['Wv'], 'L0_xattn_Wo': _L0_xattn_in['Wo'], 'L0_ffn_Wg': _L0_ffn_in['Wg'], 'L0_ffn_W1': _L0_ffn_in['W1'], 'L0_ffn_W2': _L0_ffn_in['W2'], 'L0_ffn_W3': _L0_ffn_in['W3']}

def reference(x, ctx_1024, mask_1x1xSxS2_bk0, g_xattn, g_ffn, L0_xattn_Wq, L0_xattn_Wk, L0_xattn_Wv, L0_xattn_Wo, L0_ffn_Wg, L0_ffn_W1, L0_ffn_W2, L0_ffn_W3):
    import jax
    import jax.numpy as jnp

    def _L0_xattn_ref(inputs_q, inputs_kv, mask, Wq, Wk, Wv, Wo):
        import jax, jax.numpy as jnp
        import numpy as np
        B, T, D = (2, 512, 256)
        H, HD = (16, 64)
        b, t, _ = inputs_q.shape
        q = (inputs_q @ Wq).reshape(b, -1, H, HD)
        k = (inputs_kv @ Wk).reshape(b, -1, H, HD)
        v = (inputs_kv @ Wv).reshape(b, -1, H, HD)
        scores = jnp.einsum('bthd,bThd->bhtT', q, k) * (1.0 / jnp.sqrt(HD))
        scores = jnp.where(mask, scores, jnp.finfo(jnp.float32).min)
        attn = jax.nn.softmax(scores, axis=-1)
        out = jnp.einsum('bhtT,bThd->bthd', attn, v).reshape(b, t, H * HD)
        return out @ Wo

    def _L0_ffn_ref(x, Wg, W1, W2, W3):
        import jax, jax.numpy as jnp
        import numpy as np
        B, S, D = (4, 256, 256)
        E, K = (8, 2)
        H = 2 * D
        gate_out = jnp.einsum('bsd,ed->bse', x, Wg)
        top_v, top_i = jax.lax.top_k(gate_out, K)
        probs = jax.nn.softmax(top_v, axis=-1)
        out = jnp.zeros_like(x)
        for e in range(E):
            w_e = jnp.sum(probs * (top_i == e), axis=-1)
            h1 = jnp.einsum('bsd,hd->bsh', x, W1[e])
            h2 = jnp.einsum('bsd,hd->bsh', x, W2[e])
            g = h1 * jax.nn.sigmoid(h1) * h2
            y = jnp.einsum('bsh,dh->bsd', g, W3[e])
            out = out + y * w_e[..., None]
        return out
    x = x + jnp.tanh(g_xattn[0]) * _L0_xattn_ref(_layernorm(x, axis=-1), ctx_1024, mask_1x1xSxS2_bk0, L0_xattn_Wq, L0_xattn_Wk, L0_xattn_Wv, L0_xattn_Wo)
    x = x + jnp.tanh(g_ffn[0]) * _L0_ffn_ref(_layernorm(x, axis=-1), L0_ffn_Wg, L0_ffn_W1, L0_ffn_W2, L0_ffn_W3)
    return x

_drawn_inputs = setup_inputs


def setup_inputs(seed=0):
    import zlib

    import numpy as np

    out = dict(_drawn_inputs(seed))
    spreads = {}
    factors = {'L0_ffn_Wg': 5.688, 'L0_ffn_W1': 4.778, 'L0_ffn_W2': 4.734, 'L0_ffn_W3': 4.72}
    for name, (base, spread) in spreads.items():
        noise = np.random.default_rng([zlib.crc32(name.encode()), seed]).standard_normal(out[name].shape)
        drawn = base * np.exp(spread * noise) if base else spread * noise
        out[name] = jnp.asarray(drawn.astype(out[name].dtype))
    for name, factor in factors.items():
        out[name] = (out[name] * factor).astype(out[name].dtype)
    return out
```

```python
from contextlib import ExitStack

import concourse.bass as bass
from concourse import mybir

F32 = mybir.dt.float32
F32R = mybir.dt.float32r
BF16 = mybir.dt.bfloat16
I32 = mybir.dt.int32
U8 = mybir.dt.uint8
ALU = mybir.AluOpType
ACT = mybir.ActivationFunctionType
AX = mybir.AxisListType

P = 128
S = 2048
SK = 1601
D = 256
H = 16
HD = 64
KT = D // P
NT = S // P
DUMMY = NT
NB = 4
BK = 400
LASTK = SK - (NB - 1) * BK
LASTP = 404
NS = 4
STRIP = LASTP // NS
EVEN = LASTK + LASTK % 2
SKP = (NB - 1) * BK + LASTP
LAST0 = (NB - 1) * BK
VW = HD + 1
MASKED = float(2.0 ** 125)
EPS = 1e-5
NE = 8
FH = 512
HT = FH // P
REGION = S + P
NG = 2 * S // P + NE - 1
NSCHED = NG + 1


def block_of(b):
    last = b == NB - 1
    return b * BK, LASTK if last else BK, EVEN if last else BK, STRIP if last else BK // NS


def build(nc, x, ctxT, mask, g_xattn, g_ffn, Wq, Wk, Wv, Wo, WgT, W1T, W2T, W3T, out):
    with ExitStack() as ctx:
        def sb(name, shape, dt, scope=ctx):
            return scope.enter_context(nc.sbuf_tensor(name, shape, dt))

        def psum(name):
            return ctx.enter_context(nc.psum_tensor(name, [P, 512], F32))

        def sem(name):
            return ctx.enter_context(nc.semaphore(name))

        xs = sb("xs", [P, NT + 1, D], F32)
        xnT = sb("xnT", [P, KT, (NT + 1) * P], F32)
        ident = sb("ident", [P, P], F32)
        ones = sb("ones", [P, P], F32)
        before = sb("before", [P, P], F32)
        stat = sb("stat", [P, 4, NT], F32)
        gates = sb("gates", [P, 2], F32)
        tanh_g = sb("tanh_g", [P, 2], F32)
        rowflag = sb("rowflag", [P, 4], F32)
        plainflag = sb("plainflag", [1, 1], I32)
        wg_sb = sb("wg_sb", [P, KT, NE], F32)
        rank = sb("rank", [P, NE], F32)
        number = sb("number", [P, NE], F32)
        fill = sb("fill", [P, NT], F32)
        turn = sb("turn", [P, NSCHED], F32)
        with ExitStack() as attn:
            biases = sb("biases", [P, NT + 1, LASTK], BF16, attn)
            bias_cur = sb("bias_cur", [P, 2, LASTK], BF16, attn)
            q_parts = sb("q_parts", [P, H, P], F32R, attn)
            o_rows = sb("o_rows", [P, H * HD], F32, attn)
            oT = sb("oT", [P, H // 2, P], F32, attn)
            ctxT_sb = sb("ctxT_sb", [P, KT, SKP], F32, attn)
            wq_sb = sb("wq_sb", [P, KT, H * HD], F32, attn)
            wv_sb = sb("wv_sb", [P, KT, H * HD], F32, attn)
            wo_sb = sb("wo_sb", [P, H // 2, D], F32, attn)
            with ExitStack() as early:
                mask8 = sb("mask8", [P, NT, SKP], U8, early)
                xc = sb("xc", [P, NT, D], F32, early)
                sq = sb("sq", [P, NT, D], F32, early)
            with ExitStack() as fast:
                k_hi = sb("k_hi", [P, H, EVEN], F32R, fast)
                k_lo = sb("k_lo", [P, H, EVEN], F32R, fast)
                v_aug = sb("v_aug", [STRIP, NS, H, VW], F32, fast)
                wk2_sb = sb("wk2_sb", [P, KT, H, 2, HD], F32, fast)
                masked = sb("masked", [P, 2, LASTK], F32, fast)
                probs = sb("probs", [P, 2, LASTP], F32, fast)
                probsT = sb("probsT", [STRIP, 2, NS * P], F32, fast)
                neg_max = sb("neg_max", [P, 2], F32, fast)
                inv_sum = sb("inv_sum", [P, 2, 4], F32, fast)
            with ExitStack() as slow:
                g_v = sb("g_v", [STRIP, NB * NS, H, VW], F32, slow)
                g_wk = sb("g_wk", [P, KT, H * HD], F32, slow)
                g_wk2 = sb("g_wk2", [P, KT, 2, HD], F32, slow)
                g_q = sb("g_q", [P, P], F32R, slow)
                g_khi = sb("g_khi", [P, EVEN], F32R, slow)
                g_klo = sb("g_klo", [P, EVEN], F32R, slow)
                g_mask8 = sb("g_mask8", [P, SK], U8, slow)
                g_bias = sb("g_bias", [P, SK], BF16, slow)
                g_probs = sb("g_probs", [P, SKP], F32, slow)
                g_probsT = sb("g_probsT", [STRIP, NS * P], F32, slow)
                g_min = sb("g_min", [P, 8], F32, slow)
        with ExitStack() as ffn:
            w1_sb = sb("w1_sb", [P, KT, NE, FH], F32, ffn)
            w2_sb = sb("w2_sb", [P, KT, NE, FH], F32, ffn)
            w3_sb = sb("w3_sb", [P, HT, NE, D], F32, ffn)
            xn2 = sb("xn2", [P, NT, D], F32, ffn)
            sq2 = sb("sq2", [P, NT, D], F32, ffn)
            chosen = sb("chosen", [P, 2, NT, NE], F32, ffn)
            logits = sb("logits", [P, NT, NE], F32, ffn)
            work = sb("work", [P, NT, NE], F32, ffn)
            both = sb("both", [P, NT, NE], F32, ffn)
            sums = sb("sums", [P, 2, NT, NE], F32, ffn)
            place_f = sb("place_f", [P, NT, NE], F32, ffn)
            top = sb("top", [P, 2, NT], F32, ffn)
            pick = sb("pick", [P, NT], F32, ffn)
            weight = sb("weight", [P, 2, NT], F32, ffn)
            denom = sb("denom", [P, 2, NT], F32, ffn)
            place = sb("place", [P, 2, NT], I32, ffn)
            y_place = sb("y_place", [P, 2, NT], I32, ffn)
            y_starts = sb("y_starts", [P, NE], F32, ffn)
            tiles = sb("tiles", [P, 4, NE], F32, ffn)
            has_tile = sb("has_tile", [P, NE, NT], F32, ffn)
            sched_f = sb("sched_f", [1, 4, NSCHED, NE], F32, ffn)
            sched_s = sb("sched_s", [1, 2, NSCHED], F32, ffn)
            sched = sb("sched", [1, 2, NSCHED], I32, ffn)
            pad_row_f = sb("pad_row_f", [1, NE], F32, ffn)
            pad_row = sb("pad_row", [1, NE], I32, ffn)
            zeros = sb("zeros", [P, D], F32, ffn)
            xg = sb("xg", [P, 2, D], F32, ffn)
            xgT = sb("xgT", [P, 2, KT, P], F32, ffn)
            silu = sb("silu", [P, FH], F32, ffn)
            gated = sb("gated", [P, FH], F32, ffn)
            gatedT = sb("gatedT", [P, HT, P], F32, ffn)
            yg = sb("yg", [P, 2, D], F32, ffn)
            y_rows = sb("y_rows", [P, 4, 2, D], F32, ffn)

        ps_s = [psum("ps_s0"), psum("ps_s1")]
        ps_t = [psum("ps_t0"), psum("ps_t1")]
        ps_o = [psum("ps_o0"), psum("ps_o1")]
        ps_a, ps_b = psum("ps_a"), psum("ps_b")

        x_in, w_in, mask_in, g_in = sem("x_in"), sem("w_in"), sem("mask_in"), sem("g_in")
        mask_pad = sem("mask_pad")
        const_ready, pads_ready = sem("const_ready"), sem("pads_ready")
        ln = sem("ln")
        centred_sq, std_ready = sem("centred_sq"), sem("std_ready")
        tanh_ready = sem("tanh_ready")
        flag_step, flag_sum, flag_ready = sem("flag_step"), sem("flag_sum"), sem("flag_ready")
        xnT_ps, xnT_act, xnT_dve = sem("xnT_ps"), sem("xnT_act"), sem("xnT_dve")
        q_ps, q_hi, q_split = sem("q_ps"), sem("q_hi"), sem("q_split")
        k_ps, k_hi_ready, k_lo_ready = sem("k_ps"), sem("k_hi_ready"), sem("k_lo_ready")
        v_ps, v_act, v_dve = sem("v_ps"), sem("v_act"), sem("v_dve")
        bias_ready = sem("bias_ready")
        scores_ready, masked_ready, probs_ready = sem("scores_ready"), sem("masked_ready"), sem("probs_ready")
        probsT_ps, probsT_act, probsT_dve = sem("probsT_ps"), sem("probsT_act"), sem("probsT_dve")
        pv_ready, inv_ready, o_ready = sem("pv_ready"), sem("inv_ready"), sem("o_ready")
        oT_a_ps, oT_b_ps, oT_a, oT_b = sem("oT_a_ps"), sem("oT_b_ps"), sem("oT_a"), sem("oT_b")
        wo_ps, x2_ready = sem("wo_ps"), sem("x2_ready")
        attention_done = sem("attention_done")
        stored = sem("stored")
        carried = sem("carried")

        g_w_in, g_mask_in, g_bias_ready, g_pads = sem("g_w_in"), sem("g_mask_in"), sem("g_bias_ready"), sem("g_pads")
        g_v_ps, g_v_ready, g_staged = sem("g_v_ps"), sem("g_v_ready"), sem("g_staged")
        g_k_ps, g_khi_ready, g_klo_ready = sem("g_k_ps"), sem("g_khi_ready"), sem("g_klo_ready")
        g_scores_ready, g_masked_ready, g_min_ready = sem("g_scores_ready"), sem("g_masked_ready"), sem("g_min_ready")
        g_probs_ready, g_probsT_ps, g_probsT_ready = sem("g_probs_ready"), sem("g_probsT_ps"), sem("g_probsT_ready")
        g_pv_block, g_inv_ready, g_o_ready = sem("g_pv_block"), sem("g_inv_ready"), sem("g_o_ready")
        g_oT_ps, g_oT_ready, g_wo_ps, g_x2_ready = sem("g_oT_ps"), sem("g_oT_ready"), sem("g_wo_ps"), sem("g_x2_ready")

        xn2_ready, sq2_ready, std2_ready, ln2 = sem("xn2_ready"), sem("sq2_ready"), sem("std2_ready"), sem("ln2")
        xn2T_ps, xn2T_act, xn2T_dve = sem("xn2T_ps"), sem("xn2T_act"), sem("xn2T_dve")
        logits_ps, both_ready, prefix_ps = sem("logits_ps"), sem("both_ready"), sem("prefix_ps")
        route, exp_gap_ready, diff_ready = sem("route"), sem("exp_gap_ready"), sem("diff_ready")
        places_ready, y_places_ready = sem("places_ready"), sem("y_places_ready")
        sched_ready, zeros_ready = sem("sched_ready"), sem("zeros_ready")
        scattered, padded = sem("scattered"), sem("padded")
        expert_in = [sem(f"expert{e}_in") for e in range(NE)]
        experts_ready = sem("experts_ready")
        xg_in = [sem("xg0_in"), sem("xg1_in")]
        xgT_ps, xgT_ready = sem("xgT_ps"), sem("xgT_ready")
        h1_ps, h2_ps, silu_ready, gated_ready = sem("h1_ps"), sem("h2_ps"), sem("silu_ready"), sem("gated_ready")
        gatedT_ps, gatedT_ready = sem("gatedT_ps"), sem("gatedT_ready")
        y_ps, y_ready = sem("y_ps"), sem("y_ready")
        y_out = [sem("y0_out"), sem("y1_out")]
        y_back = [sem(f"y_back{n}") for n in range(4)]
        out_ready = sem("out_ready")
        wg_in = sem("wg_in")

        x_regrouped = nc.dram_tensor("x_regrouped", (NE * REGION, D), F32, kind="Internal").ap()
        y_regrouped = nc.dram_tensor("y_regrouped", (NG * P, D), F32, kind="Internal").ap()

        block = ctx.enter_context(nc.Block())

        def table(eng, row, s, top_value):
            return eng.value_load(sched[0:1, row, bass.ds(s, 1)], min_val=0, max_val=top_value)


        def last_block_only(eng):
            eng.wait_ge(flag_ready, 1)
            return eng.value_load(plainflag[0:1, 0:1], min_val=0, max_val=1) == 1

        W_ALL = 16 * 8

        PADS = 3
        ENGINES = 5
        CONSTS = 9
        BIAS0 = 2

        @block.sync
        def _(sp):
            sp.dma_start(xs[:, 1:, :], x.rearrange("(t p) d -> p t d", p=P)).then_inc(x_in, 16)
            sp.wait_ge(mask_pad, 1)
            sp.dma_start(mask8[:, :, 0:SK], mask.rearrange("(t p) k -> p t k", p=P)).then_inc(mask_in, 16)
            sp.dma_start(wq_sb[:, :, :], Wq.rearrange("(k p) n -> p k n", p=P)).then_inc(w_in, 16)
            sp.dma_start(ctxT_sb[:, :, 0:SK], ctxT.rearrange("(k p) n -> p k n", p=P)).then_inc(w_in, 16)
            for copy in range(2):
                for k in range(KT):
                    sp.dma_start(wk2_sb[:, k, :, copy, :],
                                 Wk[k * P:(k + 1) * P, :].rearrange("p (h d) -> p h d", h=H)).then_inc(w_in, 16)
            sp.dma_start(wv_sb[:, :, :], Wv.rearrange("(k p) n -> p k n", p=P)).then_inc(w_in, 16)
            sp.dma_start(wo_sb[:, :, :], Wo.rearrange("(k p) n -> p k n", p=P)).then_inc(w_in, 16)
            sp.dma_start(wg_sb[:, :, :], WgT.rearrange("(k p) e -> p k e", p=P)).then_inc(wg_in, 16)
            with sp.If(last_block_only(sp)):
                sp.nop().then_inc(attention_done, 1)
            with sp.Else():
                sp.wait_ge(w_in, W_ALL)
                sp.dma_start(g_wk[:, :, :], Wk.rearrange("(k p) n -> p k n", p=P)).then_inc(g_w_in, 16)
                with sp.Fori(0, NT) as i:
                    sp.wait_ge(g_bias_ready, i + 1)
                    sp.dma_start(g_mask8[:, :], mask[bass.ts(i, P), :]).then_inc(g_mask_in, 16)
                sp.nop().then_inc(attention_done, 1)
            sp.wait_ge(attention_done, ENGINES)
            for e in range(NE):
                sp.dma_start(w1_sb[:, :, e, :], W1T[e].rearrange("(k p) n -> p k n", p=P)).then_inc(expert_in[e], 16)
                sp.dma_start(w2_sb[:, :, e, :], W2T[e].rearrange("(k p) n -> p k n", p=P)).then_inc(expert_in[e], 16)
                sp.dma_start(w3_sb[:, :, e, :], W3T[e].rearrange("(k p) n -> p k n", p=P)).then_inc(expert_in[e], 16)
            sp.wait_ge(sched_ready, 1)
            sp.wait_ge(zeros_ready, 1)
            for e in range(NE):
                row = sp.value_load(pad_row[0:1, e:e + 1], min_val=0, max_val=(NE - 1) * REGION + S)
                sp.dma_start(x_regrouped[bass.ds(row, P), :], zeros[:, :]).then_inc(padded, 16)
            sp.wait_ge(padded, 16 * NE)
            sp.wait_ge(scattered, 16 * 2 * NT)

            def load_tile(s, buf, turns):
                if not (isinstance(turns, int) and turns == 0):
                    sp.wait_ge(xgT_ps, s - 1)
                row = table(sp, 0, s, (NE - 1) * REGION + S)
                sp.dma_start(xg[:, buf, :], x_regrouped[bass.ds(row, P), :]).then_inc(xg_in[buf], 16)

            def store_tile(s, buf):
                sp.wait_ge(y_ready, s + 2)
                sp.dma_start(y_regrouped[bass.ts(s, P), :], yg[:, buf, :]).then_inc(y_out[buf], 16)

            load_tile(0, 0, 0)
            load_tile(1, 1, 0)
            with sp.Fori(0, (NG - 3) // 2) as i:
                for b in range(2):
                    load_tile(2 * i + b + 2, b, i + 1)
                    store_tile(2 * i + b, b)
            load_tile(NG - 1, 0, 1)
            load_tile(NG, 1, 1)
            for s in range(NG - 3, NG):
                store_tile(s, s % 2)
            for c in range(4):
                sp.wait_ge(out_ready, 4 * c + 4)
                sp.dma_start(out[c * 4 * P:(c + 1) * 4 * P, :].rearrange("(t p) d -> p t d", p=P),
                             xs[:, 4 * c + 1:4 * c + 5, :]).then_inc(stored, 16)
            sp.wait_ge(stored, 64)

        @block.gpsimd
        def _(pool):
            pool.memset(mask8[:, :, SKP - 4:], 0).then_inc(mask_pad, 1)
            pool.dma_start(gates[:, 0:1], g_xattn.partition_broadcast(P)).then_inc(g_in, 16)
            pool.dma_start(gates[:, 1:2], g_ffn.partition_broadcast(P)).then_inc(g_in, 16)
            pool.memset(ident[:, :], 0.0).then_inc(const_ready, 1)
            pool.wait_ge(const_ready, 1)
            pool.affine_select(out=ident[:, :], in_=ident[:, :], compare_op=ALU.not_equal, fill=1.0, base=0,
                               pattern=[[-1, P]], channel_multiplier=1).then_inc(const_ready, 1)
            pool.memset(ones[:, :], 1.0).then_inc(const_ready, 1)
            pool.memset(before[:, :], 1.0).then_inc(const_ready, 1)
            pool.wait_ge(const_ready, 4)
            pool.affine_select(out=before[:, :], in_=before[:, :], compare_op=ALU.is_gt, fill=0.0, base=0,
                               pattern=[[1, P]], channel_multiplier=-1).then_inc(const_ready, 1)
            for tile, base, step, n in ((rank, NE, -1, NE), (number, 0, 1, NE), (fill, 0, P, NT), (turn, 0, 1, NSCHED)):
                pool.iota(tile[:, :], pattern=[[step, n]], base=base, channel_multiplier=0,
                          allow_small_or_imprecise_dtypes=True).then_inc(const_ready, 1)
            pool.memset(xs[:, 0, :], 0.0).then_inc(x2_ready, 1)
            pool.memset(xnT[:, :, NT * P:], 0.0).then_inc(pads_ready, 1)
            pool.memset(ctxT_sb[:, :, SK:], 0.0).then_inc(pads_ready, 1)
            pool.memset(biases[:, DUMMY, :], 0.0).then_inc(pads_ready, 1)
            pool.memset(o_rows[:, :], 0.0).then_inc(o_ready, 4)
            with pool.If(last_block_only(pool)):
                pool.memset(v_aug[:, :, :, HD:], 1.0).then_inc(bias_ready, 1)
                pool.memset(probs[:, :, LASTK:], 0.0).then_inc(bias_ready, 1)
                for half in range(2):
                    pool.tensor_copy(bias_cur[:, half, :], biases[:, 0, :]).then_inc(bias_ready, 1)
                with pool.Fori(0, NT) as i:
                    for half in range(2):
                        pool.wait_ge(masked_ready, H * i + 8 * half + 8)
                        pool.sem_inc(carried, 1)
                        pool.tensor_copy(bias_cur[:, half, :], biases[:, i + 1, :]).then_inc(bias_ready, 1)
                pool.wait_ge(bias_ready, BIAS0 + 2 * NT + 2)
                pool.nop().then_inc(attention_done, 1)
            with pool.Else():
                pool.wait_ge(w_in, W_ALL)
                pool.memset(g_v[:, :, :, HD:], 1.0).then_inc(g_pads, 1)
                pool.memset(g_probs[:, SK:], 0.0).then_inc(g_pads, 1)
                pool.wait_ge(g_pads, 2)
                pool.nop().then_inc(attention_done, 1)

            pool.wait_ge(attention_done, ENGINES)
            pool.memset(zeros[:, :], 0.0).then_inc(zeros_ready, 1)
            pool.wait_ge(xn2_ready, 1)
            pool.wait_ge(places_ready, 1)
            for t in range(NT):
                for c in range(2):
                    pool.indirect_dma_start(out=x_regrouped, out_offset=bass.IndirectOffsetOnAxis(ap=place[:, c, t:t + 1], axis=0),
                                            in_=xn2[:, t, :], in_offset=None).then_inc(scattered, 16)
            for e in range(NE):
                pool.wait_ge(expert_in[e], 48)
                pool.nop().then_inc(experts_ready, 1)
            pool.wait_ge(y_places_ready, 1)
            pool.wait_ge(y_out[0], 16 * ((NG + 1) // 2))
            pool.wait_ge(y_out[1], 16 * (NG // 2))
            for t in range(NT):
                if t >= 4:
                    pool.wait_ge(out_ready, t - 3)
                for c in range(2):
                    pool.indirect_dma_start(out=y_rows[:, t % 4, c, :], out_offset=None, in_=y_regrouped,
                                            in_offset=bass.IndirectOffsetOnAxis(ap=y_place[:, c, t:t + 1], axis=0))\
                        .then_inc(y_back[t % 4], 16)

        @block.scalar
        def _(act):
            act.wait_ge(ln, 3)
            act.activation(sq[:, :, :], xc[:, :, :], ACT.Square).then_inc(centred_sq, 1)
            act.wait_ge(ln, 5)
            act.activation(stat[:, 2, :], stat[:, 1, :], ACT.Sqrt).then_inc(std_ready, 1)
            act.wait_ge(g_in, 32)
            act.activation(tanh_g[:, :], gates[:, :], ACT.Tanh).then_inc(tanh_ready, 1)
            for c in range(0, 8, 2):
                act.wait_ge(xnT_ps, c + 1)
                k, t0 = c // 4, 4 * (c % 4)
                act.copy(xnT[:, k, t0 * P:(t0 + 4) * P], ps_s[0][:, :]).then_inc(xnT_act, 1)

            def q_high_parts(half, batch):
                act.wait_ge(q_ps, batch + 1)
                src = ps_a[:, :].rearrange("p (c n) -> p c n", c=4)
                act.copy(q_parts[0:HD, 8 * half:8 * half + 8:2, :], src[0:HD]).then_inc(q_hi, 1)
                act.copy(q_parts[HD:P, 8 * half + 1:8 * half + 8:2, :], src[HD:P]).then_inc(q_hi, 1)

            def fast_attention():
                for h in range(H):
                    act.wait_ge(k_ps, h + 1)
                    act.mul(k_hi[:, h, :], [ps_a, ps_b][h % 2][:, 0:EVEN], -1.0).then_inc(k_hi_ready, 1)
                for c in range(0, 2 * NS, 2):
                    act.wait_ge(v_ps, c + 1)
                    act.copy(v_aug[:, c // 2, 0:8, 0:HD],
                             ps_s[0][0:STRIP, :].rearrange("p (h d) -> p h d", h=8)).then_inc(v_act, 1)
                for half in range(2):
                    q_high_parts(half, half)

                def exps(i, k):
                    n = H * i + k
                    act.wait_ge(masked_ready, n + 1)
                    if not (isinstance(n, int) and n < 2):
                        act.wait_ge(probsT_ps, n - 1)
                    act.activation(probs[:, k % 2, 0:LASTK], masked[:, k % 2, :], ACT.Exp,
                                   bias=neg_max[:, k % 2:k % 2 + 1], scale=-1.0).then_inc(probs_ready, 1)

                def copies(i, k):
                    n = H * i + k
                    act.wait_ge(probsT_ps, n + 1)
                    if not (isinstance(n, int) and n < 2):
                        act.wait_ge(pv_ready, n - 1)
                    act.copy(probsT[:, 0, :], ps_t[0][0:STRIP, :]).then_inc(probsT_act, 1)

                def oT_copies(i, step):
                    if step == 1:
                        act.wait_ge(oT_a_ps, i + 1)
                        act.copy(oT[:, 0:4, :], ps_b[:, :].rearrange("p (c n) -> p c n", c=4)).then_inc(oT_a, 1)
                    if step == 2:
                        act.wait_ge(oT_b_ps, i + 1)
                        act.copy(oT[:, 4:8, :], ps_a[:, :].rearrange("p (c n) -> p c n", c=4)).then_inc(oT_b, 1)

                for k in range(5):
                    exps(0, k)
                    if k in (1, 3):
                        copies(0, k - 1)
                with act.Fori(0, NT) as i:
                    for j in range(H):
                        exps(i, j + 5)
                        if j % 2 == 0:
                            copies(i, j + 4)
                        oT_copies(i, j)
                        if j == 7:
                            q_high_parts(0, 2 * i + 2)
                        if j == 15:
                            q_high_parts(1, 2 * i + 3)
                for step in (1, 2):
                    oT_copies(NT, step)
                act.wait_ge(probs_ready, H * NT + 5)
                act.wait_ge(oT_b, NT + 1)
                act.nop().then_inc(attention_done, 1)

            with act.If(last_block_only(act)):
                fast_attention()
            def full_attention():
                act.sem_inc(g_probsT_ready, 1)
                for c in range(2 * NB * NS):
                    act.wait_ge(g_v_ps, c + 1)
                    half, w = c % 2, block_of(c // 2 // NS)[3]
                    act.copy(g_v[0:w, c // 2, 8 * half:8 * half + 8, 0:HD],
                             ps_s[half][0:w, :].rearrange("p (h d) -> p h d", h=8)).then_inc(g_v_ready, 1)
                with act.Fori(0, NT) as i:
                    for half in range(2):
                        q_high_parts(half, 2 * i + half)
                    with act.Fori(0, H) as h:
                        n = H * i + h
                        for b in range(NB):
                            act.wait_ge(g_k_ps, NB * n + b + 1)
                            act.mul(g_khi[:, 0:block_of(b)[2]], ps_a[:, 0:block_of(b)[2]], -1.0).then_inc(g_khi_ready, 1)
                        act.wait_ge(g_min_ready, n + 1)
                        act.activation(g_probs[:, 0:SK], g_probs[:, 0:SK], ACT.Exp, bias=g_min[:, 4:5], scale=-1.0)\
                           .then_inc(g_probs_ready, 1)
                        for b in range(NB):
                            w = block_of(b)[3]
                            act.wait_ge(g_probsT_ps, NB * n + b + 1)
                            act.copy(g_probsT[0:w, :], ps_t[0][0:w, :]).then_inc(g_probsT_ready, 1)
                    for half in range(2):
                        act.wait_ge(g_oT_ps, 2 * i + half + 1)
                        act.copy(oT[:, 4 * half:4 * half + 4, :],
                                 [ps_b, ps_a][half][:, :].rearrange("p (c n) -> p c n", c=4)).then_inc(g_oT_ready, 1)
                act.wait_ge(g_oT_ready, 2 * NT)
                act.nop().then_inc(attention_done, 1)

            with act.Else():
                full_attention()

            act.wait_ge(attention_done, ENGINES)
            act.wait_ge(ln2, 3)
            act.activation(sq2[:, :, :], xn2[:, :, :], ACT.Square).then_inc(sq2_ready, 1)
            act.wait_ge(ln2, 5)
            act.activation(stat[:, 2, :], stat[:, 1, :], ACT.Sqrt).then_inc(std2_ready, 1)
            for c in range(0, 8, 2):
                act.wait_ge(xn2T_ps, c + 1)
                k, t0 = c // 4, 4 * (c % 4)
                act.copy(xnT[:, k, t0 * P:(t0 + 4) * P], ps_s[0][:, :]).then_inc(xn2T_act, 1)
            act.wait_ge(diff_ready, 1)
            act.activation(denom[:, 0, :], pick[:, :], ACT.Exp).then_inc(exp_gap_ready, 1)

            def copy_xgT(s, buf):
                act.wait_ge(xgT_ps, s + 1)
                act.copy(xgT[:, buf, :, :], ps_t[1][:, 0:KT * P].rearrange("p (k n) -> p k n", k=KT))\
                   .then_inc(xgT_ready, 1)

            def silu_of(s):
                act.wait_ge(h1_ps, s + 1)
                if not (isinstance(s, int) and s == 0):
                    act.wait_ge(gated_ready, s)
                act.activation(silu[:, :], ps_s[0][:, :], ACT.Silu).then_inc(silu_ready, 1)

            def copy_gatedT(s):
                act.wait_ge(gatedT_ps, s + 1)
                if not (isinstance(s, int) and s == 0):
                    act.wait_ge(y_ps, s + 1)
                act.copy(gatedT[:, :, :], ps_t[0][:, :].rearrange("p (k n) -> p k n", k=HT)).then_inc(gatedT_ready, 1)

            act.sem_inc(gatedT_ready, 1)
            copy_xgT(0, 0)
            silu_of(0)
            copy_xgT(1, 1)
            with act.Fori(0, (NG - 1) // 2) as i:
                for b in range(2):
                    s = 2 * i + b
                    copy_gatedT(s)
                    silu_of(s + 1)
                    copy_xgT(s + 2, b)
            copy_gatedT(NG - 1)

        @block.vector
        def _(dve):
            def rows(col):
                return stat[:, col, :].unsqueeze(2).to_broadcast([P, NT, D])

            dve.wait_ge(x_in, 16)
            dve.tensor_reduce(stat[:, 0, :], xs[:, 1:, :], AX.X, ALU.add).then_inc(ln, 1)
            dve.wait_ge(ln, 1)
            dve.tensor_scalar(stat[:, 0, :], stat[:, 0, :], 1.0 / D, None, ALU.mult).then_inc(ln, 1)
            dve.wait_ge(ln, 2)
            dve.tensor_tensor(xc[:, :, :], xs[:, 1:, :], rows(0), ALU.subtract).then_inc(ln, 1)
            dve.wait_ge(centred_sq, 1)
            dve.tensor_reduce(stat[:, 1, :], sq[:, :, :], AX.X, ALU.add).then_inc(ln, 1)
            dve.wait_ge(ln, 4)
            dve.tensor_scalar(stat[:, 1, :], stat[:, 1, :], 1.0 / D, EPS, ALU.mult, ALU.add).then_inc(ln, 1)
            dve.wait_ge(std_ready, 1)
            dve.reciprocal(stat[:, 3, :], stat[:, 2, :]).then_inc(ln, 1)
            dve.wait_ge(ln, 6)
            dve.tensor_tensor(xc[:, :, :], xc[:, :, :], rows(3), ALU.mult).then_inc(ln, 1)

            dve.wait_ge(mask_in, 16)
            dve.wait_ge(pads_ready, PADS)
            words = mask8[:, :, :].bitcast(I32)
            dve.tensor_reduce(rowflag[:, 0:1], words[:, :, 0:LAST0 // 4], AX.XY, ALU.max).then_inc(flag_step, 1)
            dve.tensor_reduce(stat[:, 0, :], words[:, :, LAST0 // 4:], AX.X, ALU.max).then_inc(flag_step, 1)
            dve.wait_ge(flag_step, 2)
            dve.tensor_reduce(rowflag[:, 1:2], stat[:, 0, :], AX.X, ALU.min).then_inc(flag_step, 1)
            dve.wait_ge(flag_step, 3)
            dve.tensor_scalar(rowflag[:, 2:3], rowflag[:, 0:1], 0.0, None, ALU.is_equal).then_inc(flag_step, 1)
            dve.tensor_scalar(rowflag[:, 3:4], rowflag[:, 1:2], 0.0, None, ALU.is_gt).then_inc(flag_step, 1)
            dve.wait_ge(flag_step, 5)
            dve.tensor_tensor(rowflag[:, 0:1], rowflag[:, 2:3], rowflag[:, 3:4], ALU.mult).then_inc(flag_step, 1)
            dve.tensor_scalar(biases[:, 0:NT, :], mask8[:, :, LAST0:SK], -MASKED, MASKED, ALU.mult, ALU.add)\
               .then_inc(flag_step, 1)
            for c in range(1, 8, 2):
                dve.wait_ge(xnT_ps, c + 1)
                k, t0 = c // 4, 4 * (c % 4)
                dve.tensor_copy(xnT[:, k, t0 * P:(t0 + 4) * P], ps_s[1][:, :]).then_inc(xnT_dve, 1)
            dve.wait_ge(flag_sum, 1)
            dve.tensor_scalar(plainflag[:, :], ps_o[0][0:1, 0:1], float(P), None, ALU.is_equal)\
               .then_inc(flag_ready, 1)

            def q_low_parts(half, batch):
                dve.wait_ge(q_hi, 2 * batch + 2)
                src = ps_a[:, :].rearrange("p (c n) -> p c n", c=4)
                even = q_parts[:, 8 * half:8 * half + 8:2, :]
                odd = q_parts[:, 8 * half + 1:8 * half + 8:2, :]
                dve.tensor_tensor(even[HD:P], src[0:HD], even[0:HD], ALU.subtract)
                dve.tensor_tensor(odd[0:HD], src[HD:P], odd[HD:P], ALU.subtract).then_inc(q_split, 1)

            def fast_attention():
                for h in range(H):
                    dve.wait_ge(k_hi_ready, h + 1)
                    dve.scalar_tensor_tensor(out=k_lo[:, h, :], in0=[ps_a, ps_b][h % 2][:, 0:EVEN], scalar=-1.0,
                                             in1=k_hi[:, h, :], op0=ALU.mult, op1=ALU.subtract)\
                       .then_inc(k_lo_ready, 1)
                for c in range(1, 2 * NS, 2):
                    dve.wait_ge(v_ps, c + 1)
                    dve.tensor_copy(v_aug[:, c // 2, 8:16, 0:HD],
                                    ps_s[1][0:STRIP, :].rearrange("p (h d) -> p h d", h=8)).then_inc(v_dve, 1)
                for half in range(2):
                    q_low_parts(half, half)

                def mask_and_max(i, k):
                    n = H * i + k
                    if k % 8 == 0:
                        dve.wait_ge(bias_ready, BIAS0 + 2 * (i + k // H) + k % H // 8 + 1)
                    dve.wait_ge(scores_ready, n + 1)
                    if not (isinstance(n, int) and n < 2):
                        dve.wait_ge(probs_ready, n - 1)
                    if not isinstance(n, int):
                        dve.sem_inc(carried, 1)
                    dve.tensor_tensor_reduce(masked[:, k % 2, :], ps_s[k % 2][:, 0:LASTK],
                                             bias_cur[:, k % H // 8, :], HD ** -0.5, 3e38, ALU.add, ALU.min,
                                             neg_max[:, k % 2:k % 2 + 1]).then_inc(masked_ready, 1)

                def copies(i, k):
                    n = H * i + k
                    dve.wait_ge(probsT_ps, n + 1)
                    if not (isinstance(n, int) and n < 2):
                        dve.wait_ge(pv_ready, n - 1)
                    dve.tensor_copy(probsT[:, 1, :], ps_t[1][0:STRIP, :]).then_inc(probsT_dve, 1)

                def normalise(i, quad):
                    q = 4 * i + quad
                    dve.wait_ge(pv_ready, H * i + 4 * quad + 4)
                    src = ps_o[quad % 2][:, 0:4 * VW].rearrange("p (h d) -> p h d", h=4)
                    inv = inv_sum[:, quad % 2, :].unsqueeze(2)
                    dve.reciprocal(inv, src[:, :, HD:]).then_inc(inv_ready, 1)
                    dve.wait_ge(inv_ready, q + 1)
                    dve.wait_ge(oT_a_ps if quad < 2 else oT_b_ps, i + 1)
                    dve.tensor_tensor(o_rows[:, quad * 4 * HD:(quad + 1) * 4 * HD].rearrange("p (h d) -> p h d", h=4),
                                      src[:, :, 0:HD], inv.to_broadcast([P, 4, HD]), ALU.mult).then_inc(o_ready, 1)

                def residual(i):
                    dve.wait_ge(wo_ps, i + 1)
                    dve.scalar_tensor_tensor(out=xs[:, i, :], in0=ps_b[:, 0:D], scalar=tanh_g[:, 0:1],
                                             in1=xs[:, i, :], op0=ALU.mult, op1=ALU.add).then_inc(x2_ready, 1)

                dve.wait_ge(tanh_ready, 1)
                for k in range(6):
                    mask_and_max(0, k)
                    if k in (3, 5):
                        copies(0, k - 2)
                with dve.Fori(0, NT) as i:
                    for j in range(H):
                        mask_and_max(i, j + 6)
                        if j % 2 == 1:
                            copies(i, j + 4)
                        if j % 4 == 3:
                            normalise(i, j // 4)
                        if j == 8:
                            q_low_parts(0, 2 * i + 2)
                        if j == 12:
                            residual(i)
                        if j == 15:
                            q_low_parts(1, 2 * i + 3)
                residual(NT)
                dve.wait_ge(x2_ready, NT + 2)
                dve.nop().then_inc(attention_done, 1)

            with dve.If(last_block_only(dve)):
                fast_attention()
            def full_attention():
                for free in (g_klo_ready, g_masked_ready, g_o_ready, g_x2_ready, g_bias_ready, q_split):
                    dve.sem_inc(free, 1)
                dve.wait_ge(g_w_in, 16)
                with dve.Fori(0, NT) as i:
                    dve.wait_ge(g_mask_in, 16 * i + 16)
                    dve.tensor_scalar(g_bias[:, :], g_mask8[:, :], -MASKED, MASKED, ALU.mult, ALU.add)\
                       .then_inc(g_bias_ready, 1)
                    for half in range(2):
                        q_low_parts(half, 2 * i + half)
                    dve.wait_ge(q_split, 2 * i + 3)
                    dve.wait_ge(g_bias_ready, i + 2)
                    dve.sem_inc(carried, 1)
                    with dve.Fori(0, H) as h:
                        n = H * i + h
                        dve.wait_ge(g_pv_block, NB * n + 1)
                        dve.tensor_copy(g_q[:, :], q_parts[:, bass.ds(h, 1), :].squeeze(1)).then_inc(g_staged, 1)
                        for copy in range(2):
                            dve.tensor_copy(g_wk2[:, :, copy, :], g_wk[:, :, bass.ds(h * HD, HD)]).then_inc(g_staged, 1)
                        for b in range(NB):
                            k0, keys, even, _ = block_of(b)
                            dve.wait_ge(g_khi_ready, NB * n + b + 1)
                            dve.scalar_tensor_tensor(out=g_klo[:, 0:even], in0=ps_a[:, 0:even], scalar=-1.0,
                                                     in1=g_khi[:, 0:even], op0=ALU.mult, op1=ALU.subtract)\
                               .then_inc(g_klo_ready, 1)
                            dve.wait_ge(g_scores_ready, NB * n + b + 1)
                            dve.sem_inc(carried, 1)
                            dve.tensor_tensor_reduce(g_probs[:, k0:k0 + keys], ps_s[0][:, 0:keys],
                                                     g_bias[:, k0:k0 + keys], HD ** -0.5, 3e38, ALU.add, ALU.min,
                                                     g_min[:, b:b + 1]).then_inc(g_masked_ready, 1)
                        dve.wait_ge(g_masked_ready, NB * n + NB + 1)
                        dve.tensor_reduce(g_min[:, 4:5], g_min[:, 0:NB], AX.X, ALU.min).then_inc(g_min_ready, 1)
                        dve.wait_ge(g_pv_block, NB * n + NB + 1)
                        dve.reciprocal(g_min[:, 5:6], ps_o[0][:, HD:VW]).then_inc(g_inv_ready, 1)
                        dve.wait_ge(g_inv_ready, n + 1)
                        dve.tensor_scalar(o_rows[:, bass.ds(h * HD, HD)], ps_o[0][:, 0:HD], g_min[:, 5:6], None,
                                          ALU.mult).then_inc(g_o_ready, 1)
                    dve.wait_ge(g_wo_ps, i + 1)
                    dve.scalar_tensor_tensor(out=xs[:, i + 1, :], in0=ps_b[:, 0:D], scalar=tanh_g[:, 0:1],
                                             in1=xs[:, i + 1, :], op0=ALU.mult, op1=ALU.add).then_inc(g_x2_ready, 1)
                dve.wait_ge(g_x2_ready, NT + 1)
                dve.nop().then_inc(attention_done, 1)

            with dve.Else():
                full_attention()

            dve.wait_ge(attention_done, ENGINES)
            dve.tensor_reduce(stat[:, 0, :], xs[:, 1:, :], AX.X, ALU.add).then_inc(ln2, 1)
            dve.wait_ge(ln2, 1)
            dve.tensor_scalar(stat[:, 0, :], stat[:, 0, :], 1.0 / D, None, ALU.mult).then_inc(ln2, 1)
            dve.wait_ge(ln2, 2)
            dve.tensor_tensor(xn2[:, :, :], xs[:, 1:, :], rows(0), ALU.subtract).then_inc(ln2, 1)
            dve.wait_ge(sq2_ready, 1)
            dve.tensor_reduce(stat[:, 1, :], sq2[:, :, :], AX.X, ALU.add).then_inc(ln2, 1)
            dve.wait_ge(ln2, 4)
            dve.tensor_scalar(stat[:, 1, :], stat[:, 1, :], 1.0 / D, EPS, ALU.mult, ALU.add).then_inc(ln2, 1)
            dve.wait_ge(std2_ready, 1)
            dve.reciprocal(stat[:, 3, :], stat[:, 2, :]).then_inc(ln2, 1)
            dve.wait_ge(ln2, 6)
            dve.tensor_tensor(xn2[:, :, :], xn2[:, :, :], rows(3), ALU.mult).then_inc(xn2_ready, 1)
            for c in range(1, 8, 2):
                dve.wait_ge(xn2T_ps, c + 1)
                k, t0 = c // 4, 4 * (c % 4)
                dve.tensor_copy(xnT[:, k, t0 * P:(t0 + 4) * P], ps_s[1][:, :]).then_inc(xn2T_dve, 1)

            routed = [0]

            def step(ins):
                routed[0] += 1
                ins.then_inc(route, 1)
                dve.wait_ge(route, routed[0])

            def per_expert(v):
                return v.unsqueeze(2).to_broadcast([P, NT, NE])

            def per_tile(v):
                return v.unsqueeze(1).to_broadcast([P, NT, NE])

            dve.wait_ge(logits_ps, 1)
            step(dve.tensor_copy(logits[:, :, :], ps_o[1][:, 0:NT * NE].rearrange("p (t e) -> p t e", e=NE)))
            for c in range(2):
                step(dve.tensor_reduce(top[:, c, :], logits[:, :, :], AX.X, ALU.max))
                step(dve.tensor_tensor(work[:, :, :], logits[:, :, :], per_expert(top[:, c, :]), ALU.is_equal))
                step(dve.tensor_tensor(work[:, :, :], work[:, :, :], per_tile(rank[:, :]), ALU.mult))
                step(dve.tensor_reduce(pick[:, :], work[:, :, :], AX.X, ALU.max))
                step(dve.tensor_tensor(chosen[:, c, :, :], per_tile(rank[:, :]), per_expert(pick[:, :]), ALU.is_equal))
                if c == 0:
                    step(dve.scalar_tensor_tensor(out=logits[:, :, :], in0=chosen[:, 0, :, :], scalar=-3e38,
                                                  in1=logits[:, :, :], op0=ALU.mult, op1=ALU.add))
            dve.tensor_tensor(both[:, :, :], chosen[:, 0, :, :], chosen[:, 1, :, :], ALU.add).then_inc(both_ready, 1)
            dve.tensor_tensor(pick[:, :], top[:, 1, :], top[:, 0, :], ALU.subtract).then_inc(diff_ready, 1)
            dve.wait_ge(exp_gap_ready, 1)
            step(dve.tensor_scalar(denom[:, 1, :], denom[:, 0, :], 1.0, None, ALU.add))
            step(dve.reciprocal(denom[:, 1, :], denom[:, 1, :]))
            step(dve.tensor_scalar(weight[:, 0, :], denom[:, 1, :], tanh_g[:, 1:2], None, ALU.mult))
            step(dve.tensor_tensor(weight[:, 1, :], weight[:, 0, :], denom[:, 0, :], ALU.mult))

            dve.wait_ge(prefix_ps, 1)
            step(dve.tensor_copy(sums[:, 0, :, :], ps_b[:, 0:NT * NE].rearrange("p (t e) -> p t e", e=NE)))
            src = 0
            for shift in (1, 2, 4, 8):
                a, b = sums[:, src, :, :], sums[:, 1 - src, :, :]
                step(dve.tensor_copy(b[:, 0:shift, :], a[:, 0:shift, :]))
                step(dve.tensor_tensor(b[:, shift:, :], a[:, shift:, :], a[:, 0:NT - shift, :], ALU.add))
                src = 1 - src
            upto = sums[:, src, :, :]
            in_tile = ps_a[:, 0:NT * NE].rearrange("p (t e) -> p t e", e=NE)
            step(dve.tensor_scalar(tiles[:, 3, :], number[:, :], float(REGION), None, ALU.mult))
            step(dve.tensor_tensor(place_f[:, :, :], in_tile, per_tile(tiles[:, 3, :]), ALU.add))
            step(dve.tensor_tensor(place_f[:, 1:, :], place_f[:, 1:, :], upto[:, 0:NT - 1, :], ALU.add))
            for c in range(2):
                step(dve.tensor_tensor(work[:, :, :], place_f[:, :, :], chosen[:, c, :, :], ALU.mult))
                step(dve.tensor_reduce(top[:, c, :], work[:, :, :], AX.X, ALU.add))
            dve.tensor_copy(place[:, :, :], top[:, :, :]).then_inc(places_ready, 1)
            total = upto[:, NT - 1, :]
            step(dve.tensor_tensor(has_tile[:, :, :], total.unsqueeze(2).to_broadcast([P, NE, NT]),
                                   fill[:, :].unsqueeze(1).to_broadcast([P, NE, NT]), ALU.is_gt))
            step(dve.tensor_reduce(tiles[:, 0, :], has_tile[:, :, :], AX.X, ALU.add))
            src = 0
            for shift in (1, 2, 4):
                a, b = tiles[:, src, :], tiles[:, src + 1, :] if src < 2 else tiles[:, 0, :]
                step(dve.tensor_copy(b[:, 0:shift], a[:, 0:shift]))
                step(dve.tensor_tensor(b[:, shift:], a[:, shift:], a[:, 0:NE - shift], ALU.add))
                src = (src + 1) % 3
            ends = tiles[0:1, src, :]
            def spread(v):
                return v.unsqueeze(1).to_broadcast([1, NSCHED, NE])

            turns = turn[0:1, :].unsqueeze(2).to_broadcast([1, NSCHED, NE])
            past_end, past_start, mine, val = (sched_f[:, n, :, :] for n in range(4))
            step(dve.tensor_tensor(past_end, turns, spread(ends), ALU.is_ge))
            step(dve.memset(past_start[:, :, 0:1], 1.0))
            step(dve.tensor_copy(past_start[:, :, 1:], past_end[:, :, 0:NE - 1]))
            step(dve.tensor_tensor(mine, past_start, past_end, ALU.subtract))
            step(dve.tensor_scalar(pad_row_f[:, 1:], ends[:, 0:NE - 1], -float(P), None, ALU.mult))
            step(dve.memset(pad_row_f[:, 0:1], 0.0))
            step(dve.tensor_tensor(pad_row_f[:, :], pad_row_f[:, :], tiles[0:1, 3, :], ALU.add))
            step(dve.scalar_tensor_tensor(out=val, in0=turns, scalar=float(P), in1=spread(pad_row_f[:, :]),
                                          op0=ALU.mult, op1=ALU.add))
            step(dve.tensor_tensor(val, val, mine, ALU.mult))
            step(dve.tensor_reduce(sched_s[:, 0, :], val, AX.X, ALU.add))
            step(dve.tensor_tensor(val, mine, spread(number[0:1, :]), ALU.mult))
            step(dve.tensor_reduce(sched_s[:, 1, :], val, AX.X, ALU.add))
            step(dve.tensor_copy(sched[:, :, :], sched_s[:, :, :]))
            step(dve.tensor_scalar(y_starts[:, 1:], tiles[:, src, 0:NE - 1], float(P), None, ALU.mult))
            step(dve.memset(y_starts[:, 0:1], 0.0))
            step(dve.tensor_tensor(y_starts[:, :], y_starts[:, :], tiles[:, 3, :], ALU.subtract))
            step(dve.tensor_tensor(place_f[:, :, :], place_f[:, :, :], per_tile(y_starts[:, :]), ALU.add))
            for c in range(2):
                step(dve.tensor_tensor(work[:, :, :], place_f[:, :, :], chosen[:, c, :, :], ALU.mult))
                step(dve.tensor_reduce(top[:, c, :], work[:, :, :], AX.X, ALU.add))
            dve.tensor_copy(y_place[:, :, :], top[:, :, :]).then_inc(y_places_ready, 1)
            step(dve.tensor_tensor(pad_row_f[:, :], tiles[0:1, 3, :], total[0:1, :], ALU.add))
            dve.tensor_copy(pad_row[:, :], pad_row_f[:, :]).then_inc(sched_ready, 1)

            def gate(s):
                dve.wait_ge(silu_ready, s + 1)
                dve.wait_ge(h2_ps, s + 1)
                if not (isinstance(s, int) and s == 0):
                    dve.wait_ge(gatedT_ps, s)
                dve.tensor_tensor(gated[:, :], ps_s[1][:, :], silu[:, :], ALU.mult).then_inc(gated_ready, 1)

            def copy_y(s, buf, turns):
                dve.wait_ge(y_ps, s + 2)
                if not (isinstance(turns, int) and turns == 0):
                    dve.wait_ge(y_out[buf], 16 * turns)
                dve.tensor_copy(yg[:, buf, :], ps_o[0][:, 0:D]).then_inc(y_ready, 1)

            dve.sem_inc(y_ready, 1)
            gate(0)
            gate(1)
            copy_y(0, 0, 0)
            gate(2)
            copy_y(1, 1, 0)
            with dve.Fori(1, (NG - 1) // 2) as i:
                for b in range(2):
                    gate(2 * i + b + 1)
                    copy_y(2 * i + b, b, i)
            copy_y(NG - 1, 0, (NG - 1) // 2)
            for t in range(NT):
                dve.wait_ge(y_back[t % 4], 32 * (t // 4 + 1))
                for c in range(2):
                    ins = dve.scalar_tensor_tensor(out=xs[:, t + 1, :], in0=y_rows[:, t % 4, c, :],
                                                   scalar=weight[:, c, t:t + 1], in1=xs[:, t + 1, :],
                                                   op0=ALU.mult, op1=ALU.add)
                    if c == 0:
                        step(ins)
                ins.then_inc(out_ready, 1)

        @block.tensor
        def _(pe):
            pe.wait_ge(const_ready, CONSTS)
            pe.wait_ge(ln, 7)
            for c in range(8):
                k, t0 = c // 4, 4 * (c % 4)
                if c >= 2:
                    pe.wait_ge([xnT_act, xnT_dve][c % 2], c // 2)
                for t in range(4):
                    last = pe.transpose(ps_s[c % 2][:, t * P:(t + 1) * P], xc[:, t0 + t, k * P:(k + 1) * P],
                                        ident[:, :])
                last.then_inc(xnT_ps, 1)
            pe.wait_ge(flag_step, 6)
            pe.matmul(ps_o[0][0:1, 0:1], ones[:, 0:1], rowflag[:, 0:1], start=True, stop=True).then_inc(flag_sum, 1)
            pe.wait_ge(w_in, W_ALL)
            pe.wait_ge(pads_ready, PADS)
            pe.wait_ge(xnT_act, 4)
            pe.wait_ge(xnT_dve, 4)

            def project_q(pair, i):
                for k in range(KT):
                    mm = pe.matmul(ps_a[:, pair % 4 * P:(pair % 4 + 1) * P], wq_sb[:, k, pair * P:(pair + 1) * P],
                                   xnT[:, k, bass.ts(i, P)], start=(k == 0), stop=(k == KT - 1))
                return mm

            def fast_attention():
                for h in range(H):
                    if h >= 2:
                        pe.wait_ge(k_lo_ready, h - 1)
                    for k in range(KT):
                        mm = pe.matmul([ps_a, ps_b][h % 2][:, 0:EVEN],
                                       wk2_sb[:, k, h, :, :].rearrange("p c d -> p (c d)"),
                                       ctxT_sb[:, k, LAST0:LAST0 + EVEN], start=(k == 0), stop=(k == KT - 1))
                    mm.then_inc(k_ps, 1)
                for c in range(2 * NS):
                    s, half = c // 2, c % 2
                    if c >= 2:
                        pe.wait_ge([v_act, v_dve][c % 2], c // 2)
                    for k in range(KT):
                        mm = pe.matmul(ps_s[c % 2][0:STRIP, :],
                                       ctxT_sb[:, k, LAST0 + s * STRIP:LAST0 + (s + 1) * STRIP],
                                       wv_sb[:, k, half * 512:(half + 1) * 512], start=(k == 0), stop=(k == KT - 1))
                    mm.then_inc(v_ps, 1)
                pe.wait_ge(k_lo_ready, H)
                for half in range(2):
                    if half:
                        pe.wait_ge(q_split, 1)
                    for pair in range(4 * half, 4 * half + 4):
                        mm = project_q(pair, 0)
                    mm.then_inc(q_ps, 1)
                pe.wait_ge(v_act, NS)
                pe.wait_ge(v_dve, NS)
                pe.wait_ge(bias_ready, BIAS0)

                def scores(i, k):
                    n, h = H * i + k, k % H
                    if k % 8 == 0:
                        pe.wait_ge(q_split, 2 * (i + k // H) + h // 8 + 1)
                    if not (isinstance(n, int) and n < 2):
                        pe.wait_ge(masked_ready, n - 1)
                    pe.matmul(ps_s[k % 2][:, 0:EVEN], q_parts[:, h, :], k_hi[:, h, :], start=True, stop=False)
                    pe.matmul(ps_s[k % 2][:, 0:EVEN], q_parts[:, h, :], k_lo[:, h, :], start=False, stop=True)\
                      .then_inc(scores_ready, 1)

                def transposes(i, k):
                    n = H * i + k
                    pe.wait_ge(probs_ready, n + 1)
                    if not (isinstance(n, int) and n < 2):
                        pe.wait_ge([probsT_act, probsT_dve][k % 2], H // 2 * i + k // 2)
                    for s in range(NS):
                        mm = pe.transpose(ps_t[k % 2][0:STRIP, s * P:(s + 1) * P],
                                          probs[:, k % 2, s * STRIP:(s + 1) * STRIP], ident[:, :])
                    mm.then_inc(probsT_ps, 1)

                def probs_v(i, k):
                    h = k % H
                    pe.wait_ge([probsT_act, probsT_dve][k % 2], H // 2 * i + k // 2 + 1)
                    if k % 4 == 0 and k >= 4:
                        pe.wait_ge(o_ready, 4 * i + k // 4 + 3)
                    dst = ps_o[h // 4 % 2][:, h % 4 * VW:(h % 4 + 1) * VW]
                    for s in range(NS):
                        mm = pe.matmul(dst, probsT[:, k % 2, s * P:(s + 1) * P], v_aug[:, s, h, :],
                                       start=(s == 0), stop=(s == NS - 1))
                    mm.then_inc(pv_ready, 1)

                def out_projection(i, step):
                    if step == 0:
                        pe.wait_ge(o_ready, 4 * i + 4)
                        pe.wait_ge(x2_ready, i + 1)
                        for p in range(4):
                            mm = pe.transpose(ps_b[:, p * P:(p + 1) * P], o_rows[:, p * P:(p + 1) * P], ident[:, :])
                        mm.then_inc(oT_a_ps, 1)
                    if step == 1:
                        pe.wait_ge(q_split, 2 * i + 2)
                        for p in range(4):
                            mm = pe.transpose(ps_a[:, p * P:(p + 1) * P], o_rows[:, (4 + p) * P:(5 + p) * P],
                                              ident[:, :])
                        mm.then_inc(oT_b_ps, 1)
                    if step == 7:
                        pe.wait_ge(oT_a, i + 1)
                        pe.wait_ge(oT_b, i + 1)
                    if 7 <= step <= 10:
                        for p in (2 * (step - 7), 2 * (step - 7) + 1):
                            mm = pe.matmul(ps_b[:, 0:D], oT[:, p, :], wo_sb[:, p, :], start=(p == 0),
                                           stop=(p == H // 2 - 1))
                        if step == 10:
                            mm.then_inc(wo_ps, 1)

                def next_queries(i, step):
                    if step == 3:
                        pe.wait_ge(oT_b, i + 1)
                    if step == 11:
                        pe.wait_ge(q_split, 2 * i + 3)
                    if 3 <= step <= 6 or 11 <= step <= 14:
                        mm = project_q(step - 3 if step < 7 else step - 7, i + 1)
                        if step in (6, 14):
                            mm.then_inc(q_ps, 1)

                for k in range(6):
                    scores(0, k)
                    if k >= 2:
                        transposes(0, k - 2)
                for k in range(2):
                    probs_v(0, k)
                with pe.Fori(0, NT) as i:
                    for j in range(H):
                        scores(i, j + 6)
                        transposes(i, j + 4)
                        probs_v(i, j + 2)
                        out_projection(i, j)
                        next_queries(i, j)
                for step in range(11):
                    out_projection(NT, step)
                pe.wait_ge(wo_ps, NT + 1)
                pe.nop().then_inc(attention_done, 1)

            with pe.If(last_block_only(pe)):
                fast_attention()
            def full_attention():
                pe.sem_inc(g_pv_block, 1)
                for c in range(2 * NB * NS):
                    half, s, (k0, _, _, w) = c % 2, c // 2 % NS, block_of(c // 2 // NS)
                    if c >= 2:
                        pe.wait_ge(g_v_ready, c - 1)
                    for k in range(KT):
                        mm = pe.matmul(ps_s[half][0:w, :], ctxT_sb[:, k, k0 + s * w:k0 + (s + 1) * w],
                                       wv_sb[:, k, half * 512:(half + 1) * 512], start=(k == 0), stop=(k == KT - 1))
                    mm.then_inc(g_v_ps, 1)
                pe.wait_ge(g_v_ready, 2 * NB * NS)
                pe.wait_ge(g_pads, 2)
                with pe.Fori(0, NT) as i:
                    pe.wait_ge(g_x2_ready, i + 1)
                    for half in range(2):
                        pe.wait_ge(q_split, 2 * i + half + 1)
                        for pair in range(4 * half, 4 * half + 4):
                            mm = project_q(pair, i)
                        mm.then_inc(q_ps, 1)
                    pe.wait_ge(q_split, 2 * i + 3)
                    pe.sem_inc(carried, 1)
                    with pe.Fori(0, H) as h:
                        n = H * i + h
                        pe.wait_ge(g_staged, 3 * n + 3)
                        for b in range(NB):
                            k0, keys, even, _ = block_of(b)
                            pe.wait_ge(g_klo_ready, NB * n + b + 1)
                            for k in range(KT):
                                mm = pe.matmul(ps_a[:, 0:even], g_wk2[:, k, :, :].rearrange("p c d -> p (c d)"),
                                               ctxT_sb[:, k, k0:k0 + even], start=(k == 0), stop=(k == KT - 1))
                            mm.then_inc(g_k_ps, 1)
                            pe.wait_ge(g_klo_ready, NB * n + b + 2)
                            pe.wait_ge(g_masked_ready, NB * n + b + 1)
                            pe.matmul(ps_s[0][:, 0:even], g_q[:, :], g_khi[:, 0:even], start=True, stop=False)
                            pe.matmul(ps_s[0][:, 0:even], g_q[:, :], g_klo[:, 0:even], start=False, stop=True)\
                              .then_inc(g_scores_ready, 1)
                        pe.wait_ge(g_probs_ready, n + 1)
                        pe.wait_ge(g_o_ready, n + 1)
                        for b in range(NB):
                            k0, _, _, w = block_of(b)
                            pe.wait_ge(g_probsT_ready, NB * n + b + 1)
                            for s in range(NS):
                                mm = pe.transpose(ps_t[0][0:w, s * P:(s + 1) * P],
                                                  g_probs[:, k0 + s * w:k0 + (s + 1) * w], ident[:, :])
                            mm.then_inc(g_probsT_ps, 1)
                            pe.wait_ge(g_probsT_ready, NB * n + b + 2)
                            for s in range(NS):
                                mm = pe.matmul(ps_o[0][:, 0:VW], g_probsT[0:w, s * P:(s + 1) * P],
                                               g_v[0:w, b * NS + s, bass.ds(h, 1), :].squeeze(1),
                                               start=(b == 0 and s == 0), stop=(b == NB - 1 and s == NS - 1))
                            mm.then_inc(g_pv_block, 1)
                    pe.wait_ge(g_o_ready, H * i + H + 1)
                    for half in range(2):
                        for p in range(4):
                            mm = pe.transpose([ps_b, ps_a][half][:, p * P:(p + 1) * P],
                                              o_rows[:, (4 * half + p) * P:(4 * half + p + 1) * P], ident[:, :])
                        mm.then_inc(g_oT_ps, 1)
                    pe.wait_ge(g_oT_ready, 2 * i + 2)
                    for p in range(H // 2):
                        mm = pe.matmul(ps_b[:, 0:D], oT[:, p, :], wo_sb[:, p, :], start=(p == 0), stop=(p == H // 2 - 1))
                    mm.then_inc(g_wo_ps, 1)
                pe.wait_ge(g_wo_ps, NT)
                pe.nop().then_inc(attention_done, 1)

            with pe.Else():
                full_attention()

            pe.wait_ge(attention_done, ENGINES)
            pe.wait_ge(xn2_ready, 1)
            for c in range(8):
                k, t0 = c // 4, 4 * (c % 4)
                if c >= 2:
                    pe.wait_ge([xn2T_act, xn2T_dve][c % 2], c // 2)
                for t in range(4):
                    mm = pe.transpose(ps_s[c % 2][:, t * P:(t + 1) * P], xn2[:, t0 + t, k * P:(k + 1) * P], ident[:, :])
                mm.then_inc(xn2T_ps, 1)
            pe.wait_ge(xn2T_act, 4)
            pe.wait_ge(xn2T_dve, 4)
            pe.wait_ge(wg_in, 16)
            for t in range(NT):
                for k in range(KT):
                    mm = pe.matmul(ps_o[1][:, t * NE:(t + 1) * NE], xnT[:, k, t * P:(t + 1) * P], wg_sb[:, k, :],
                                   start=(k == 0), stop=(k == KT - 1))
            mm.then_inc(logits_ps, 1)
            pe.wait_ge(both_ready, 1)
            flat = both[:, :, :].rearrange("p t e -> p (t e)")
            pe.matmul(ps_a[:, 0:NT * NE], before[:, :], flat, start=True, stop=True)
            pe.matmul(ps_b[:, 0:NT * NE], ones[:, :], flat, start=True, stop=True).then_inc(prefix_ps, 1)

            def transpose_x(s, buf, turns):
                pe.wait_ge(xg_in[buf], 16 * (turns + 1))
                if not (isinstance(s, int) and s == 0):
                    pe.wait_ge(xgT_ready, s)
                for k in range(KT):
                    mm = pe.transpose(ps_t[1][:, k * P:(k + 1) * P], xg[:, buf, k * P:(k + 1) * P], ident[:, :])
                mm.then_inc(xgT_ps, 1)

            def hidden(s, buf, expert, w, bank, done):
                for k in range(KT):
                    mm = pe.matmul(bank[:, :], xgT[:, buf, k, :], w[:, k, bass.ds(expert, 1), :].squeeze(1), start=(k == 0), stop=(k == KT - 1))
                mm.then_inc(done, 1)

            def first_hidden(s, buf, expert):
                pe.wait_ge(xgT_ready, s + 1)
                pe.wait_ge(experts_ready, expert + 1)
                if not (isinstance(s, int) and s == 0):
                    pe.wait_ge(silu_ready, s)
                hidden(s, buf, expert, w1_sb, ps_s[0], h1_ps)

            def second_hidden(s, buf, expert):
                if not (isinstance(s, int) and s == 0):
                    pe.wait_ge(gated_ready, s)
                hidden(s, buf, expert, w2_sb, ps_s[1], h2_ps)

            def transpose_gated(s):
                pe.wait_ge(gated_ready, s + 1)
                pe.wait_ge(gatedT_ready, s + 1)
                for k in range(HT):
                    mm = pe.transpose(ps_t[0][:, k * P:(k + 1) * P], gated[:, k * P:(k + 1) * P], ident[:, :])
                mm.then_inc(gatedT_ps, 1)

            def project_down(s, expert):
                pe.wait_ge(gatedT_ready, s + 2)
                pe.wait_ge(y_ready, s + 1)
                for k in range(HT):
                    mm = pe.matmul(ps_o[0][:, 0:D], gatedT[:, k, :], w3_sb[:, k, bass.ds(expert, 1), :].squeeze(1), start=(k == 0), stop=(k == HT - 1))
                mm.then_inc(y_ps, 1)

            pe.sem_inc(y_ps, 1)
            pe.wait_ge(sched_ready, 1)
            transpose_x(0, 0, 0)
            expert = table(pe, 1, 0, NE - 1)
            first_hidden(0, 0, expert)
            second_hidden(0, 0, expert)
            transpose_x(1, 1, 0)
            with pe.Fori(0, (NG - 1) // 2) as i:
                for b in range(2):
                    s = 2 * i + b
                    ahead = table(pe, 1, s + 1, NE - 1)
                    first_hidden(s + 1, 1 - b, ahead)
                    transpose_gated(s)
                    second_hidden(s + 1, 1 - b, ahead)
                    now = table(pe, 1, s, NE - 1)
                    transpose_x(s + 2, b, i + 1)
                    project_down(s, now)
            transpose_gated(NG - 1)
            project_down(NG - 1, table(pe, 1, NG - 1, NE - 1))


_INS = ["x", "ctx_1024", "mask_1x1xSxS2_bk0", "g_xattn", "g_ffn", "L0_xattn_Wq", "L0_xattn_Wk", "L0_xattn_Wv",
        "L0_xattn_Wo", "L0_ffn_Wg", "L0_ffn_W1", "L0_ffn_W2", "L0_ffn_W3"]


def kernel(**inputs):
    import numpy as np
    import concourse.bacc as bacc
    from concourse.bass_utils import run_bass_kernel_spmd

    a = {name: np.asarray(inputs[name]) for name in _INS}
    laid_out = {
        "x": a["x"][0],
        "ctxT": a["ctx_1024"][0].T,
        "mask": a["mask_1x1xSxS2_bk0"][0, 0],
        "g_xattn": a["g_xattn"],
        "g_ffn": a["g_ffn"],
        "Wq": a["L0_xattn_Wq"],
        "Wk": a["L0_xattn_Wk"],
        "Wv": a["L0_xattn_Wv"],
        "Wo": a["L0_xattn_Wo"],
        "WgT": a["L0_ffn_Wg"].T,
        "W1T": a["L0_ffn_W1"].transpose(0, 2, 1),
        "W2T": a["L0_ffn_W2"].transpose(0, 2, 1),
        "W3T": a["L0_ffn_W3"].transpose(0, 2, 1),
    }
    nc = bacc.Bacc("TRN2", target_bir_lowering=False, num_devices=1)
    arrays, args = {}, []
    for name, v in laid_out.items():
        v = np.ascontiguousarray(v)
        arrays[name + "_dram"] = v
        args.append(nc.dram_tensor(name + "_dram", v.shape, mybir.dt.from_np(v.dtype), kind="ExternalInput").ap())
    args.append(nc.dram_tensor("out_dram", (S, D), F32, kind="ExternalOutput").ap())
    build(nc, *args)
    r = run_bass_kernel_spmd(nc, [arrays], core_ids=[0])
    return r.results[0]["out_dram"].reshape(1, S, D)
```

```python
from contextlib import ExitStack

import concourse.bass as bass
from concourse import mybir

F32 = mybir.dt.float32
F32R = mybir.dt.float32r
BF16 = mybir.dt.bfloat16
I32 = mybir.dt.int32
U8 = mybir.dt.uint8
ALU = mybir.AluOpType
ACT = mybir.ActivationFunctionType
AX = mybir.AxisListType

P = 128
S = 2048
SK = 1601
D = 256
H = 16
HD = 64
KT = D // P
NT = S // P
PAIR = 2 * P
NI = NT // 2
LOW0 = 32
UNITS = 2 * H
NB = 4
BK = 400
LASTK = SK - (NB - 1) * BK
LASTP = 404
NS = 4
STRIP = LASTP // NS
EVEN = LASTK + LASTK % 2
SKP = (NB - 1) * BK + LASTP
MT = 2
NM = NT // MT
LAST0 = (NB - 1) * BK
VW = HD + 1
MASKED = float(2.0 ** 125)
EPS = 1e-5
NE = 8
FH = 512
HT = FH // P
REGION = S + P
NG = 2 * S // P + NE - 1
NSCHED = NG
NOWHERE = NE * REGION
W_COL, ID_COL, XW = D, D + 1, D + 2
RING = 4


def block_of(b):
    last = b == NB - 1
    return b * BK, LASTK if last else BK, EVEN if last else BK, STRIP if last else BK // NS


def build(nc, x, ctxT, mask, g_xattn, g_ffn, Wq, Wk, Wv, Wo, WgT, W1T, W2T, W3T, out):
    with ExitStack() as ctx:
        def sb(name, shape, dt, scope=ctx):
            return scope.enter_context(nc.sbuf_tensor(name, shape, dt))

        def psum(name):
            return ctx.enter_context(nc.psum_tensor(name, [P, 512], F32))

        def sem(name):
            return ctx.enter_context(nc.semaphore(name))

        xs = sb("xs", [P, NT, D], F32)
        xnT = sb("xnT", [P, KT, S], F32)
        ident = sb("ident", [P, P], F32)
        ones = sb("ones", [P, P], F32)
        before = sb("before", [P, P], F32)
        stat = sb("stat", [P, 4, NT], F32)
        gates = sb("gates", [P, 2], F32)
        tanh_g = sb("tanh_g", [P, 2], F32)
        halves = sb("halves", [P, NT, 6], F32)
        mean_var = sb("mean_var", [P, NT, 2], F32)
        word_max = sb("word_max", [P, 2, NT], F32)
        rowflag = sb("rowflag", [P, 4], F32)
        plainflag = sb("plainflag", [1, 1], I32)
        wg_sb = sb("wg_sb", [P, KT, NE], F32)
        rank = sb("rank", [P, NE], F32)
        number = sb("number", [P, NE], F32)
        row_no = sb("row_no", [P, NT + 1], F32)
        fill = sb("fill", [P, NT], F32)
        turn = sb("turn", [P, NSCHED], F32)
        with ExitStack() as attn:
            with ExitStack() as early:
                wk2_sb = sb("wk2_sb", [P, KT, H, 2, HD], F32, early)
            q_parts = sb("q_parts", [P, H, PAIR], F32R, attn)
            wq_sb = sb("wq_sb", [P, KT, H * HD], F32, attn)
            wo_sb = sb("wo_sb", [P, H // 2, D], F32, attn)
            with ExitStack() as fast:
                biases = sb("biases", [P, NT, LASTK], BF16, fast)
                k_hi = sb("k_hi", [P, H, EVEN], F32R, fast)
                k_lo = sb("k_lo", [P, H, EVEN], F32R, fast)
                v_parts = sb("v_parts", [STRIP, NS, H, 2, HD], F32R, fast)
                with ExitStack() as early:
                    ctx_last = sb("ctx_last", [P, KT, LASTP], F32, early)
                    wk_sb = sb("wk_sb", [P, KT, H * HD], F32, early)
                    wv_sb = sb("wv_sb", [P, KT, H * HD], F32, early)
                    mask8 = sb("mask8", [P, 2, MT, SKP], U8, early)
                    xn = sb("xn", [P, NT, D], F32, early)
                bias_cur = sb("bias_cur", [P, 2, 2, LASTK], BF16, fast)
                masked = sb("masked", [P, 2, LASTK], F32, fast)
                probs = sb("probs", [P, 2, LASTP], F32, fast)
                probsT = sb("probsT", [STRIP, 2, NS, 2, PAIR], F32R, fast)
                oT = sb("oT", [P, 4, PAIR], F32, fast)
                neg_max = sb("neg_max", [P, 2], F32, fast)
                sum_exp = sb("sum_exp", [P, 2, 2, 4], F32, fast)
                inv_sum = sb("inv_sum", [P, 2, 4], F32, fast)
                invT = sb("invT", [LOW0 + 4, PAIR], F32R, fast)
                head_of_f = sb("head_of_f", [LOW0 + 4, 2, 2, HD], F32, fast)
                head_of = sb("head_of", [LOW0 + 4, 2, 2, HD], F32R, fast)
            with ExitStack() as slow:
                g_ctxT = sb("g_ctxT", [P, KT, SKP], F32, slow)
                g_v = sb("g_v", [STRIP, NB * NS, H, VW], F32, slow)
                g_wv = sb("g_wv", [P, KT, H * HD], F32, slow)
                o_rows = sb("o_rows", [P, H * HD], F32, slow)
                g_oT = sb("g_oT", [P, H // 2, P], F32, slow)
                g_wk = sb("g_wk", [P, KT, H * HD], F32, slow)
                g_wk2 = sb("g_wk2", [P, KT, 2, HD], F32, slow)
                g_q = sb("g_q", [P, P], F32R, slow)
                g_khi = sb("g_khi", [P, EVEN], F32R, slow)
                g_klo = sb("g_klo", [P, EVEN], F32R, slow)
                g_mask8 = sb("g_mask8", [P, SK], U8, slow)
                g_bias = sb("g_bias", [P, SK], BF16, slow)
                g_probs = sb("g_probs", [P, SKP], F32, slow)
                g_probsT = sb("g_probsT", [STRIP, NS * P], F32, slow)
                g_min = sb("g_min", [P, 8], F32, slow)
        with ExitStack() as ffn:
            w1_sb = sb("w1_sb", [P, KT, NE, FH], F32, ffn)
            w2_sb = sb("w2_sb", [P, KT, NE, FH], F32, ffn)
            w3_sb = sb("w3_sb", [P, HT, NE, D], F32, ffn)
            xn2 = sb("xn2", [P, 2, NT, XW], F32, ffn)
            sq2 = sb("sq2", [P, NT, D], F32, ffn)
            chosen = sb("chosen", [P, 2, NT, NE], F32, ffn)
            logits = sb("logits", [P, NT, NE], F32, ffn)
            work = sb("work", [P, NT, NE], F32, ffn)
            both = sb("both", [P, NT, NE], F32, ffn)
            sums = sb("sums", [P, 2, NT, NE], F32, ffn)
            place_f = sb("place_f", [P, NT, NE], F32, ffn)
            top = sb("top", [P, 2, NT], F32, ffn)
            pick = sb("pick", [P, NT], F32, ffn)
            weight = sb("weight", [P, 2, NT], F32, ffn)
            denom = sb("denom", [P, 2, NT], F32, ffn)
            place = sb("place", [P, 2, NT], I32, ffn)
            tiles = sb("tiles", [P, 4, NE], F32, ffn)
            has_tile = sb("has_tile", [P, NE, NT], F32, ffn)
            sched_f = sb("sched_f", [1, 4, NSCHED, NE], F32, ffn)
            sched_s = sb("sched_s", [1, 2, NSCHED], F32, ffn)
            sched = sb("sched", [1, 2, NSCHED], I32, ffn)
            pad_row_f = sb("pad_row_f", [1, NE], F32, ffn)
            pad_row = sb("pad_row", [1, NE], I32, ffn)
            pads = sb("pads", [P, XW], F32, ffn)
            xg = sb("xg", [P, RING, XW], F32, ffn)
            ids = sb("ids", [P, RING], I32, ffn)
            xgT = sb("xgT", [P, 2, KT, P], F32, ffn)
            silu = sb("silu", [P, FH], F32, ffn)
            gated = sb("gated", [P, FH], F32, ffn)
            gatedT = sb("gatedT", [P, HT, P], F32, ffn)
            yg = sb("yg", [P, 2, D], F32, ffn)

        ps_s = [psum("ps_s0"), psum("ps_s1")]
        ps_t = [psum("ps_t0"), psum("ps_t1")]
        ps_o = [psum("ps_o0"), psum("ps_o1")]
        ps_a, ps_b = psum("ps_a"), psum("ps_b")

        x_in, w_in, g_in = sem("x_in"), sem("w_in"), sem("g_in")
        kv_in, wv_in, wk2_act, wk2_dve = sem("kv_in"), sem("wv_in"), sem("wk2_act"), sem("wk2_dve")
        mask_in = [sem("mask0_in"), sem("mask1_in")]
        mask_pad, mask_seen, biases_ready = sem("mask_pad"), sem("mask_seen"), sem("biases_ready")
        const_ready, pads_ready = sem("const_ready"), sem("pads_ready")
        ln_stat, ln = sem("ln_stat"), sem("ln")
        std_ready, xn_ready = sem("std_ready"), sem("xn_ready")
        tanh_ready = sem("tanh_ready")
        flag_step, flag_sum, flag_ready = sem("flag_step"), sem("flag_sum"), sem("flag_ready")
        xnT_ps, xnT_act, xnT_dve = sem("xnT_ps"), sem("xnT_act"), sem("xnT_dve")
        q_ps, q_hi, q_split = sem("q_ps"), sem("q_hi"), sem("q_split")
        k_ps, k_hi_ready, k_lo_ready = sem("k_ps"), sem("k_hi_ready"), sem("k_lo_ready")
        v_ps, v_hi_ready, v_lo_ready = sem("v_ps"), sem("v_hi_ready"), sem("v_lo_ready")
        pads_set, bias_in = sem("pads_set"), [sem("bias0_in"), sem("bias1_in")]
        scores_ready, masked_ready, probs_ready = sem("scores_ready"), sem("masked_ready"), sem("probs_ready")
        inv_ready, invT_ps, invT_hi, invT_lo = sem("inv_ready"), sem("invT_ps"), sem("invT_hi"), sem("invT_lo")
        inv_spread, normed, head_of_set = sem("inv_spread"), sem("normed"), sem("head_of_set")
        probsT_ps, probsT_hi, probsT_lo = sem("probsT_ps"), sem("probsT_hi"), sem("probsT_lo")
        pv_ready, o_low, oT_ready = sem("pv_ready"), sem("o_low"), sem("oT_ready")
        wo_ps, x2_ready = sem("wo_ps"), sem("x2_ready")
        attention_done = sem("attention_done")
        stored = sem("stored")
        carried = sem("carried")

        g_w_in, g_mask_in, g_bias_ready, g_pads = sem("g_w_in"), sem("g_mask_in"), sem("g_bias_ready"), sem("g_pads")
        g_v_ps, g_v_ready, g_staged = sem("g_v_ps"), sem("g_v_ready"), sem("g_staged")
        g_k_ps, g_khi_ready, g_klo_ready = sem("g_k_ps"), sem("g_khi_ready"), sem("g_klo_ready")
        g_scores_ready, g_masked_ready, g_min_ready = sem("g_scores_ready"), sem("g_masked_ready"), sem("g_min_ready")
        g_probs_ready, g_probsT_ps, g_probsT_ready = sem("g_probs_ready"), sem("g_probsT_ps"), sem("g_probsT_ready")
        g_pv_block, g_inv_ready, g_o_ready = sem("g_pv_block"), sem("g_inv_ready"), sem("g_o_ready")
        g_oT_ps, g_oT_ready, g_wo_ps, g_x2_ready = sem("g_oT_ps"), sem("g_oT_ready"), sem("g_wo_ps"), sem("g_x2_ready")

        xn2_ready, sq2_ready, std2_ready, ln2 = sem("xn2_ready"), sem("sq2_ready"), sem("std2_ready"), sem("ln2")
        xn2T_ps, xn2T_act, xn2T_dve = sem("xn2T_ps"), sem("xn2T_act"), sem("xn2T_dve")
        logits_ps, both_ready, prefix_ps = sem("logits_ps"), sem("both_ready"), sem("prefix_ps")
        route, exp_gap_ready, diff_ready = sem("route"), sem("exp_gap_ready"), sem("diff_ready")
        places_ready, weights_set, ids_set = sem("places_ready"), sem("weights_set"), sem("ids_set")
        sched_ready, pads_made, xn2_twice = sem("sched_ready"), sem("pads_made"), sem("xn2_twice")
        scattered, padded = sem("scattered"), sem("padded")
        expert_in = [sem(f"expert{e}_in") for e in range(NE)]
        experts_ready = sem("experts_ready")
        xg_in = [sem(f"xg{n}_in") for n in range(RING)]
        xgT_ps, xgT_ready = sem("xgT_ps"), sem("xgT_ready")
        h1_ps, h2_ps, silu_ready, gated_ready = sem("h1_ps"), sem("h2_ps"), sem("silu_ready"), sem("gated_ready")
        gatedT_ps, gatedT_ready = sem("gatedT_ps"), sem("gatedT_ready")
        y_ps, y_ready = sem("y_ps"), sem("y_ready")
        ids_ready, added = sem("ids_ready"), sem("added")
        wg_in = sem("wg_in")

        x_regrouped = nc.dram_tensor("x_regrouped", (NOWHERE + P, XW), F32, kind="Internal").ap()

        block = ctx.enter_context(nc.Block())

        def first(n, count):
            return isinstance(n, int) and n < count

        def table(eng, row, s, top_value):
            return eng.value_load(sched[0:1, row, bass.ds(s, 1)], min_val=0, max_val=top_value)


        def settled(eng):
            eng.wait_ge(w_in, W_ALL)
            eng.wait_ge(k_lo_ready, H)
            eng.wait_ge(v_lo_ready, 2 * NS)
            eng.wait_ge(biases_ready, NM)
            eng.wait_ge(pads_set, 1)

        def last_block_only(eng):
            eng.wait_ge(flag_ready, 1)
            return eng.value_load(plainflag[0:1, 0:1], min_val=0, max_val=1) == 1

        W_ALL = 16 * 2

        CTX_WK = 16 * 2
        PADS = 1
        ENGINES = 5
        CONSTS = 10


        @block.sync
        def _(sp):
            sp.dma_start(ctx_last[:, :, 0:LASTK], ctxT[:, LAST0:].rearrange("(k p) n -> p k n", p=P)).then_inc(kv_in, 16)
            sp.dma_start(wk_sb[:, :, :], Wk.rearrange("(k p) n -> p k n", p=P)).then_inc(kv_in, 16)
            sp.dma_start(xs[:, :, :], x.rearrange("(t p) d -> p t d", p=P)).then_inc(x_in, 16)
            sp.dma_start(wv_sb[:, :, :], Wv.rearrange("(k p) n -> p k n", p=P)).then_inc(wv_in, 16)
            sp.wait_ge(mask_pad, 1)
            for c in range(NM):
                if c >= 2:
                    sp.wait_ge(mask_seen, 2 * c - 2)
                    sp.wait_ge(biases_ready, c - 1)
                sp.dma_start(mask8[:, c % 2, :, 0:SK], mask[c * MT * P:(c + 1) * MT * P, :]
                             .rearrange("(t p) k -> p t k", p=P)).then_inc(mask_in[c % 2], 16)
                if c == 1:
                    sp.dma_start(wq_sb[:, :, :], Wq.rearrange("(k p) n -> p k n", p=P)).then_inc(w_in, 16)
                    sp.dma_start(wo_sb[:, :, :], Wo.rearrange("(k p) n -> p k n", p=P)).then_inc(w_in, 16)
            sp.dma_start(wg_sb[:, :, :], WgT.rearrange("(k p) e -> p k e", p=P)).then_inc(wg_in, 16)
            with sp.If(last_block_only(sp)):
                sp.wait_ge(biases_ready, NM)
                for half in range(2):
                    sp.dma_start(bias_cur[:, half, :, :], biases[:, 0:2, :]).then_inc(bias_in[half], 16)
                with sp.Fori(1, NI) as i:
                    for half in range(2):
                        sp.wait_ge(masked_ready, UNITS * i - UNITS + H * (half + 1))
                        sp.dma_start(bias_cur[:, half, :, :], biases[:, bass.ds(2 * i, 2), :]).then_inc(bias_in[half], 16)
                sp.nop().then_inc(attention_done, 1)
            with sp.Else():
                settled(sp)
                sp.dma_start(g_wk[:, :, :], Wk.rearrange("(k p) n -> p k n", p=P)).then_inc(g_w_in, 16)
                sp.dma_start(g_wv[:, :, :], Wv.rearrange("(k p) n -> p k n", p=P)).then_inc(g_w_in, 16)
                sp.dma_start(g_ctxT[:, :, 0:SK], ctxT.rearrange("(k p) n -> p k n", p=P)).then_inc(g_w_in, 16)
                with sp.Fori(0, NT) as i:
                    sp.wait_ge(g_bias_ready, i + 1)
                    sp.dma_start(g_mask8[:, :], mask[bass.ts(i, P), :]).then_inc(g_mask_in, 16)
                sp.nop().then_inc(attention_done, 1)
            sp.wait_ge(attention_done, ENGINES)
            for e in range(NE):
                sp.dma_start(w1_sb[:, :, e, :], W1T[e].rearrange("(k p) n -> p k n", p=P)).then_inc(expert_in[e], 16)
                sp.dma_start(w2_sb[:, :, e, :], W2T[e].rearrange("(k p) n -> p k n", p=P)).then_inc(expert_in[e], 16)
                sp.dma_start(w3_sb[:, :, e, :], W3T[e].rearrange("(k p) n -> p k n", p=P)).then_inc(expert_in[e], 16)
            for c in range(4):
                sp.dma_start(out[c * 4 * P:(c + 1) * 4 * P, :].rearrange("(t p) d -> p t d", p=P),
                             xs[:, 4 * c:4 * c + 4, :]).then_inc(stored, 16)
            sp.wait_ge(pads_made, 2)
            sp.dma_start(out[S:, :], pads[:, 0:D]).then_inc(stored, 16)
            sp.dma_start(x_regrouped[NOWHERE:, :], pads[:, :]).then_inc(padded, 16)
            sp.wait_ge(sched_ready, 1)
            for e in range(NE):
                row = sp.value_load(pad_row[0:1, e:e + 1], min_val=0, max_val=(NE - 1) * REGION + S)
                sp.dma_start(x_regrouped[bass.ds(row, P), :], pads[:, :]).then_inc(padded, 16)
            sp.wait_ge(padded, 16 * (NE + 1))
            sp.wait_ge(scattered, 16 * 2 * NT)

            def load_tile(i, k):
                s = RING * i + k
                if not first(s, RING):
                    sp.wait_ge(y_ready, s - RING + 2)
                row = table(sp, 0, s, NOWHERE)
                sp.dma_start(xg[:, k % RING, :], x_regrouped[bass.ds(row, P), :]).then_inc(xg_in[k % RING], 16)

            for k in range(RING):
                load_tile(0, k)
            with sp.Fori(1, NG // RING) as i:
                for k in range(RING):
                    load_tile(i, k)
            for k in range(NG % RING):
                load_tile(NG // RING, k)
            sp.wait_ge(stored, 5 * 16)
            sp.wait_ge(added, 16 * NG)

        @block.gpsimd
        def _(pool):
            pool.memset(mask8[:, :, :, SKP - 4:], 0).then_inc(mask_pad, 1)
            pool.memset(ctx_last[:, :, LASTK:], 0.0).then_inc(pads_ready, 1)
            pool.dma_start(gates[:, 0:1], g_xattn.partition_broadcast(P)).then_inc(g_in, 16)
            pool.dma_start(gates[:, 1:2], g_ffn.partition_broadcast(P)).then_inc(g_in, 16)
            pool.memset(ident[:, :], 0.0).then_inc(const_ready, 1)
            pool.wait_ge(const_ready, 1)
            pool.affine_select(out=ident[:, :], in_=ident[:, :], compare_op=ALU.not_equal, fill=1.0, base=0,
                               pattern=[[-1, P]], channel_multiplier=1).then_inc(const_ready, 1)
            pool.memset(ones[:, :], 1.0).then_inc(const_ready, 1)
            pool.memset(before[:, :], 1.0).then_inc(const_ready, 1)
            pool.wait_ge(const_ready, 4)
            pool.affine_select(out=before[:, :], in_=before[:, :], compare_op=ALU.is_gt, fill=0.0, base=0,
                               pattern=[[1, P]], channel_multiplier=-1).then_inc(const_ready, 1)
            for tile, base, step, n in ((rank, NE, -1, NE), (number, 0, 1, NE), (fill, 0, P, NT), (turn, 0, 1, NSCHED)):
                pool.iota(tile[:, :], pattern=[[step, n]], base=base, channel_multiplier=0,
                          allow_small_or_imprecise_dtypes=True).then_inc(const_ready, 1)
            pool.iota(row_no[:, :], pattern=[[P, NT + 1]], base=0, channel_multiplier=1,
                      allow_small_or_imprecise_dtypes=True).then_inc(const_ready, 1)
            for c in range(NM):
                pool.wait_ge(mask_in[c % 2], 16 * (c // 2 + 1))
                pool.tensor_scalar(biases[:, c * MT:(c + 1) * MT, :], mask8[:, c % 2, :, LAST0:SK], -MASKED, MASKED,
                                   ALU.mult, ALU.add).then_inc(biases_ready, 1)
            pool.wait_ge(xnT_ps, 8)
            pool.wait_ge(biases_ready, NM)
            pool.memset(probs[:, :, LASTK:], 0.0).then_inc(pads_set, 1)
            with pool.If(last_block_only(pool)):
                pool.memset(invT[:, :].bitcast(F32), 0.0).then_inc(head_of_set, 1)
                pool.memset(head_of_f[:, :, :, :], 0.0).then_inc(head_of_set, 1)
                for part in range(2):
                    pool.wait_ge(head_of_set, part + 2)
                    pool.affine_select(out=head_of_f[:, :, :, :], in_=head_of_f[:, :, :, :], compare_op=ALU.not_equal,
                                       fill=1.0, base=-part * LOW0, pattern=[[-2, 2], [-1, 2], [0, HD]],
                                       channel_multiplier=1).then_inc(head_of_set, 1)
                pool.wait_ge(head_of_set, 4)
                pool.tensor_copy(head_of[:, :, :, :], head_of_f[:, :, :, :]).then_inc(head_of_set, 1)
                pool.wait_ge(head_of_set, 5)
                pool.nop().then_inc(attention_done, 1)
            with pool.Else():
                settled(pool)
                pool.memset(g_ctxT[:, :, SK:], 0.0).then_inc(g_pads, 1)
                pool.memset(g_v[:, :, :, HD:], 1.0).then_inc(g_pads, 1)
                pool.memset(g_probs[:, SK:], 0.0).then_inc(g_pads, 1)
                pool.wait_ge(g_pads, 3)
                pool.nop().then_inc(attention_done, 1)

            pool.wait_ge(attention_done, ENGINES)
            pool.memset(pads[:, :], 0.0).then_inc(pads_made, 1)
            pool.wait_ge(pads_made, 1)
            pool.tensor_copy(pads[:, ID_COL:], row_no[:, NT:]).then_inc(pads_made, 1)
            for c in range(2):
                pool.tensor_copy(xn2[:, c, :, ID_COL:], row_no[:, 0:NT].unsqueeze(2)).then_inc(ids_set, 1)
            pool.wait_ge(ids_set, 2)
            pool.wait_ge(weights_set, 2)
            pool.wait_ge(xn2_ready, 1)
            pool.wait_ge(xn2_twice, 1)
            pool.wait_ge(places_ready, 1)
            for t in range(NT):
                for c in range(2):
                    pool.indirect_dma_start(out=x_regrouped, out_offset=bass.IndirectOffsetOnAxis(ap=place[:, c, t:t + 1], axis=0),
                                            in_=xn2[:, c, t, :], in_offset=None).then_inc(scattered, 16)
            for e in range(NE):
                pool.wait_ge(expert_in[e], 48)
                pool.nop().then_inc(experts_ready, 1)
            pool.wait_ge(stored, 5 * 16)

            def add_tile(i, k):
                s = RING * i + k
                pool.wait_ge(y_ready, s + 2)
                pool.wait_ge(ids_ready, s + 1)
                if not first(s, 1):
                    pool.wait_ge(added, 16 * s)
                if not isinstance(s, int):
                    pool.sem_inc(carried, 1)
                pool.indirect_dma_start(out=out, out_offset=bass.IndirectOffsetOnAxis(ap=ids[:, k % RING:k % RING + 1], axis=0),
                                        in_=yg[:, k % 2, :], in_offset=None, compute_op=ALU.add).then_inc(added, 16)

            for k in range(RING):
                add_tile(0, k)
            with pool.Fori(1, NG // RING) as i:
                for k in range(RING):
                    add_tile(i, k)
            for k in range(NG % RING):
                add_tile(NG // RING, k)

        @block.scalar
        def _(act):
            act.wait_ge(kv_in, CTX_WK)
            for copy in range(2):
                act.copy(wk2_sb[:, 0, :, copy, :], wk_sb[:, 0, :].rearrange("p (h d) -> p h d", h=H)).then_inc(wk2_act, 1)
            for h in range(H):
                if h == H // 2:
                    act.wait_ge(ln, 2)
                    act.activation(stat[:, 2, :], stat[:, 1, :], ACT.Sqrt).then_inc(std_ready, 1)
                act.wait_ge(k_ps, h + 1)
                act.mul(k_hi[:, h, :], [ps_a, ps_b][h % 2][:, 0:EVEN], -1.0).then_inc(k_hi_ready, 1)
            for c in range(0, 8, 2):
                act.wait_ge(xnT_ps, c + 1)
                k, t0 = c % 2, 4 * (c // 2)
                act.copy(xnT[:, k, t0 * P:(t0 + 4) * P], ps_t[0][:, :]).then_inc(xnT_act, 1)
                for half in range(2):
                    act.wait_ge(v_ps, c + half + 1)
                    act.copy(v_parts[:, c // 2, 8 * half:8 * half + 8, 0, :],
                             ps_s[half][0:STRIP, :].rearrange("p (h d) -> p h d", h=8)).then_inc(v_hi_ready, 1)
            act.wait_ge(g_in, 32)
            act.activation(tanh_g[:, :], gates[:, :], ACT.Tanh).then_inc(tanh_ready, 1)

            def q_high_parts(b, batch, odd, bank=ps_a):
                act.wait_ge(q_ps, batch + 1)
                src = bank[:, :].rearrange("p (c n) -> p c n", c=2)
                p0 = odd * HD
                act.copy(q_parts[p0:p0 + HD, 4 * b + odd:4 * b + 4:2, :], src[p0:p0 + HD]).then_inc(q_hi, 1)

            for b in range(4):
                for odd in range(2):
                    q_high_parts(b, b, odd, [ps_a, ps_b][b % 2])

            def fast_attention():
                def exps(i, k):
                    n = UNITS * i + k
                    act.wait_ge(masked_ready, n + 1)
                    if not first(n, 2):
                        act.wait_ge(probsT_ps, n - 1)
                    act.activation(probs[:, k % 2, 0:LASTK], masked[:, k % 2, :], ACT.Exp,
                                   bias=neg_max[:, k % 2:k % 2 + 1], scale=-1.0,
                                   accum_out=sum_exp[:, k // 8 % 2, k % 2, k // 2 % 4:k // 2 % 4 + 1]).then_inc(probs_ready, 1)

                def high_inverses(i, g):
                    act.wait_ge(invT_ps, 4 * i + g + 1)
                    act.copy(invT[0:4, :], ps_b[0:4, 0:PAIR]).then_inc(invT_hi, 1)

                def high_probs(i, k):
                    n, head = UNITS * i + k, H * i + k // 2
                    act.wait_ge(probsT_ps, n + 1)
                    if not first(head, 2):
                        act.wait_ge(pv_ready, head - 1)
                    act.copy(probsT[:, k // 2 % 2, :, 0, k % 2 * P:(k % 2 + 1) * P],
                             ps_t[k % 2][0:STRIP, :].rearrange("p (s n) -> p s n", s=NS)).then_inc(probsT_hi, 1)

                def output_of_low_v(i, h):
                    act.wait_ge(pv_ready, H * i + h + 1)
                    if not first(4 * i + h // 4, 2):
                        act.wait_ge(wo_ps, 4 * i + h // 4 - 1)
                    p0 = h % 2 * HD
                    act.copy(oT[p0:p0 + HD, h // 2 % 4, :], ps_o[h % 2][HD:P, 0:PAIR]).then_inc(o_low, 1)

                def step(i, j, last=False):
                    if not (last and j + 5 >= UNITS):
                        exps(i, j + 5)
                    if j + 4 >= 0 and not (last and j + 4 >= UNITS):
                        high_probs(i, j + 4)
                    if j >= 0 and j % 2 == 1:
                        output_of_low_v(i, j // 2)
                    if j >= 0 and j % 8 == 4:
                        high_inverses(i, j // 8)
                    if j >= 0 and j % 8 == 6 and not last:
                        q_high_parts(j // 8, 4 * i + 4 + j // 8, 0)
                    if j >= 8 and j % 8 == 0 and not last:
                        q_high_parts(j // 8 - 1, 4 * i + 3 + j // 8, 1)
                    if j == 0 and not first(i, 1):
                        q_high_parts(3, 4 * i + 3, 1)

                for j in range(-5, UNITS):
                    step(0, j)
                with act.Fori(1, NI - 1) as i:
                    for j in range(UNITS):
                        step(i, j)
                for j in range(UNITS):
                    step(NI - 1, j, last=True)
                act.wait_ge(probs_ready, UNITS * NI)
                act.wait_ge(o_low, H * NI)
                act.nop().then_inc(attention_done, 1)

            with act.If(last_block_only(act)):
                fast_attention()
            def full_attention():
                settled(act)
                act.sem_inc(g_probsT_ready, 1)
                for c in range(2 * NB * NS):
                    act.wait_ge(g_v_ps, c + 1)
                    half, w = c % 2, block_of(c // 2 // NS)[3]
                    act.copy(g_v[0:w, c // 2, 8 * half:8 * half + 8, 0:HD],
                             ps_s[half][0:w, :].rearrange("p (h d) -> p h d", h=8)).then_inc(g_v_ready, 1)
                with act.Fori(0, NT) as i:
                    for half in range(2):
                        act.wait_ge(q_ps, 2 * i + half + 5)
                        src = ps_a[:, :].rearrange("p (c n) -> p c n", c=4)
                        act.copy(q_parts[0:HD, 8 * half:8 * half + 8:2, 0:P], src[0:HD]).then_inc(q_hi, 1)
                        act.copy(q_parts[HD:P, 8 * half + 1:8 * half + 8:2, 0:P], src[HD:P]).then_inc(q_hi, 1)
                    with act.Fori(0, H) as h:
                        n = H * i + h
                        for b in range(NB):
                            act.wait_ge(g_k_ps, NB * n + b + 1)
                            act.mul(g_khi[:, 0:block_of(b)[2]], ps_a[:, 0:block_of(b)[2]], -1.0).then_inc(g_khi_ready, 1)
                        act.wait_ge(g_min_ready, n + 1)
                        act.activation(g_probs[:, 0:SK], g_probs[:, 0:SK], ACT.Exp, bias=g_min[:, 4:5], scale=-1.0)\
                           .then_inc(g_probs_ready, 1)
                        for b in range(NB):
                            w = block_of(b)[3]
                            act.wait_ge(g_probsT_ps, NB * n + b + 1)
                            act.copy(g_probsT[0:w, :], ps_t[0][0:w, :]).then_inc(g_probsT_ready, 1)
                    for half in range(2):
                        act.wait_ge(g_oT_ps, 2 * i + half + 1)
                        act.copy(g_oT[:, 4 * half:4 * half + 4, :],
                                 [ps_b, ps_a][half][:, :].rearrange("p (c n) -> p c n", c=4)).then_inc(g_oT_ready, 1)
                act.wait_ge(g_oT_ready, 2 * NT)
                act.nop().then_inc(attention_done, 1)

            with act.Else():
                full_attention()

            act.wait_ge(attention_done, ENGINES)
            act.wait_ge(ln2, 3)
            act.activation(sq2[:, :, :], xn2[:, 0, :, 0:D], ACT.Square).then_inc(sq2_ready, 1)
            act.wait_ge(ln2, 5)
            act.activation(stat[:, 2, :], stat[:, 1, :], ACT.Sqrt).then_inc(std2_ready, 1)
            for c in range(0, 8, 2):
                act.wait_ge(xn2T_ps, c + 1)
                k, t0 = c // 4, 4 * (c % 4)
                act.copy(xnT[:, k, t0 * P:(t0 + 4) * P], ps_s[0][:, :]).then_inc(xn2T_act, 1)
            act.copy(xn2[:, 1, :, 0:D], xn2[:, 0, :, 0:D]).then_inc(xn2_twice, 1)
            act.wait_ge(diff_ready, 1)
            act.activation(denom[:, 0, :], pick[:, :], ACT.Exp).then_inc(exp_gap_ready, 1)

            def copy_xgT(s, buf):
                act.wait_ge(xgT_ps, s + 1)
                act.copy(xgT[:, buf, :, :], ps_t[1][:, 0:KT * P].rearrange("p (k n) -> p k n", k=KT))\
                   .then_inc(xgT_ready, 1)

            def silu_of(s):
                act.wait_ge(h1_ps, s + 1)
                if not (isinstance(s, int) and s == 0):
                    act.wait_ge(gated_ready, s)
                act.activation(silu[:, :], ps_s[0][:, :], ACT.Silu).then_inc(silu_ready, 1)

            def copy_gatedT(s):
                act.wait_ge(gatedT_ps, s + 1)
                if not (isinstance(s, int) and s == 0):
                    act.wait_ge(y_ps, s + 1)
                act.copy(gatedT[:, :, :], ps_t[0][:, :].rearrange("p (k n) -> p k n", k=HT)).then_inc(gatedT_ready, 1)

            def ffn_tile(i, k):
                s = RING * i + k
                copy_gatedT(s)
                if not (isinstance(s, int) and s + 1 >= NG):
                    silu_of(s + 1)
                if not (isinstance(s, int) and s + 2 >= NG):
                    copy_xgT(s + 2, k % 2)

            act.sem_inc(gatedT_ready, 1)
            copy_xgT(0, 0)
            silu_of(0)
            copy_xgT(1, 1)
            with act.Fori(0, NG // RING) as i:
                for k in range(RING):
                    ffn_tile(i, k)
            for k in range(NG % RING):
                ffn_tile(NG // RING, k)

        @block.vector
        def _(dve):
            def rows(col):
                return stat[:, col, :].unsqueeze(2).to_broadcast([P, NT, D])

            dve.wait_ge(kv_in, CTX_WK)
            for copy in range(2):
                dve.tensor_copy(wk2_sb[:, 1, :, copy, :], wk_sb[:, 1, :].rearrange("p (h d) -> p h d", h=H))\
                   .then_inc(wk2_dve, 1)
            def q_low_parts(b, batch, odd, bank=ps_a):
                dve.wait_ge(q_hi, 2 * batch + odd + 1)
                src = bank[:, :].rearrange("p (c n) -> p c n", c=2)
                heads = q_parts[:, 4 * b + odd:4 * b + 4:2, :]
                p0, p1 = odd * HD, (1 - odd) * HD
                dve.tensor_tensor(heads[p1:p1 + HD], src[p0:p0 + HD], heads[p0:p0 + HD], ALU.subtract)\
                   .then_inc(q_split, 1)

            def mask_words(c):
                dve.wait_ge(mask_in[c % 2], 16 * (c // 2 + 1))
                words = mask8[:, c % 2, :, :].bitcast(I32)
                dve.tensor_reduce(word_max[:, 0, c:c + 1], words[:, :, 0:LAST0 // 4], AX.XY, ALU.max).then_inc(mask_seen, 1)
                dve.tensor_reduce(word_max[:, 1, c * MT:(c + 1) * MT], words[:, :, LAST0 // 4:], AX.X, ALU.max)\
                   .then_inc(mask_seen, 1)

            def k_low(h):
                dve.wait_ge(k_hi_ready, h + 1)
                dve.scalar_tensor_tensor(out=k_lo[:, h, :], in0=[ps_a, ps_b][h % 2][:, 0:EVEN], scalar=-1.0,
                                         in1=k_hi[:, h, :], op0=ALU.mult, op1=ALU.subtract)\
                   .then_inc(k_lo_ready, 1)

            for h in range(H // 2):
                k_low(h)
                if h == 0:
                    dve.wait_ge(x_in, 16)
                for t in (2 * h, 2 * h + 1):
                    dve.bn_stats(halves[:, t, :], xs[:, t, :]).then_inc(ln_stat, 1)
            dve.wait_ge(ln_stat, NT)
            for t in range(NT):
                dve.bn_aggr(mean_var[:, t, :], halves[:, t, :]).then_inc(ln_stat, 1)
            dve.wait_ge(ln_stat, 2 * NT)
            dve.tensor_copy(stat[:, 0, :], mean_var[:, :, 0]).then_inc(ln, 1)
            dve.tensor_scalar(stat[:, 1, :], mean_var[:, :, 1], EPS, None, ALU.add).then_inc(ln, 1)
            dve.wait_ge(std_ready, 1)
            dve.reciprocal(stat[:, 3, :], stat[:, 2, :]).then_inc(ln, 1)
            dve.wait_ge(ln, 3)
            for h in range(H // 2, H):
                for t in (2 * h - NT, 2 * h - NT + 1):
                    dve.tensor_scalar(xn[:, t, :], xs[:, t, :], stat[:, 0, t:t + 1], stat[:, 3, t:t + 1],
                                      ALU.subtract, ALU.mult).then_inc(xn_ready, 1)
                k_low(h)
            for c in range(1, 8, 2):
                dve.wait_ge(xnT_ps, c + 1)
                k, t0 = c % 2, 4 * (c // 2)
                dve.tensor_copy(xnT[:, k, t0 * P:(t0 + 4) * P], ps_t[1][:, :]).then_inc(xnT_dve, 1)
                for half in range(2):
                    dve.wait_ge(v_hi_ready, c + half)
                    v = v_parts[:, c // 2, 8 * half:8 * half + 8, :, :]
                    dve.tensor_tensor(v[:, :, 1, :], ps_s[half][0:STRIP, :].rearrange("p (h d) -> p h d", h=8),
                                      v[:, :, 0, :], ALU.subtract).then_inc(v_lo_ready, 1)
                mask_words(c - 1)
                mask_words(c)
            dve.wait_ge(mask_seen, 2 * NM)
            dve.tensor_reduce(rowflag[:, 0:1], word_max[:, 0, 0:NM], AX.X, ALU.max).then_inc(flag_step, 1)
            dve.tensor_reduce(rowflag[:, 1:2], word_max[:, 1, :], AX.X, ALU.min).then_inc(flag_step, 1)
            dve.wait_ge(flag_step, 2)
            dve.tensor_scalar(rowflag[:, 2:3], rowflag[:, 0:1], 0.0, None, ALU.is_equal).then_inc(flag_step, 1)
            dve.tensor_scalar(rowflag[:, 3:4], rowflag[:, 1:2], 0.0, None, ALU.is_gt).then_inc(flag_step, 1)
            dve.wait_ge(flag_step, 4)
            dve.tensor_tensor(rowflag[:, 0:1], rowflag[:, 2:3], rowflag[:, 3:4], ALU.mult).then_inc(flag_step, 1)
            for b in range(4):
                for odd in range(2):
                    q_low_parts(b, b, odd, [ps_a, ps_b][b % 2])
            dve.wait_ge(flag_sum, 1)
            dve.tensor_scalar(plainflag[:, :], ps_o[0][0:1, 0:1], float(P), None, ALU.is_equal)\
               .then_inc(flag_ready, 1)

            def fast_attention():
                def mask_and_max(i, k):
                    n = UNITS * i + k
                    if k % H == 0:
                        dve.wait_ge(bias_in[k % UNITS // H], 16 * (i + k // UNITS) + 16)
                    dve.wait_ge(scores_ready, n + 1)
                    if not first(n, 2):
                        dve.wait_ge(probs_ready, n - 1)
                    if not isinstance(n, int):
                        dve.sem_inc(carried, 1)
                    dve.tensor_tensor_reduce(masked[:, k % 2, :], ps_s[k % 2][:, 0:LASTK],
                                             bias_cur[:, k % UNITS // H, k % 2, :], HD ** -0.5, 3e38, ALU.add, ALU.min,
                                             neg_max[:, k % 2:k % 2 + 1]).then_inc(masked_ready, 1)

                def inverses(i, g):
                    dve.wait_ge(probs_ready, UNITS * i + 8 * g + 8)
                    if not first(4 * i + g, 1):
                        dve.wait_ge(invT_ps, 4 * i + g)
                    dve.reciprocal(inv_sum[:, :, :], sum_exp[:, g % 2, :, :]).then_inc(inv_ready, 1)

                def low_inverses(i, g):
                    dve.wait_ge(invT_hi, 4 * i + g + 1)
                    dve.tensor_tensor(invT[LOW0:LOW0 + 4, :], ps_b[0:4, 0:PAIR], invT[0:4, :], ALU.subtract)\
                       .then_inc(invT_lo, 1)

                def normalise(i, g):
                    dve.wait_ge(inv_spread, 4 * i + g + 1)
                    dve.wait_ge(oT_ready, H * i + 4 * g + 4)
                    four = oT[:, g % 2 * 2:g % 2 * 2 + 2, :]
                    dve.tensor_tensor(four, ps_b[:, :].rearrange("p (c n) -> p c n", c=2), four, ALU.mult)\
                       .then_inc(normed, 1)

                def low_probs(i, k):
                    dve.wait_ge(probsT_hi, UNITS * i + k + 1)
                    unit = probsT[:, k // 2 % 2, :, :, k % 2 * P:(k % 2 + 1) * P]
                    dve.tensor_tensor(unit[:, :, 1, :], ps_t[k % 2][0:STRIP, :].rearrange("p (s n) -> p s n", s=NS),
                                      unit[:, :, 0, :], ALU.subtract).then_inc(probsT_lo, 1)

                def output(i, h):
                    dve.wait_ge(o_low, H * i + h + 1)
                    p0 = h % 2 * HD
                    dst = oT[p0:p0 + HD, h // 2 % 4, :]
                    dve.tensor_tensor(dst, ps_o[h % 2][0:HD, 0:PAIR], dst, ALU.add).then_inc(oT_ready, 1)

                def residual(i, g):
                    dve.wait_ge(wo_ps, 4 * i + g + 1)
                    two = xs[:, bass.ds(2 * i, 2), :]
                    dve.scalar_tensor_tensor(out=two, in0=ps_b[:, :].rearrange("p (t d) -> p t d", t=2),
                                             scalar=tanh_g[:, 0:1], in1=two, op0=ALU.mult, op1=ALU.add)\
                       .then_inc(x2_ready, 1)

                def step(i, j, last=False):
                    if not (last and j + 6 >= UNITS):
                        mask_and_max(i, j + 6)
                    if j >= 0 and j % 8 == 3:
                        inverses(i, j // 8)
                    if j + 4 >= 0 and not (last and j + 4 >= UNITS):
                        low_probs(i, j + 4)
                    if j >= 0 and j % 2 == 1:
                        output(i, j // 2)
                    if j >= 0 and j % 8 == 5:
                        low_inverses(i, j // 8)
                    if j >= 0 and j % 8 == 7:
                        normalise(i, j // 8)
                    if j >= 0 and j % 8 == 6 and not last:
                        q_low_parts(j // 8, 4 * i + 4 + j // 8, 0)
                    if j >= 8 and j % 8 == 0 and not last:
                        q_low_parts(j // 8 - 1, 4 * i + 3 + j // 8, 1)
                    if j == 0 and not first(i, 1):
                        q_low_parts(3, 4 * i + 3, 1)
                    if j >= 10 and j % 8 == 2:
                        residual(i, j // 8 - 1)
                    if j == 2 and not first(i, 1):
                        residual(i - 1, 3)

                dve.wait_ge(tanh_ready, 1)
                for j in range(-6, UNITS):
                    step(0, j)
                with dve.Fori(1, NI - 1) as i:
                    for j in range(UNITS):
                        step(i, j)
                for j in range(UNITS):
                    step(NI - 1, j, last=True)
                residual(NI - 1, 3)
                dve.wait_ge(x2_ready, 4 * NI)
                dve.nop().then_inc(attention_done, 1)

            with dve.If(last_block_only(dve)):
                fast_attention()
            def full_attention():
                settled(dve)
                for free in (g_klo_ready, g_masked_ready, g_o_ready, g_x2_ready, g_bias_ready):
                    dve.sem_inc(free, 1)
                dve.wait_ge(g_w_in, 48)
                with dve.Fori(0, NT) as i:
                    dve.wait_ge(g_mask_in, 16 * i + 16)
                    dve.tensor_scalar(g_bias[:, :], g_mask8[:, :], -MASKED, MASKED, ALU.mult, ALU.add)\
                       .then_inc(g_bias_ready, 1)
                    for half in range(2):
                        dve.wait_ge(q_hi, 4 * i + 2 * half + 10)
                        src = ps_a[:, :].rearrange("p (c n) -> p c n", c=4)
                        even = q_parts[:, 8 * half:8 * half + 8:2, 0:P]
                        odd = q_parts[:, 8 * half + 1:8 * half + 8:2, 0:P]
                        dve.tensor_tensor(even[HD:P], src[0:HD], even[0:HD], ALU.subtract)
                        dve.tensor_tensor(odd[0:HD], src[HD:P], odd[HD:P], ALU.subtract).then_inc(q_split, 1)
                    dve.wait_ge(q_split, 2 * i + 10)
                    dve.wait_ge(g_bias_ready, i + 2)
                    dve.sem_inc(carried, 1)
                    with dve.Fori(0, H) as h:
                        n = H * i + h
                        dve.wait_ge(g_pv_block, NB * n + 1)
                        dve.tensor_copy(g_q[:, :], q_parts[:, bass.ds(h, 1), 0:P].squeeze(1)).then_inc(g_staged, 1)
                        for copy in range(2):
                            dve.tensor_copy(g_wk2[:, :, copy, :], g_wk[:, :, bass.ds(h * HD, HD)]).then_inc(g_staged, 1)
                        for b in range(NB):
                            k0, keys, even, _ = block_of(b)
                            dve.wait_ge(g_khi_ready, NB * n + b + 1)
                            dve.scalar_tensor_tensor(out=g_klo[:, 0:even], in0=ps_a[:, 0:even], scalar=-1.0,
                                                     in1=g_khi[:, 0:even], op0=ALU.mult, op1=ALU.subtract)\
                               .then_inc(g_klo_ready, 1)
                            dve.wait_ge(g_scores_ready, NB * n + b + 1)
                            dve.sem_inc(carried, 1)
                            dve.tensor_tensor_reduce(g_probs[:, k0:k0 + keys], ps_s[0][:, 0:keys],
                                                     g_bias[:, k0:k0 + keys], HD ** -0.5, 3e38, ALU.add, ALU.min,
                                                     g_min[:, b:b + 1]).then_inc(g_masked_ready, 1)
                        dve.wait_ge(g_masked_ready, NB * n + NB + 1)
                        dve.tensor_reduce(g_min[:, 4:5], g_min[:, 0:NB], AX.X, ALU.min).then_inc(g_min_ready, 1)
                        dve.wait_ge(g_pv_block, NB * n + NB + 1)
                        dve.reciprocal(g_min[:, 5:6], ps_o[0][:, HD:VW]).then_inc(g_inv_ready, 1)
                        dve.wait_ge(g_inv_ready, n + 1)
                        dve.tensor_scalar(o_rows[:, bass.ds(h * HD, HD)], ps_o[0][:, 0:HD], g_min[:, 5:6], None,
                                          ALU.mult).then_inc(g_o_ready, 1)
                    dve.wait_ge(g_wo_ps, i + 1)
                    dve.scalar_tensor_tensor(out=xs[:, i, :], in0=ps_b[:, 0:D], scalar=tanh_g[:, 0:1],
                                             in1=xs[:, i, :], op0=ALU.mult, op1=ALU.add).then_inc(g_x2_ready, 1)
                dve.wait_ge(g_x2_ready, NT + 1)
                dve.nop().then_inc(attention_done, 1)

            with dve.Else():
                full_attention()

            dve.wait_ge(attention_done, ENGINES)
            dve.tensor_reduce(stat[:, 0, :], xs[:, :, :], AX.X, ALU.add).then_inc(ln2, 1)
            dve.wait_ge(ln2, 1)
            dve.tensor_scalar(stat[:, 0, :], stat[:, 0, :], 1.0 / D, None, ALU.mult).then_inc(ln2, 1)
            dve.wait_ge(ln2, 2)
            dve.tensor_tensor(xn2[:, 0, :, 0:D], xs[:, :, :], rows(0), ALU.subtract).then_inc(ln2, 1)
            dve.wait_ge(sq2_ready, 1)
            dve.tensor_reduce(stat[:, 1, :], sq2[:, :, :], AX.X, ALU.add).then_inc(ln2, 1)
            dve.wait_ge(ln2, 4)
            dve.tensor_scalar(stat[:, 1, :], stat[:, 1, :], 1.0 / D, EPS, ALU.mult, ALU.add).then_inc(ln2, 1)
            dve.wait_ge(std2_ready, 1)
            dve.reciprocal(stat[:, 3, :], stat[:, 2, :]).then_inc(ln2, 1)
            dve.wait_ge(ln2, 6)
            dve.tensor_tensor(xn2[:, 0, :, 0:D], xn2[:, 0, :, 0:D], rows(3), ALU.mult).then_inc(xn2_ready, 1)
            for c in range(1, 8, 2):
                dve.wait_ge(xn2T_ps, c + 1)
                k, t0 = c // 4, 4 * (c % 4)
                dve.tensor_copy(xnT[:, k, t0 * P:(t0 + 4) * P], ps_s[1][:, :]).then_inc(xn2T_dve, 1)

            routed = [0]

            def step(ins):
                routed[0] += 1
                ins.then_inc(route, 1)
                dve.wait_ge(route, routed[0])

            def per_expert(v):
                return v.unsqueeze(2).to_broadcast([P, NT, NE])

            def per_tile(v):
                return v.unsqueeze(1).to_broadcast([P, NT, NE])

            dve.wait_ge(logits_ps, 1)
            step(dve.tensor_copy(logits[:, :, :], ps_o[1][:, 0:NT * NE].rearrange("p (t e) -> p t e", e=NE)))
            for c in range(2):
                step(dve.tensor_reduce(top[:, c, :], logits[:, :, :], AX.X, ALU.max))
                step(dve.tensor_tensor(work[:, :, :], logits[:, :, :], per_expert(top[:, c, :]), ALU.is_equal))
                step(dve.tensor_tensor(work[:, :, :], work[:, :, :], per_tile(rank[:, :]), ALU.mult))
                step(dve.tensor_reduce(pick[:, :], work[:, :, :], AX.X, ALU.max))
                step(dve.tensor_tensor(chosen[:, c, :, :], per_tile(rank[:, :]), per_expert(pick[:, :]), ALU.is_equal))
                if c == 0:
                    step(dve.scalar_tensor_tensor(out=logits[:, :, :], in0=chosen[:, 0, :, :], scalar=-3e38,
                                                  in1=logits[:, :, :], op0=ALU.mult, op1=ALU.add))
            dve.tensor_tensor(both[:, :, :], chosen[:, 0, :, :], chosen[:, 1, :, :], ALU.add).then_inc(both_ready, 1)
            dve.tensor_tensor(pick[:, :], top[:, 1, :], top[:, 0, :], ALU.subtract).then_inc(diff_ready, 1)
            dve.wait_ge(exp_gap_ready, 1)
            step(dve.tensor_scalar(denom[:, 1, :], denom[:, 0, :], 1.0, None, ALU.add))
            step(dve.reciprocal(denom[:, 1, :], denom[:, 1, :]))
            step(dve.tensor_scalar(weight[:, 0, :], denom[:, 1, :], tanh_g[:, 1:2], None, ALU.mult))
            step(dve.tensor_tensor(weight[:, 1, :], weight[:, 0, :], denom[:, 0, :], ALU.mult))
            for c in range(2):
                dve.tensor_copy(xn2[:, c, :, W_COL:W_COL + 1], weight[:, c, :].unsqueeze(2)).then_inc(weights_set, 1)

            dve.wait_ge(prefix_ps, 1)
            step(dve.tensor_copy(sums[:, 0, :, :], ps_b[:, 0:NT * NE].rearrange("p (t e) -> p t e", e=NE)))
            src = 0
            for shift in (1, 2, 4, 8):
                a, b = sums[:, src, :, :], sums[:, 1 - src, :, :]
                step(dve.tensor_copy(b[:, 0:shift, :], a[:, 0:shift, :]))
                step(dve.tensor_tensor(b[:, shift:, :], a[:, shift:, :], a[:, 0:NT - shift, :], ALU.add))
                src = 1 - src
            upto = sums[:, src, :, :]
            in_tile = ps_a[:, 0:NT * NE].rearrange("p (t e) -> p t e", e=NE)
            step(dve.tensor_scalar(tiles[:, 3, :], number[:, :], float(REGION), None, ALU.mult))
            step(dve.tensor_tensor(place_f[:, :, :], in_tile, per_tile(tiles[:, 3, :]), ALU.add))
            step(dve.tensor_tensor(place_f[:, 1:, :], place_f[:, 1:, :], upto[:, 0:NT - 1, :], ALU.add))
            for c in range(2):
                step(dve.tensor_tensor(work[:, :, :], place_f[:, :, :], chosen[:, c, :, :], ALU.mult))
                step(dve.tensor_reduce(top[:, c, :], work[:, :, :], AX.X, ALU.add))
            dve.tensor_copy(place[:, :, :], top[:, :, :]).then_inc(places_ready, 1)
            total = upto[:, NT - 1, :]
            step(dve.tensor_tensor(has_tile[:, :, :], total.unsqueeze(2).to_broadcast([P, NE, NT]),
                                   fill[:, :].unsqueeze(1).to_broadcast([P, NE, NT]), ALU.is_gt))
            step(dve.tensor_reduce(tiles[:, 0, :], has_tile[:, :, :], AX.X, ALU.add))
            src = 0
            for shift in (1, 2, 4):
                a, b = tiles[:, src, :], tiles[:, src + 1, :] if src < 2 else tiles[:, 0, :]
                step(dve.tensor_copy(b[:, 0:shift], a[:, 0:shift]))
                step(dve.tensor_tensor(b[:, shift:], a[:, shift:], a[:, 0:NE - shift], ALU.add))
                src = (src + 1) % 3
            ends = tiles[0:1, src, :]
            def spread(v):
                return v.unsqueeze(1).to_broadcast([1, NSCHED, NE])

            turns = turn[0:1, :].unsqueeze(2).to_broadcast([1, NSCHED, NE])
            past_end, past_start, mine, val = (sched_f[:, n, :, :] for n in range(4))
            step(dve.tensor_tensor(past_end, turns, spread(ends), ALU.is_ge))
            step(dve.memset(past_start[:, :, 0:1], 1.0))
            step(dve.tensor_copy(past_start[:, :, 1:], past_end[:, :, 0:NE - 1]))
            step(dve.tensor_tensor(mine, past_start, past_end, ALU.subtract))
            step(dve.tensor_scalar(pad_row_f[:, 1:], ends[:, 0:NE - 1], -float(P), None, ALU.mult))
            step(dve.memset(pad_row_f[:, 0:1], 0.0))
            step(dve.tensor_tensor(pad_row_f[:, :], pad_row_f[:, :], tiles[0:1, 3, :], ALU.add))
            step(dve.scalar_tensor_tensor(out=val, in0=turns, scalar=float(P), in1=spread(pad_row_f[:, :]),
                                          op0=ALU.mult, op1=ALU.add))
            step(dve.tensor_tensor(val, val, mine, ALU.mult))
            step(dve.tensor_reduce(sched_s[:, 0, :], val, AX.X, ALU.add))
            step(dve.scalar_tensor_tensor(out=sched_s[:, 0, :].unsqueeze(2), in0=past_end[:, :, NE - 1:], scalar=float(NOWHERE),
                                          in1=sched_s[:, 0, :].unsqueeze(2), op0=ALU.mult, op1=ALU.add))
            step(dve.tensor_tensor(val, mine, spread(number[0:1, :]), ALU.mult))
            step(dve.tensor_reduce(sched_s[:, 1, :], val, AX.X, ALU.add))
            step(dve.tensor_copy(sched[:, :, :], sched_s[:, :, :]))
            step(dve.tensor_tensor(pad_row_f[:, :], tiles[0:1, 3, :], total[0:1, :], ALU.add))
            dve.tensor_copy(pad_row[:, :], pad_row_f[:, :]).then_inc(sched_ready, 1)

            def gate(s):
                dve.wait_ge(silu_ready, s + 1)
                dve.wait_ge(h2_ps, s + 1)
                if not (isinstance(s, int) and s == 0):
                    dve.wait_ge(gatedT_ps, s)
                dve.tensor_tensor(gated[:, :], ps_s[1][:, :], silu[:, :], ALU.mult).then_inc(gated_ready, 1)

            def weigh(i, k):
                s = RING * i + k
                dve.wait_ge(xg_in[k % RING], 16 * (i + k // RING + 1))
                if not first(s, RING):
                    dve.wait_ge(added, 16 * (s - RING + 1))
                dve.tensor_copy(ids[:, k % RING:k % RING + 1], xg[:, k % RING, ID_COL:]).then_inc(ids_ready, 1)
                dve.wait_ge(y_ps, s + 2)
                if not first(s, 2):
                    dve.wait_ge(added, 16 * (s - 1))
                dve.tensor_scalar(yg[:, k % 2, :], ps_o[0][:, 0:D], xg[:, k % RING, W_COL:W_COL + 1], None, ALU.mult)\
                   .then_inc(y_ready, 1)

            def ffn_tile(i, k):
                s = RING * i + k
                if not (isinstance(s, int) and s + 1 >= NG):
                    gate(s + 1)
                weigh(i, k)

            dve.sem_inc(y_ready, 1)
            gate(0)
            for k in range(RING):
                ffn_tile(0, k)
            with dve.Fori(1, NG // RING) as i:
                for k in range(RING):
                    ffn_tile(i, k)
            for k in range(NG % RING):
                ffn_tile(NG // RING, k)

        @block.tensor
        def _(pe):
            pe.wait_ge(const_ready, CONSTS)
            pe.wait_ge(pads_ready, PADS)
            pe.wait_ge(wk2_act, 2)
            pe.wait_ge(wk2_dve, 2)
            for h in range(H):
                if h >= 2:
                    pe.wait_ge(k_lo_ready, h - 1)
                for k in range(KT):
                    mm = pe.matmul([ps_a, ps_b][h % 2][:, 0:EVEN],
                                   wk2_sb[:, k, h, :, :].rearrange("p c d -> p (c d)"),
                                   ctx_last[:, k, 0:EVEN], start=(k == 0), stop=(k == KT - 1))
                mm.then_inc(k_ps, 1)
            for c in range(8):
                s, half, k, t0 = c // 2, c % 2, c % 2, 4 * (c // 2)
                pe.wait_ge(xn_ready, t0 + 4)
                if c >= 2:
                    pe.wait_ge([xnT_act, xnT_dve][c % 2], c // 2)
                    pe.wait_ge(v_lo_ready, c - 1)
                if c == 0:
                    pe.wait_ge(wv_in, 16)
                for t in range(4):
                    last = pe.transpose(ps_t[c % 2][:, t * P:(t + 1) * P], xn[:, t0 + t, k * P:(k + 1) * P],
                                        ident[:, :])
                last.then_inc(xnT_ps, 1)
                for k in range(KT):
                    mm = pe.matmul(ps_s[c % 2][0:STRIP, :], ctx_last[:, k, s * STRIP:(s + 1) * STRIP],
                                   wv_sb[:, k, half * 512:(half + 1) * 512], start=(k == 0), stop=(k == KT - 1))
                mm.then_inc(v_ps, 1)
            def project_q(pair, k, i, bank=ps_a):
                return pe.matmul(bank[:, pair % 2 * PAIR:(pair % 2 + 1) * PAIR], wq_sb[:, k, pair * P:(pair + 1) * P],
                                 xnT[:, k, bass.ts(i, PAIR)], start=(k == 0), stop=(k == KT - 1))

            pe.wait_ge(w_in, W_ALL)
            pe.wait_ge(k_lo_ready, H)
            pe.wait_ge(xnT_act, 4)
            pe.wait_ge(xnT_dve, 4)
            for b in range(4):
                if b >= 2:
                    pe.wait_ge(q_split, 2 * b - 2)
                for pair in (2 * b, 2 * b + 1):
                    for k in range(KT):
                        mm = project_q(pair, k, 0, [ps_a, ps_b][b % 2])
                mm.then_inc(q_ps, 1)
            pe.wait_ge(flag_step, 5)
            pe.matmul(ps_o[0][0:1, 0:1], ones[:, 0:1], rowflag[:, 0:1], start=True, stop=True).then_inc(flag_sum, 1)

            def fast_attention():
                pe.wait_ge(v_lo_ready, 2 * NS)
                pe.wait_ge(pads_set, 1)
                pe.wait_ge(head_of_set, 5)

                def scores(i, k):
                    n, h, t = UNITS * i + k, k // 2 % H, k % 2
                    if k % 8 == 0:
                        pe.wait_ge(q_split, 2 * (4 * i + k // 8 + 1))
                    if not first(n, 2):
                        pe.wait_ge(masked_ready, n - 1)
                    q = q_parts[:, h, t * P:(t + 1) * P]
                    pe.matmul(ps_s[t][:, 0:EVEN], q, k_hi[:, h, :], start=True, stop=False)
                    pe.matmul(ps_s[t][:, 0:EVEN], q, k_lo[:, h, :], start=False, stop=True).then_inc(scores_ready, 1)

                def transposes(i, k):
                    n, t = UNITS * i + k, k % 2
                    pe.wait_ge(probs_ready, n + 1)
                    if not first(n, 2):
                        pe.wait_ge(probsT_lo, n - 1)
                    for s in range(NS):
                        mm = pe.transpose(ps_t[t][0:STRIP, s * P:(s + 1) * P],
                                          probs[:, t, s * STRIP:(s + 1) * STRIP], ident[:, :])
                    mm.then_inc(probsT_ps, 1)

                def probs_v(i, h, part):
                    if part == 0:
                        pe.wait_ge(probsT_lo, UNITS * i + 2 * h + 2)
                        if not first(H * i + h, 2):
                            pe.wait_ge(oT_ready, H * i + h - 1)
                    for s in range(part * NS // 2, (part + 1) * NS // 2):
                        for c in range(2):
                            mm = pe.matmul(ps_o[h % 2][:, 0:PAIR],
                                           v_parts[:, s, h % H, :, :].rearrange("p c d -> p (c d)"),
                                           probsT[:, h % 2, s, c, :], start=(s == 0 and c == 0),
                                           stop=(s == NS - 1 and c == 1))
                    if part == 1:
                        mm.then_inc(pv_ready, 1)

                def transpose_inverses(i, g):
                    pe.wait_ge(inv_ready, 4 * i + g + 1)
                    if not first(4 * i + g, 1):
                        pe.wait_ge(x2_ready, 4 * i + g)
                    for t in range(2):
                        mm = pe.transpose(ps_b[0:4, t * P:(t + 1) * P], inv_sum[:, t, :], ident[:, :])
                    mm.then_inc(invT_ps, 1)

                def spread_inverses(i, g):
                    pe.wait_ge(invT_lo, 4 * i + g + 1)
                    for c in range(2):
                        mm = pe.matmul(ps_b[:, c * PAIR:(c + 1) * PAIR], head_of[:, c, :, :].rearrange("p h d -> p (h d)"),
                                       invT[:, :], start=True, stop=True)
                    mm.then_inc(inv_spread, 1)

                def out_projection(i, g):
                    pe.wait_ge(normed, 4 * i + g + 1)
                    for t in range(2):
                        for p in (2 * g, 2 * g + 1):
                            mm = pe.matmul(ps_b[:, t * D:(t + 1) * D], oT[:, p % 4, t * P:(t + 1) * P], wo_sb[:, p, :],
                                           start=(p == 2 * g), stop=(p == 2 * g + 1))
                    mm.then_inc(wo_ps, 1)

                def next_queries(i, j):
                    b, part = j // 8, j % 8 - 2
                    if part == 0:
                        pe.wait_ge(q_split, 2 * (4 * i + 4 + b))
                    if 0 <= part < 4:
                        mm = project_q(2 * b + part // 2, part % 2, i + 1)
                        if part == 3:
                            mm.then_inc(q_ps, 1)

                def step(i, j, last=False):
                    if not (last and j + 6 >= UNITS):
                        scores(i, j + 6)
                    if j + 4 >= 0 and not (last and j + 4 >= UNITS):
                        transposes(i, j + 4)
                    if j >= 0 and j % 2 == 0:
                        probs_v(i, j // 2, 1)
                    if j >= -1 and j % 2 == 1 and not (last and j == UNITS - 1):
                        probs_v(i, (j + 1) // 2, 0)
                    if j >= 0 and j % 8 == 4:
                        transpose_inverses(i, j // 8)
                    if j >= 0 and j % 8 == 6:
                        spread_inverses(i, j // 8)
                    if j >= 9 and j % 8 == 1:
                        out_projection(i, j // 8 - 1)
                    if j == 1 and not first(i, 1):
                        out_projection(i - 1, 3)
                    if j >= 0 and not last:
                        next_queries(i, j)

                for j in range(-6, UNITS):
                    step(0, j)
                with pe.Fori(1, NI - 1) as i:
                    for j in range(UNITS):
                        step(i, j)
                for j in range(UNITS):
                    step(NI - 1, j, last=True)
                out_projection(NI - 1, 3)
                pe.wait_ge(wo_ps, 4 * NI)
                pe.nop().then_inc(attention_done, 1)

            with pe.If(last_block_only(pe)):
                fast_attention()
            def full_attention():
                settled(pe)
                pe.wait_ge(g_pads, 3)
                pe.wait_ge(g_w_in, 48)
                pe.sem_inc(g_pv_block, 1)
                for c in range(2 * NB * NS):
                    half, s, (k0, _, _, w) = c % 2, c // 2 % NS, block_of(c // 2 // NS)
                    if c >= 2:
                        pe.wait_ge(g_v_ready, c - 1)
                    for k in range(KT):
                        mm = pe.matmul(ps_s[half][0:w, :], g_ctxT[:, k, k0 + s * w:k0 + (s + 1) * w],
                                       g_wv[:, k, half * 512:(half + 1) * 512], start=(k == 0), stop=(k == KT - 1))
                    mm.then_inc(g_v_ps, 1)
                pe.wait_ge(g_v_ready, 2 * NB * NS)
                with pe.Fori(0, NT) as i:
                    pe.wait_ge(g_x2_ready, i + 1)
                    for half in range(2):
                        pe.wait_ge(q_split, 2 * i + half + 8)
                        for pair in range(4):
                            for k in range(KT):
                                mm = pe.matmul(ps_a[:, pair * P:(pair + 1) * P],
                                               wq_sb[:, k, (4 * half + pair) * P:(4 * half + pair + 1) * P],
                                               xnT[:, k, bass.ts(i, P)], start=(k == 0), stop=(k == KT - 1))
                        mm.then_inc(q_ps, 1)
                    pe.wait_ge(q_split, 2 * i + 10)
                    pe.sem_inc(carried, 1)
                    with pe.Fori(0, H) as h:
                        n = H * i + h
                        pe.wait_ge(g_staged, 3 * n + 3)
                        for b in range(NB):
                            k0, keys, even, _ = block_of(b)
                            pe.wait_ge(g_klo_ready, NB * n + b + 1)
                            for k in range(KT):
                                mm = pe.matmul(ps_a[:, 0:even], g_wk2[:, k, :, :].rearrange("p c d -> p (c d)"),
                                               g_ctxT[:, k, k0:k0 + even], start=(k == 0), stop=(k == KT - 1))
                            mm.then_inc(g_k_ps, 1)
                            pe.wait_ge(g_klo_ready, NB * n + b + 2)
                            pe.wait_ge(g_masked_ready, NB * n + b + 1)
                            pe.matmul(ps_s[0][:, 0:even], g_q[:, :], g_khi[:, 0:even], start=True, stop=False)
                            pe.matmul(ps_s[0][:, 0:even], g_q[:, :], g_klo[:, 0:even], start=False, stop=True)\
                              .then_inc(g_scores_ready, 1)
                        pe.wait_ge(g_probs_ready, n + 1)
                        pe.wait_ge(g_o_ready, n + 1)
                        for b in range(NB):
                            k0, _, _, w = block_of(b)
                            pe.wait_ge(g_probsT_ready, NB * n + b + 1)
                            for s in range(NS):
                                mm = pe.transpose(ps_t[0][0:w, s * P:(s + 1) * P],
                                                  g_probs[:, k0 + s * w:k0 + (s + 1) * w], ident[:, :])
                            mm.then_inc(g_probsT_ps, 1)
                            pe.wait_ge(g_probsT_ready, NB * n + b + 2)
                            for s in range(NS):
                                mm = pe.matmul(ps_o[0][:, 0:VW], g_probsT[0:w, s * P:(s + 1) * P],
                                               g_v[0:w, b * NS + s, bass.ds(h, 1), :].squeeze(1),
                                               start=(b == 0 and s == 0), stop=(b == NB - 1 and s == NS - 1))
                            mm.then_inc(g_pv_block, 1)
                    pe.wait_ge(g_o_ready, H * i + H + 1)
                    for half in range(2):
                        for p in range(4):
                            mm = pe.transpose([ps_b, ps_a][half][:, p * P:(p + 1) * P],
                                              o_rows[:, (4 * half + p) * P:(4 * half + p + 1) * P], ident[:, :])
                        mm.then_inc(g_oT_ps, 1)
                    pe.wait_ge(g_oT_ready, 2 * i + 2)
                    for p in range(H // 2):
                        mm = pe.matmul(ps_b[:, 0:D], g_oT[:, p, :], wo_sb[:, p, :], start=(p == 0), stop=(p == H // 2 - 1))
                    mm.then_inc(g_wo_ps, 1)
                pe.wait_ge(g_wo_ps, NT)
                pe.nop().then_inc(attention_done, 1)

            with pe.Else():
                full_attention()

            pe.wait_ge(attention_done, ENGINES)
            pe.wait_ge(xn2_ready, 1)
            for c in range(8):
                k, t0 = c // 4, 4 * (c % 4)
                if c >= 2:
                    pe.wait_ge([xn2T_act, xn2T_dve][c % 2], c // 2)
                for t in range(4):
                    mm = pe.transpose(ps_s[c % 2][:, t * P:(t + 1) * P], xn2[:, 0, t0 + t, k * P:(k + 1) * P], ident[:, :])
                mm.then_inc(xn2T_ps, 1)
            pe.wait_ge(xn2T_act, 4)
            pe.wait_ge(xn2T_dve, 4)
            pe.wait_ge(wg_in, 16)
            for t in range(NT):
                for k in range(KT):
                    mm = pe.matmul(ps_o[1][:, t * NE:(t + 1) * NE], xnT[:, k, t * P:(t + 1) * P], wg_sb[:, k, :],
                                   start=(k == 0), stop=(k == KT - 1))
            mm.then_inc(logits_ps, 1)
            pe.wait_ge(both_ready, 1)
            flat = both[:, :, :].rearrange("p t e -> p (t e)")
            pe.matmul(ps_a[:, 0:NT * NE], before[:, :], flat, start=True, stop=True)
            pe.matmul(ps_b[:, 0:NT * NE], ones[:, :], flat, start=True, stop=True).then_inc(prefix_ps, 1)

            def transpose_x(i, k):
                s = RING * i + k
                pe.wait_ge(xg_in[k % RING], 16 * (i + k // RING + 1))
                if not (isinstance(s, int) and s == 0):
                    pe.wait_ge(xgT_ready, s)
                for c in range(KT):
                    mm = pe.transpose(ps_t[1][:, c * P:(c + 1) * P], xg[:, k % RING, c * P:(c + 1) * P], ident[:, :])
                mm.then_inc(xgT_ps, 1)

            def hidden(s, buf, expert, w, bank, done):
                for k in range(KT):
                    mm = pe.matmul(bank[:, :], xgT[:, buf, k, :], w[:, k, bass.ds(expert, 1), :].squeeze(1), start=(k == 0), stop=(k == KT - 1))
                mm.then_inc(done, 1)

            def first_hidden(s, buf, expert):
                pe.wait_ge(xgT_ready, s + 1)
                pe.wait_ge(experts_ready, expert + 1)
                if not (isinstance(s, int) and s == 0):
                    pe.wait_ge(silu_ready, s)
                hidden(s, buf, expert, w1_sb, ps_s[0], h1_ps)

            def second_hidden(s, buf, expert):
                if not (isinstance(s, int) and s == 0):
                    pe.wait_ge(gated_ready, s)
                hidden(s, buf, expert, w2_sb, ps_s[1], h2_ps)

            def transpose_gated(s):
                pe.wait_ge(gated_ready, s + 1)
                pe.wait_ge(gatedT_ready, s + 1)
                for k in range(HT):
                    mm = pe.transpose(ps_t[0][:, k * P:(k + 1) * P], gated[:, k * P:(k + 1) * P], ident[:, :])
                mm.then_inc(gatedT_ps, 1)

            def project_down(s, expert):
                pe.wait_ge(gatedT_ready, s + 2)
                pe.wait_ge(y_ready, s + 1)
                for k in range(HT):
                    mm = pe.matmul(ps_o[0][:, 0:D], gatedT[:, k, :], w3_sb[:, k, bass.ds(expert, 1), :].squeeze(1), start=(k == 0), stop=(k == HT - 1))
                mm.then_inc(y_ps, 1)

            pe.sem_inc(y_ps, 1)
            pe.wait_ge(sched_ready, 1)
            transpose_x(0, 0)
            expert = table(pe, 1, 0, NE - 1)
            first_hidden(0, 0, expert)
            second_hidden(0, 0, expert)
            transpose_x(0, 1)

            def ffn_tile(i, k):
                s = RING * i + k
                last = isinstance(s, int)
                if not (last and s + 1 >= NG):
                    ahead = table(pe, 1, s + 1, NE - 1)
                    first_hidden(s + 1, (k + 1) % 2, ahead)
                transpose_gated(s)
                if not (last and s + 1 >= NG):
                    second_hidden(s + 1, (k + 1) % 2, ahead)
                now = table(pe, 1, s, NE - 1)
                if not (last and s + 2 >= NG):
                    transpose_x(i, k + 2)
                project_down(s, now)

            with pe.Fori(0, NG // RING) as i:
                for k in range(RING):
                    ffn_tile(i, k)
            for k in range(NG % RING):
                ffn_tile(NG // RING, k)


_INS = ["x", "ctx_1024", "mask_1x1xSxS2_bk0", "g_xattn", "g_ffn", "L0_xattn_Wq", "L0_xattn_Wk", "L0_xattn_Wv",
        "L0_xattn_Wo", "L0_ffn_Wg", "L0_ffn_W1", "L0_ffn_W2", "L0_ffn_W3"]


def kernel(**inputs):
    import numpy as np
    import concourse.bacc as bacc
    from concourse.bass_utils import run_bass_kernel_spmd

    a = {name: np.asarray(inputs[name]) for name in _INS}
    laid_out = {
        "x": a["x"][0],
        "ctxT": a["ctx_1024"][0].T,
        "mask": a["mask_1x1xSxS2_bk0"][0, 0],
        "g_xattn": a["g_xattn"],
        "g_ffn": a["g_ffn"],
        "Wq": a["L0_xattn_Wq"],
        "Wk": a["L0_xattn_Wk"],
        "Wv": a["L0_xattn_Wv"],
        "Wo": a["L0_xattn_Wo"],
        "WgT": a["L0_ffn_Wg"].T,
        "W1T": a["L0_ffn_W1"].transpose(0, 2, 1),
        "W2T": a["L0_ffn_W2"].transpose(0, 2, 1),
        "W3T": a["L0_ffn_W3"].transpose(0, 2, 1),
    }
    nc = bacc.Bacc("TRN2", target_bir_lowering=False, num_devices=1)
    arrays, args = {}, []
    for name, v in laid_out.items():
        v = np.ascontiguousarray(v)
        arrays[name + "_dram"] = v
        args.append(nc.dram_tensor(name + "_dram", v.shape, mybir.dt.from_np(v.dtype), kind="ExternalInput").ap())
    args.append(nc.dram_tensor("out_dram", (S + P, D), F32, kind="ExternalOutput").ap())
    build(nc, *args)
    r = run_bass_kernel_spmd(nc, [arrays], core_ids=[0])
    return r.results[0]["out_dram"][:S].reshape(1, S, D)
```

```python
from contextlib import ExitStack

import concourse.bass as bass
from concourse import mybir

F32 = mybir.dt.float32
F32R = mybir.dt.float32r
BF16 = mybir.dt.bfloat16
I32 = mybir.dt.int32
U8 = mybir.dt.uint8
ALU = mybir.AluOpType
ACT = mybir.ActivationFunctionType
AX = mybir.AxisListType

P = 128
S = 2048
SK = 1601
D = 256
H = 16
HD = 64
KT = D // P
NT = S // P
PAIR = 2 * P
NI = NT // 2
UNITS = 2 * H
LOW0 = 32
NB = 4
BK = 400
LASTK = SK - (NB - 1) * BK
LASTP = 404
NS = 4
STRIP = LASTP // NS
EVEN = LASTK + LASTK % 2
SKP = (NB - 1) * BK + LASTP
MT = 2
NM = NT // MT
LAST0 = (NB - 1) * BK
VW = HD + 1
MASKED = float(2.0 ** 125)
EPS = 1e-5
NE = 8
FH = 512
HT = FH // P
REGION = S + P
FULL = 2 * S // P
NG = FULL + NE - 1
NSCHED = NG
NOWHERE = NE * REGION
W_COL, ID_COL, XW = D, D + 1, D + 2
RSQRT_BITS = float(0x5f3759df)
EARLY = 5
RING = 4


def block_of(b):
    last = b == NB - 1
    return b * BK, LASTK if last else BK, EVEN if last else BK, STRIP if last else BK // NS


def build(nc, x, ctxT, mask, g_xattn, g_ffn, Wq, Wk, Wv, Wo, WgT, W1T, W2T, W3T, out):
    with ExitStack() as ctx:
        def sb(name, shape, dt, scope=ctx):
            return scope.enter_context(nc.sbuf_tensor(name, shape, dt))

        def psum(name):
            return ctx.enter_context(nc.psum_tensor(name, [P, 512], F32))

        def sem(name):
            return ctx.enter_context(nc.semaphore(name))

        xs = sb("xs", [P, NT, D], F32)
        xnT = sb("xnT", [P, KT, S], F32)
        ident = sb("ident", [P, P], F32)
        ones = sb("ones", [P, P], F32)
        before = sb("before", [P, P], F32)
        stat = sb("stat", [P, 4, NT], F32)
        gates = sb("gates", [P, 2], F32)
        tanh_g = sb("tanh_g", [P, 2], F32)
        halves = sb("halves", [P, NT, 6], F32)
        mean_var = sb("mean_var", [P, NT, 2], F32)
        word_max = sb("word_max", [P, 2, NT], F32)
        rowflag = sb("rowflag", [P, 4], F32)
        plainflag = sb("plainflag", [1, 1], I32)
        wg_sb = sb("wg_sb", [P, KT, NE], F32)
        rank = sb("rank", [P, NE], F32)
        number = sb("number", [P, NE], F32)
        row_no = sb("row_no", [P, NT + 1], F32)
        fill = sb("fill", [P, NT], F32)
        turn = sb("turn", [P, NSCHED], F32)
        pads = sb("pads", [P, XW], F32)
        var = sb("var", [P, 3, 2], F32)
        logits = sb("logits", [P, 2, NE], F32)
        work = sb("work", [P, 2, 2, NE], F32)
        won = sb("won", [P, 2, NE], F32)
        pick = sb("pick", [P, 2], F32)
        chosen = sb("chosen", [P, 2, 2, NE], F32)
        both = sb("both", [P, 2, NE], F32)
        top = sb("top", [P, 2, 2], F32)
        gap = sb("gap", [P, 3, 2], F32)
        counts = sb("counts", [P, 2, 2, NE], F32)
        taken = sb("taken", [P, NE], F32)
        place_f = sb("place_f", [P, 2, NE], F32)
        place = sb("place", [P, 2, 2], I32)
        with ExitStack() as attn:
            with ExitStack() as early:
                wk2_sb = sb("wk2_sb", [P, KT, H, 2, HD], F32, early)
            q_parts = sb("q_parts", [P, H, PAIR], F32R, attn)
            wq_sb = sb("wq_sb", [P, KT, H * HD], F32, attn)
            wo_sb = sb("wo_sb", [P, H // 2, D], F32, attn)
            with ExitStack() as fast:
                biases = sb("biases", [P, NT, LASTK], BF16, fast)
                k_hi = sb("k_hi", [P, H, EVEN], F32R, fast)
                k_lo = sb("k_lo", [P, H, EVEN], F32R, fast)
                v_parts = sb("v_parts", [STRIP, NS, H, 2, HD], F32R, fast)
                with ExitStack() as early:
                    ctx_last = sb("ctx_last", [P, KT, LASTP], F32, early)
                    wk_sb = sb("wk_sb", [P, KT, H * HD], F32, early)
                    wv_sb = sb("wv_sb", [P, KT, H * HD], F32, early)
                    mask8 = sb("mask8", [P, 2, MT, SKP], U8, early)
                    xn = sb("xn", [P, NT, D], F32, early)
                bias_cur = sb("bias_cur", [P, 2, 2, LASTK], BF16, fast)
                masked = sb("masked", [P, 2, LASTK], F32, fast)
                probs = sb("probs", [P, 2, LASTP], F32, fast)
                probsT = sb("probsT", [STRIP, 2, NS, 2, PAIR], F32R, fast)
                oT = sb("oT", [P, 4, PAIR], F32, fast)
                neg_max = sb("neg_max", [P, 2], F32, fast)
                sum_exp = sb("sum_exp", [P, 2, 2, 4], F32, fast)
                inv_sum = sb("inv_sum", [P, 2, 4], F32, fast)
                invT = sb("invT", [LOW0 + 4, PAIR], F32R, fast)
                rows = sb("rows", [P, 2, 2, XW], F32, fast)
                rowsT = sb("rowsT", [P, 2, KT, P], F32, fast)
                head_of_f = sb("head_of_f", [LOW0 + 4, 2, 2, HD], F32, fast)
                head_of = sb("head_of", [LOW0 + 4, 2, 2, HD], F32R, fast)
            with ExitStack() as slow:
                g_ctxT = sb("g_ctxT", [P, KT, SKP], F32, slow)
                g_v = sb("g_v", [STRIP, NB * NS, H, VW], F32, slow)
                g_wv = sb("g_wv", [P, KT, H * HD], F32, slow)
                o_rows = sb("o_rows", [P, H * HD], F32, slow)
                g_oT = sb("g_oT", [P, H // 2, P], F32, slow)
                g_wk = sb("g_wk", [P, KT, H * HD], F32, slow)
                g_wk2 = sb("g_wk2", [P, KT, 2, HD], F32, slow)
                g_q = sb("g_q", [P, P], F32R, slow)
                g_khi = sb("g_khi", [P, EVEN], F32R, slow)
                g_klo = sb("g_klo", [P, EVEN], F32R, slow)
                g_mask8 = sb("g_mask8", [P, SK], U8, slow)
                g_bias = sb("g_bias", [P, SK], BF16, slow)
                g_probs = sb("g_probs", [P, SKP], F32, slow)
                g_probsT = sb("g_probsT", [STRIP, NS * P], F32, slow)
                g_min = sb("g_min", [P, 8], F32, slow)
        with ExitStack() as ffn:
            w1_sb = sb("w1_sb", [P, KT, NE, FH], F32, ffn)
            w2_sb = sb("w2_sb", [P, KT, NE, FH], F32, ffn)
            w3_sb = sb("w3_sb", [P, HT, NE, D], F32, ffn)
            total = sb("total", [P, NE], F32, ffn)
            tiles = sb("tiles", [P, 4, NE], F32, ffn)
            has_tile = sb("has_tile", [P, NE, NT], F32, ffn)
            sched_f = sb("sched_f", [1, 2, NSCHED, NE], F32, ffn)
            leap = sb("leap", [1, NE], F32, ffn)
            sched_s = sb("sched_s", [1, 2, NSCHED], F32, ffn)
            n_tiles = sb("n_tiles", [1, 1], I32, ffn)
            sched = sb("sched", [1, 2, NSCHED], I32, ffn)
            pad_row = sb("pad_row", [1, NE], I32, ffn)
            xg = sb("xg", [P, RING, XW], F32, ffn)
            ids = sb("ids", [P, RING], I32, ffn)
            xgT = sb("xgT", [P, 2, KT, P], F32, ffn)
            silu = sb("silu", [P, FH], F32, ffn)
            gated = sb("gated", [P, FH], F32, ffn)
            gatedT = sb("gatedT", [P, HT, P], F32, ffn)
            yg = sb("yg", [P, 2, D], F32, ffn)

        ps_s = [psum("ps_s0"), psum("ps_s1")]
        ps_t = [psum("ps_t0"), psum("ps_t1")]
        ps_o = [psum("ps_o0"), psum("ps_o1")]
        ps_a = psum("ps_a")
        ps_b = psum("ps_b")

        x_in, w_in, g_in = sem("x_in"), sem("w_in"), sem("g_in")
        kv_in, wv_in, wk2_act, wk2_dve = sem("kv_in"), sem("wv_in"), sem("wk2_act"), sem("wk2_dve")
        mask_in = [sem("mask0_in"), sem("mask1_in")]
        mask_pad, mask_seen, biases_ready = sem("mask_pad"), sem("mask_seen"), sem("biases_ready")
        const_ready, pads_ready = sem("const_ready"), sem("pads_ready")
        ln_stat, ln = sem("ln_stat"), sem("ln")
        std_ready, xn_ready = sem("std_ready"), sem("xn_ready")
        tanh_ready = sem("tanh_ready")
        flag_step, flag_sum, flag_ready = sem("flag_step"), sem("flag_sum"), sem("flag_ready")
        xnT_ps, xnT_act, xnT_dve = sem("xnT_ps"), sem("xnT_act"), sem("xnT_dve")
        q_ps, q_hi, q_split = sem("q_ps"), sem("q_hi"), sem("q_split")
        k_ps, k_hi_ready, k_lo_ready = sem("k_ps"), sem("k_hi_ready"), sem("k_lo_ready")
        v_ps, v_hi_ready, v_lo_ready = sem("v_ps"), sem("v_hi_ready"), sem("v_lo_ready")
        pads_set, bias_in = sem("pads_set"), [sem("bias0_in"), sem("bias1_in")]
        scores_ready, masked_ready, probs_ready = sem("scores_ready"), sem("masked_ready"), sem("probs_ready")
        inv_ready, invT_ps, invT_hi, invT_lo = sem("inv_ready"), sem("invT_ps"), sem("invT_hi"), sem("invT_lo")
        inv_spread, normed, head_of_set = sem("inv_spread"), sem("normed"), sem("head_of_set")
        probsT_ps, probsT_hi, probsT_lo = sem("probsT_ps"), sem("probsT_hi"), sem("probsT_lo")
        pv_ready, o_low, oT_ready = sem("pv_ready"), sem("o_low"), sem("oT_ready")
        wo_ps, x2_ready = sem("wo_ps"), sem("x2_ready")
        attention_done = sem("attention_done")
        stored = sem("stored")
        carried = sem("carried")

        g_w_in, g_mask_in, g_bias_ready, g_pads = sem("g_w_in"), sem("g_mask_in"), sem("g_bias_ready"), sem("g_pads")
        g_v_ps, g_v_ready, g_staged = sem("g_v_ps"), sem("g_v_ready"), sem("g_staged")
        g_k_ps, g_khi_ready, g_klo_ready = sem("g_k_ps"), sem("g_khi_ready"), sem("g_klo_ready")
        g_scores_ready, g_masked_ready, g_min_ready = sem("g_scores_ready"), sem("g_masked_ready"), sem("g_min_ready")
        g_probs_ready, g_probsT_ps, g_probsT_ready = sem("g_probs_ready"), sem("g_probsT_ps"), sem("g_probsT_ready")
        g_pv_block, g_inv_ready, g_o_ready = sem("g_pv_block"), sem("g_inv_ready"), sem("g_o_ready")
        g_oT_ps, g_oT_ready, g_wo_ps, g_x2_ready = sem("g_oT_ps"), sem("g_oT_ready"), sem("g_wo_ps"), sem("g_x2_ready")

        pair_added, stats_taken = sem("pair_added"), sem("stats_taken")
        stats_ready, pool_step, rows_ready = sem("stats_ready"), sem("pool_step"), sem("rows_ready")
        rowsT_ps, rowsT_ready = sem("rowsT_ps"), sem("rowsT_ready")
        logits_ps, logits_ready = sem("logits_ps"), sem("logits_ready")
        gap_ready, exp_gap_ready, denom_ready, weigher_ready = (
            sem("gap_ready"), sem("exp_gap_ready"), sem("denom_ready"), sem("weigher_ready"))
        both_ready, counts_ps, counts_ready = sem("both_ready"), sem("counts_ps"), sem("counts_ready")
        chosen_step, routed, route = sem("chosen_step"), sem("routed"), sem("route")
        leap_ready = sem("leap_ready")
        sched_ready, pads_made, pad_rows_ready = sem("sched_ready"), sem("pads_made"), sem("pad_rows_ready")
        scattered, padded = sem("scattered"), sem("padded")
        expert_in = [sem(f"expert{e}_in") for e in range(NE)]
        experts_ready = sem("experts_ready")
        xg_in = [sem(f"xg{n}_in") for n in range(RING)]
        xgT_ps, xgT_ready = sem("xgT_ps"), sem("xgT_ready")
        h1_ps, h2_ps, silu_ready, gated_ready = sem("h1_ps"), sem("h2_ps"), sem("silu_ready"), sem("gated_ready")
        gatedT_ps, gatedT_ready = sem("gatedT_ps"), sem("gatedT_ready")
        y_ps, y_ready = sem("y_ps"), sem("y_ready")
        ids_ready, added = sem("ids_ready"), sem("added")
        wg_in = sem("wg_in")

        x_regrouped = nc.dram_tensor("x_regrouped", (NOWHERE + P, XW), F32, kind="Internal").ap()

        block = ctx.enter_context(nc.Block())

        def first(n, count):
            return isinstance(n, int) and n < count

        def write_pads(eng, e0, e1):
            eng.wait_ge(pads_made, 2)
            eng.wait_ge(pad_rows_ready, 1)
            for e in range(e0, e1):
                row = eng.value_load(pad_row[0:1, e:e + 1], min_val=0, max_val=(NE - 1) * REGION + S)
                eng.dma_start(x_regrouped[bass.ds(row, P), :], pads[:, :]).then_inc(padded, 16)

        def load_expert(eng, e):
            eng.dma_start(w1_sb[:, :, e, :], W1T[e].rearrange("(k p) n -> p k n", p=P)).then_inc(expert_in[e], 16)
            eng.dma_start(w2_sb[:, :, e, :], W2T[e].rearrange("(k p) n -> p k n", p=P)).then_inc(expert_in[e], 16)
            eng.dma_start(w3_sb[:, :, e, :], W3T[e].rearrange("(k p) n -> p k n", p=P)).then_inc(expert_in[e], 16)

        def tiles_there(eng):
            eng.wait_ge(sched_ready, 2)
            return eng.value_load(n_tiles[0:1, 0:1], min_val=FULL, max_val=NG)

        def table(eng, row, s, top_value):
            return eng.value_load(sched[0:1, row, bass.ds(s, 1)], min_val=0, max_val=top_value)


        def settled(eng):
            eng.wait_ge(w_in, W_ALL)
            eng.wait_ge(k_lo_ready, H)
            eng.wait_ge(v_lo_ready, 2 * NS)
            eng.wait_ge(biases_ready, NM)
            eng.wait_ge(pads_set, 1)

        def last_block_only(eng):
            eng.wait_ge(flag_ready, 1)
            return eng.value_load(plainflag[0:1, 0:1], min_val=0, max_val=1) == 1

        W_ALL = 16 * 2

        CTX_WK = 16 * 2
        PADS = 1
        ENGINES = 5
        CONSTS = 10

        @block.sync
        def _(sp):
            sp.dma_start(ctx_last[:, :, 0:LASTK], ctxT[:, LAST0:].rearrange("(k p) n -> p k n", p=P)).then_inc(kv_in, 16)
            sp.dma_start(wk_sb[:, :, :], Wk.rearrange("(k p) n -> p k n", p=P)).then_inc(kv_in, 16)
            sp.dma_start(xs[:, :, :], x.rearrange("(t p) d -> p t d", p=P)).then_inc(x_in, 16)
            sp.dma_start(wv_sb[:, :, :], Wv.rearrange("(k p) n -> p k n", p=P)).then_inc(wv_in, 16)
            sp.wait_ge(mask_pad, 1)
            for c in range(NM):
                if c >= 2:
                    sp.wait_ge(mask_seen, 2 * c - 2)
                    sp.wait_ge(biases_ready, c - 1)
                sp.dma_start(mask8[:, c % 2, :, 0:SK], mask[c * MT * P:(c + 1) * MT * P, :]
                             .rearrange("(t p) k -> p t k", p=P)).then_inc(mask_in[c % 2], 16)
                if c == 1:
                    sp.dma_start(wq_sb[:, :, :], Wq.rearrange("(k p) n -> p k n", p=P)).then_inc(w_in, 16)
                    sp.dma_start(wo_sb[:, :, :], Wo.rearrange("(k p) n -> p k n", p=P)).then_inc(w_in, 16)
                    sp.dma_start(wg_sb[:, :, :], WgT.rearrange("(k p) e -> p k e", p=P)).then_inc(wg_in, 16)
            with sp.If(last_block_only(sp)):
                sp.wait_ge(biases_ready, NM)
                for half in range(2):
                    sp.dma_start(bias_cur[:, half, :, :], biases[:, 0:2, :]).then_inc(bias_in[half], 16)
                with sp.Fori(1, NI) as i:
                    for half in range(2):
                        sp.wait_ge(masked_ready, UNITS * i - UNITS + H * (half + 1))
                        sp.dma_start(bias_cur[:, half, :, :], biases[:, bass.ds(2 * i, 2), :]).then_inc(bias_in[half], 16)
                sp.nop().then_inc(attention_done, 1)
            with sp.Else():
                settled(sp)
                sp.dma_start(g_wk[:, :, :], Wk.rearrange("(k p) n -> p k n", p=P)).then_inc(g_w_in, 16)
                sp.dma_start(g_wv[:, :, :], Wv.rearrange("(k p) n -> p k n", p=P)).then_inc(g_w_in, 16)
                sp.dma_start(g_ctxT[:, :, 0:SK], ctxT.rearrange("(k p) n -> p k n", p=P)).then_inc(g_w_in, 16)
                with sp.Fori(0, NT) as i:
                    sp.wait_ge(g_bias_ready, i + 1)
                    sp.dma_start(g_mask8[:, :], mask[bass.ts(i, P), :]).then_inc(g_mask_in, 16)
                sp.nop().then_inc(attention_done, 1)
            sp.wait_ge(attention_done, ENGINES)
            for e in range(EARLY):
                load_expert(sp, e)
            sp.wait_ge(pads_made, 2)
            sp.dma_start(x_regrouped[NOWHERE:, :], pads[:, :]).then_inc(padded, 16)
            write_pads(sp, 0, NE // 2)
            sp.wait_ge(padded, 16 * (NE + 1))
            sp.wait_ge(scattered, 16 * 2 * NT)
            sp.wait_ge(sched_ready, 2)

            def load_tile(i, k):
                s = RING * i + k
                if not first(s, RING):
                    sp.wait_ge(y_ready, s - RING + 2)
                row = table(sp, 0, s, NOWHERE)
                sp.dma_start(xg[:, k % RING, :], x_regrouped[bass.ds(row, P), :]).then_inc(xg_in[k % RING], 16)

            for k in range(RING):
                load_tile(0, k)
            for c in range(4):
                sp.dma_start(out[c * 4 * P:(c + 1) * 4 * P, :].rearrange("(t p) d -> p t d", p=P),
                             xs[:, 4 * c:4 * c + 4, :]).then_inc(stored, 16)
            sp.dma_start(out[S:, :], pads[:, 0:D]).then_inc(stored, 16)
            for e in range(EARLY, NE):
                load_expert(sp, e)
            with sp.Fori(1, FULL // RING) as i:
                for k in range(RING):
                    load_tile(i, k)
            there = tiles_there(sp)
            for s in range(FULL, NG):
                with sp.If(there > s - RING):
                    load_tile(s // RING, s % RING)
            sp.wait_ge(stored, 5 * 16)
            sp.wait_ge(added, 16 * FULL)
            for s in range(FULL, NG):
                with sp.If(there > s - RING):
                    sp.wait_ge(xg_in[s % RING], 16 * (s // RING + 1))
                with sp.If(there > s):
                    sp.wait_ge(added, 16 * (s + 1))

        @block.gpsimd
        def _(pool):
            pool.memset(mask8[:, :, :, SKP - 4:], 0).then_inc(mask_pad, 1)
            pool.memset(ctx_last[:, :, LASTK:], 0.0).then_inc(pads_ready, 1)
            pool.dma_start(gates[:, 0:1], g_xattn.partition_broadcast(P)).then_inc(g_in, 16)
            pool.dma_start(gates[:, 1:2], g_ffn.partition_broadcast(P)).then_inc(g_in, 16)
            pool.memset(ident[:, :], 0.0).then_inc(const_ready, 1)
            pool.wait_ge(const_ready, 1)
            pool.affine_select(out=ident[:, :], in_=ident[:, :], compare_op=ALU.not_equal, fill=1.0, base=0,
                               pattern=[[-1, P]], channel_multiplier=1).then_inc(const_ready, 1)
            pool.memset(ones[:, :], 1.0).then_inc(const_ready, 1)
            pool.memset(pads[:, :], 0.0).then_inc(pads_made, 1)
            pool.memset(before[:, :], 1.0).then_inc(const_ready, 1)
            pool.wait_ge(const_ready, 4)
            pool.affine_select(out=before[:, :], in_=before[:, :], compare_op=ALU.is_gt, fill=0.0, base=0,
                               pattern=[[1, P]], channel_multiplier=-1).then_inc(const_ready, 1)
            for tile, base, step, n in ((rank, NE, -1, NE), (number, 0, 1, NE), (fill, 0, P, NT), (turn, 0, 1, NSCHED)):
                pool.iota(tile[:, :], pattern=[[step, n]], base=base, channel_multiplier=0,
                          allow_small_or_imprecise_dtypes=True).then_inc(const_ready, 1)
            pool.iota(row_no[:, :], pattern=[[P, NT + 1]], base=0, channel_multiplier=1,
                      allow_small_or_imprecise_dtypes=True).then_inc(const_ready, 1)
            for c in range(NM):
                pool.wait_ge(mask_in[c % 2], 16 * (c // 2 + 1))
                pool.tensor_scalar(biases[:, c * MT:(c + 1) * MT, :], mask8[:, c % 2, :, LAST0:SK], -MASKED, MASKED,
                                   ALU.mult, ALU.add).then_inc(biases_ready, 1)
            pool.wait_ge(xnT_ps, 8)
            pool.wait_ge(biases_ready, NM)
            pool.memset(probs[:, :, LASTK:], 0.0).then_inc(pads_set, 1)
            with pool.If(last_block_only(pool)):
                pool.memset(invT[:, :].bitcast(F32), 0.0).then_inc(head_of_set, 1)
                pool.memset(head_of_f[:, :, :, :], 0.0).then_inc(head_of_set, 1)
                for part in range(2):
                    pool.wait_ge(head_of_set, part + 2)
                    pool.affine_select(out=head_of_f[:, :, :, :], in_=head_of_f[:, :, :, :], compare_op=ALU.not_equal,
                                       fill=1.0, base=-part * LOW0, pattern=[[-2, 2], [-1, 2], [0, HD]],
                                       channel_multiplier=1).then_inc(head_of_set, 1)
                pool.wait_ge(head_of_set, 4)
                pool.tensor_copy(head_of[:, :, :, :], head_of_f[:, :, :, :]).then_inc(head_of_set, 1)
                pool.wait_ge(head_of_set, 5)
                pool.nop().then_inc(attention_done, 1)
            with pool.Else():
                settled(pool)
                pool.memset(g_ctxT[:, :, SK:], 0.0).then_inc(g_pads, 1)
                pool.memset(g_v[:, :, :, HD:], 1.0).then_inc(g_pads, 1)
                pool.memset(g_probs[:, SK:], 0.0).then_inc(g_pads, 1)
                pool.wait_ge(g_pads, 3)
                pool.nop().then_inc(attention_done, 1)

            pool.wait_ge(pads_made, 1)
            pool.wait_ge(const_ready, CONSTS)
            pool.tensor_copy(pads[:, ID_COL:], row_no[:, NT:]).then_inc(pads_made, 1)
            pool.tensor_scalar(taken[:, :], number[:, :], float(REGION), None, ALU.mult).then_inc(pads_made, 1)
            pool.wait_ge(pads_made, 3)

            STEPS = 31
            with pool.Fori(0, NI) as i:
                taken_steps = [0]

                def step(ins):
                    taken_steps[0] += 1
                    ins.then_inc(pool_step, 1)
                    ready(pool_step, STEPS * i + taken_steps[0])

                def ready(semaphore, value):
                    pool.wait_ge(semaphore, value)
                    pool.sem_inc(carried, 1)

                def per_tile(v):
                    return v.unsqueeze(1).to_broadcast([P, 2, NE])

                ready(stats_ready, i + 1)
                half, inv, t = (var[:, n, :] for n in range(3))
                step(pool.tensor_scalar(t, mean_var[:, 0:2, 1], EPS, None, ALU.add))
                step(pool.tensor_scalar(half, t, -0.5, None, ALU.mult))
                step(pool.tensor_scalar(inv.bitcast(I32), t.bitcast(I32), -0.5, RSQRT_BITS, ALU.mult, ALU.add))
                for _ in range(3):
                    step(pool.tensor_tensor(t, inv, inv, ALU.mult))
                    step(pool.tensor_tensor(t, t, half, ALU.mult))
                    step(pool.tensor_scalar(t, t, 1.5, None, ALU.add))
                    step(pool.tensor_tensor(inv, t, inv, ALU.mult))
                step(pool.tensor_tensor(rows[:, 0, :, 0:D], xs[:, bass.ds(2 * i, 2), :],
                                        mean_var[:, 0:2, 0].unsqueeze(2).to_broadcast([P, 2, D]), ALU.subtract))
                pool.tensor_tensor(rows[:, 0, :, 0:D], rows[:, 0, :, 0:D], inv.unsqueeze(2).to_broadcast([P, 2, D]),
                                   ALU.mult).then_inc(rows_ready, 1)
                ready(rows_ready, i + 1)
                step(pool.tensor_copy(rows[:, 1, :, 0:D], rows[:, 0, :, 0:D]))
                for c in range(2):
                    step(pool.tensor_copy(rows[:, c, :, ID_COL:], row_no[:, bass.ds(2 * i, 2)].unsqueeze(2)))
                ready(weigher_ready, i + 1)
                step(pool.tensor_scalar(rows[:, 0, :, W_COL], gap[:, 2, :], tanh_g[:, 1:2], None, ALU.mult))
                step(pool.tensor_tensor(rows[:, 1, :, W_COL], rows[:, 0, :, W_COL], gap[:, 1, :], ALU.mult))
                ready(counts_ready, i + 1)
                step(pool.tensor_tensor(place_f[:, :, :], counts[:, 0, :, :], per_tile(taken[:, :]), ALU.add))
                step(pool.tensor_tensor(place_f[:, 1, :], place_f[:, 1, :], counts[:, 1, 0, :], ALU.add))
                for c in range(2):
                    step(pool.tensor_tensor(work[:, c, :, :], place_f[:, :, :], chosen[:, c, :, :], ALU.mult))
                for width in (4, 2, 1):
                    step(pool.tensor_tensor(work[..., 0:width], work[..., 0:width], work[..., width:2 * width], ALU.add))
                step(pool.tensor_copy(place[:, :, :], work[:, :, :, 0]))
                for t in range(2):
                    step(pool.tensor_tensor(taken[:, :], taken[:, :], counts[:, 1, t, :], ALU.add))
                assert taken_steps[0] == STEPS
                pool.sem_inc(routed, 1)
                for t in range(2):
                    for c in range(2):
                        pool.indirect_dma_start(out=x_regrouped,
                                                out_offset=bass.IndirectOffsetOnAxis(ap=place[:, c, t:t + 1], axis=0),
                                                in_=rows[:, c, t, :], in_offset=None).then_inc(scattered, 16)
                pool.wait_ge(scattered, 64 * i + 64)
            for e in range(NE):
                pool.wait_ge(expert_in[e], 48)
                pool.nop().then_inc(experts_ready, 1)
            pool.wait_ge(stored, 5 * 16)

            def add_tile(i, k):
                s = RING * i + k
                pool.wait_ge(y_ready, s + 2)
                pool.wait_ge(ids_ready, s + 1)
                if not first(s, 1):
                    pool.wait_ge(added, 16 * s)
                if not isinstance(s, int):
                    pool.sem_inc(carried, 1)
                pool.indirect_dma_start(out=out, out_offset=bass.IndirectOffsetOnAxis(ap=ids[:, k % RING:k % RING + 1], axis=0),
                                        in_=yg[:, k % 2, :], in_offset=None, compute_op=ALU.add).then_inc(added, 16)

            for k in range(RING):
                add_tile(0, k)
            with pool.Fori(1, FULL // RING) as i:
                for k in range(RING):
                    add_tile(i, k)
            there = tiles_there(pool)
            for s in range(FULL, NG):
                with pool.If(there > s):
                    add_tile(s // RING, s % RING)

        @block.scalar
        def _(act):
            act.wait_ge(kv_in, CTX_WK)
            for copy in range(2):
                act.copy(wk2_sb[:, 0, :, copy, :], wk_sb[:, 0, :].rearrange("p (h d) -> p h d", h=H)).then_inc(wk2_act, 1)
            for h in range(H):
                if h == H // 2:
                    act.wait_ge(ln, 2)
                    act.activation(stat[:, 2, :], stat[:, 1, :], ACT.Sqrt).then_inc(std_ready, 1)
                act.wait_ge(k_ps, h + 1)
                act.mul(k_hi[:, h, :], [ps_a, ps_b][h % 2][:, 0:EVEN], -1.0).then_inc(k_hi_ready, 1)
            for c in range(0, 8, 2):
                act.wait_ge(xnT_ps, c + 1)
                k, t0 = c % 2, 4 * (c // 2)
                act.copy(xnT[:, k, t0 * P:(t0 + 4) * P], ps_t[0][:, :]).then_inc(xnT_act, 1)
                for half in range(2):
                    act.wait_ge(v_ps, c + half + 1)
                    act.copy(v_parts[:, c // 2, 8 * half:8 * half + 8, 0, :],
                             ps_s[half][0:STRIP, :].rearrange("p (h d) -> p h d", h=8)).then_inc(v_hi_ready, 1)
            act.wait_ge(g_in, 32)
            act.activation(tanh_g[:, :], gates[:, :], ACT.Tanh).then_inc(tanh_ready, 1)

            def q_high_parts(b, batch, odd, bank=ps_a):
                act.wait_ge(q_ps, batch + 1)
                src = bank[:, :].rearrange("p (c n) -> p c n", c=2)
                p0 = odd * HD
                act.copy(q_parts[p0:p0 + HD, 4 * b + odd:4 * b + 4:2, :], src[p0:p0 + HD]).then_inc(q_hi, 1)

            def routing(i, j):
                if j == 11:
                    act.wait_ge(rowsT_ps, i + 1)
                    act.copy(rowsT[:, :, :, :], ps_b[:, :].rearrange("p (t k n) -> p t k n", t=2, k=KT)).then_inc(rowsT_ready, 1)
                if j == 19:
                    act.wait_ge(logits_ps, i + 1)
                    act.copy(logits[:, :, :], ps_b[:, 0:2 * NE].rearrange("p (t e) -> p t e", t=2)).then_inc(logits_ready, 1)
                if j == 26:
                    act.wait_ge(gap_ready, i + 1)
                    act.activation(gap[:, 1, :], gap[:, 0, :], ACT.Exp).then_inc(exp_gap_ready, 1)
                if j == 27:
                    act.wait_ge(counts_ps, i + 1)
                    act.copy(counts[:, :, :, :], ps_b[:, 0:4 * NE].rearrange("p (c t e) -> p c t e", c=2, t=2))\
                       .then_inc(counts_ready, 1)

            for b in range(4):
                for odd in range(2):
                    q_high_parts(b, b, odd, [ps_a, ps_b][b % 2])

            def fast_attention():
                def exps(i, k):
                    n = UNITS * i + k
                    act.wait_ge(masked_ready, n + 1)
                    if not first(n, 2):
                        act.wait_ge(probsT_ps, n - 1)
                    act.activation(probs[:, k % 2, 0:LASTK], masked[:, k % 2, :], ACT.Exp,
                                   bias=neg_max[:, k % 2:k % 2 + 1], scale=-1.0,
                                   accum_out=sum_exp[:, k // 8 % 2, k % 2, k // 2 % 4:k // 2 % 4 + 1]).then_inc(probs_ready, 1)

                def high_inverses(i, g):
                    act.wait_ge(invT_ps, 4 * i + g + 1)
                    act.copy(invT[0:4, :], ps_b[0:4, 0:PAIR]).then_inc(invT_hi, 1)

                def high_probs(i, k):
                    n, head = UNITS * i + k, H * i + k // 2
                    act.wait_ge(probsT_ps, n + 1)
                    if not first(head, 2):
                        act.wait_ge(pv_ready, head - 1)
                    act.copy(probsT[:, k // 2 % 2, :, 0, k % 2 * P:(k % 2 + 1) * P],
                             ps_t[k % 2][0:STRIP, :].rearrange("p (s n) -> p s n", s=NS)).then_inc(probsT_hi, 1)

                def output_of_low_v(i, h):
                    act.wait_ge(pv_ready, H * i + h + 1)
                    if not first(4 * i + h // 4, 2):
                        act.wait_ge(wo_ps, 4 * i + h // 4 - 1)
                    p0 = h % 2 * HD
                    act.copy(oT[p0:p0 + HD, h // 2 % 4, :], ps_o[h % 2][HD:P, 0:PAIR]).then_inc(o_low, 1)

                def step(i, j, last=False):
                    if not (last and j + 5 >= UNITS):
                        exps(i, j + 5)
                    if j + 4 >= 0 and not (last and j + 4 >= UNITS):
                        high_probs(i, j + 4)
                    if j >= 0 and j % 2 == 1:
                        output_of_low_v(i, j // 2)
                    if j >= 0 and j % 8 == 4:
                        high_inverses(i, j // 8)
                    if j >= 0 and j % 8 == 6 and not last:
                        q_high_parts(j // 8, 4 * i + 4 + j // 8, 0)
                    if j >= 8 and j % 8 == 0 and not last:
                        q_high_parts(j // 8 - 1, 4 * i + 3 + j // 8, 1)
                    if j >= 0 and not first(i, 1):
                        routing(i - 1, j)
                    if j == 0 and not first(i, 1):
                        q_high_parts(3, 4 * i + 3, 1)

                for j in range(-5, UNITS):
                    step(0, j)
                with act.Fori(1, NI - 1) as i:
                    for j in range(UNITS):
                        step(i, j)
                for j in range(UNITS):
                    step(NI - 1, j, last=True)
                act.wait_ge(probs_ready, UNITS * NI)
                act.wait_ge(o_low, H * NI)
                act.nop().then_inc(attention_done, 1)

            with act.If(last_block_only(act)):
                fast_attention()
            def full_attention():
                settled(act)
                act.sem_inc(g_probsT_ready, 1)
                for c in range(2 * NB * NS):
                    act.wait_ge(g_v_ps, c + 1)
                    half, w = c % 2, block_of(c // 2 // NS)[3]
                    act.copy(g_v[0:w, c // 2, 8 * half:8 * half + 8, 0:HD],
                             ps_s[half][0:w, :].rearrange("p (h d) -> p h d", h=8)).then_inc(g_v_ready, 1)
                with act.Fori(0, NT) as i:
                    for half in range(2):
                        act.wait_ge(q_ps, 2 * i + half + 5)
                        src = ps_a[:, :].rearrange("p (c n) -> p c n", c=4)
                        act.copy(q_parts[0:HD, 8 * half:8 * half + 8:2, 0:P], src[0:HD]).then_inc(q_hi, 1)
                        act.copy(q_parts[HD:P, 8 * half + 1:8 * half + 8:2, 0:P], src[HD:P]).then_inc(q_hi, 1)
                    with act.Fori(0, H) as h:
                        n = H * i + h
                        for b in range(NB):
                            act.wait_ge(g_k_ps, NB * n + b + 1)
                            act.mul(g_khi[:, 0:block_of(b)[2]], ps_a[:, 0:block_of(b)[2]], -1.0).then_inc(g_khi_ready, 1)
                        act.wait_ge(g_min_ready, n + 1)
                        act.activation(g_probs[:, 0:SK], g_probs[:, 0:SK], ACT.Exp, bias=g_min[:, 4:5], scale=-1.0)\
                           .then_inc(g_probs_ready, 1)
                        for b in range(NB):
                            w = block_of(b)[3]
                            act.wait_ge(g_probsT_ps, NB * n + b + 1)
                            act.copy(g_probsT[0:w, :], ps_t[0][0:w, :]).then_inc(g_probsT_ready, 1)
                    for half in range(2):
                        act.wait_ge(g_oT_ps, 2 * i + half + 1)
                        act.copy(g_oT[:, 4 * half:4 * half + 4, :],
                                 [ps_b, ps_a][half][:, :].rearrange("p (c n) -> p c n", c=4)).then_inc(g_oT_ready, 1)
                act.wait_ge(g_oT_ready, 2 * NT)
                act.nop().then_inc(attention_done, 1)

            with act.Else():
                full_attention()

            with act.If(last_block_only(act)):
                for j in range(UNITS):
                    routing(NI - 1, j)
            with act.Else():
                with act.Fori(0, NI) as i:
                    for j in range(UNITS):
                        routing(i, j)
            act.wait_ge(attention_done, ENGINES)
            write_pads(act, NE // 2, NE)

            def copy_xgT(s, buf):
                act.wait_ge(xgT_ps, s + 1)
                act.copy(xgT[:, buf, :, :], ps_t[1][:, 0:KT * P].rearrange("p (k n) -> p k n", k=KT))\
                   .then_inc(xgT_ready, 1)

            def silu_of(s):
                act.wait_ge(h1_ps, s + 1)
                if not (isinstance(s, int) and s == 0):
                    act.wait_ge(gated_ready, s)
                act.activation(silu[:, :], ps_s[0][:, :], ACT.Silu).then_inc(silu_ready, 1)

            def copy_gatedT(s):
                act.wait_ge(gatedT_ps, s + 1)
                if not (isinstance(s, int) and s == 0):
                    act.wait_ge(y_ps, s + 1)
                act.copy(gatedT[:, :, :], ps_t[0][:, :].rearrange("p (k n) -> p k n", k=HT)).then_inc(gatedT_ready, 1)

            def ffn_tile(i, k):
                s = RING * i + k
                copy_gatedT(s)
                if not (isinstance(s, int) and s + 1 >= NG):
                    silu_of(s + 1)
                if not (isinstance(s, int) and s + 2 >= NG):
                    copy_xgT(s + 2, k % 2)

            act.sem_inc(gatedT_ready, 1)
            copy_xgT(0, 0)
            silu_of(0)
            copy_xgT(1, 1)
            with act.Fori(0, FULL // RING) as i:
                for k in range(RING):
                    ffn_tile(i, k)
            there = tiles_there(act)
            for s in range(FULL, NG):
                with act.If(there > s):
                    ffn_tile(s // RING, s % RING)

        @block.vector
        def _(dve):
            def rows(col):
                return stat[:, col, :].unsqueeze(2).to_broadcast([P, NT, D])

            dve.wait_ge(kv_in, CTX_WK)
            for copy in range(2):
                dve.tensor_copy(wk2_sb[:, 1, :, copy, :], wk_sb[:, 1, :].rearrange("p (h d) -> p h d", h=H))\
                   .then_inc(wk2_dve, 1)
            def q_low_parts(b, batch, odd, bank=ps_a):
                dve.wait_ge(q_hi, 2 * batch + odd + 1)
                src = bank[:, :].rearrange("p (c n) -> p c n", c=2)
                heads = q_parts[:, 4 * b + odd:4 * b + 4:2, :]
                p0, p1 = odd * HD, (1 - odd) * HD
                dve.tensor_tensor(heads[p1:p1 + HD], src[p0:p0 + HD], heads[p0:p0 + HD], ALU.subtract)\
                   .then_inc(q_split, 1)

            def mask_words(c):
                dve.wait_ge(mask_in[c % 2], 16 * (c // 2 + 1))
                words = mask8[:, c % 2, :, :].bitcast(I32)
                dve.tensor_reduce(word_max[:, 0, c:c + 1], words[:, :, 0:LAST0 // 4], AX.XY, ALU.max).then_inc(mask_seen, 1)
                dve.tensor_reduce(word_max[:, 1, c * MT:(c + 1) * MT], words[:, :, LAST0 // 4:], AX.X, ALU.max)\
                   .then_inc(mask_seen, 1)

            def k_low(h):
                dve.wait_ge(k_hi_ready, h + 1)
                dve.scalar_tensor_tensor(out=k_lo[:, h, :], in0=[ps_a, ps_b][h % 2][:, 0:EVEN], scalar=-1.0,
                                         in1=k_hi[:, h, :], op0=ALU.mult, op1=ALU.subtract)\
                   .then_inc(k_lo_ready, 1)

            for h in range(H // 2):
                k_low(h)
                if h == 0:
                    dve.wait_ge(x_in, 16)
                for t in (2 * h, 2 * h + 1):
                    dve.bn_stats(halves[:, t, :], xs[:, t, :]).then_inc(ln_stat, 1)
            dve.wait_ge(ln_stat, NT)
            for t in range(NT):
                dve.bn_aggr(mean_var[:, t, :], halves[:, t, :]).then_inc(ln_stat, 1)
            dve.wait_ge(ln_stat, 2 * NT)
            dve.tensor_copy(stat[:, 0, :], mean_var[:, :, 0]).then_inc(ln, 1)
            dve.tensor_scalar(stat[:, 1, :], mean_var[:, :, 1], EPS, None, ALU.add).then_inc(ln, 1)
            dve.wait_ge(std_ready, 1)
            dve.reciprocal(stat[:, 3, :], stat[:, 2, :]).then_inc(ln, 1)
            dve.wait_ge(ln, 3)
            for h in range(H // 2, H):
                for t in (2 * h - NT, 2 * h - NT + 1):
                    dve.tensor_scalar(xn[:, t, :], xs[:, t, :], stat[:, 0, t:t + 1], stat[:, 3, t:t + 1],
                                      ALU.subtract, ALU.mult).then_inc(xn_ready, 1)
                k_low(h)
            for c in range(1, 8, 2):
                dve.wait_ge(xnT_ps, c + 1)
                k, t0 = c % 2, 4 * (c // 2)
                dve.tensor_copy(xnT[:, k, t0 * P:(t0 + 4) * P], ps_t[1][:, :]).then_inc(xnT_dve, 1)
                for half in range(2):
                    dve.wait_ge(v_hi_ready, c + half)
                    v = v_parts[:, c // 2, 8 * half:8 * half + 8, :, :]
                    dve.tensor_tensor(v[:, :, 1, :], ps_s[half][0:STRIP, :].rearrange("p (h d) -> p h d", h=8),
                                      v[:, :, 0, :], ALU.subtract).then_inc(v_lo_ready, 1)
                mask_words(c - 1)
                mask_words(c)
            dve.wait_ge(mask_seen, 2 * NM)
            dve.tensor_reduce(rowflag[:, 0:1], word_max[:, 0, 0:NM], AX.X, ALU.max).then_inc(flag_step, 1)
            dve.tensor_reduce(rowflag[:, 1:2], word_max[:, 1, :], AX.X, ALU.min).then_inc(flag_step, 1)
            dve.wait_ge(flag_step, 2)
            dve.tensor_scalar(rowflag[:, 2:3], rowflag[:, 0:1], 0.0, None, ALU.is_equal).then_inc(flag_step, 1)
            dve.tensor_scalar(rowflag[:, 3:4], rowflag[:, 1:2], 0.0, None, ALU.is_gt).then_inc(flag_step, 1)
            dve.wait_ge(flag_step, 4)
            dve.tensor_tensor(rowflag[:, 0:1], rowflag[:, 2:3], rowflag[:, 3:4], ALU.mult).then_inc(flag_step, 1)
            def choose_experts(i, n):
                def spread(v):
                    return v.unsqueeze(2).to_broadcast([P, 2, NE])

                ranks = rank[:, :].unsqueeze(1).to_broadcast([P, 2, NE])
                c, n_c = n // 6, n % 6
                if n == 0:
                    dve.wait_ge(logits_ready, i + 1)
                else:
                    dve.wait_ge(chosen_step, 11 * i + n)
                if n_c == 0:
                    ins = dve.tensor_reduce(top[:, c, :], logits[:, :, :], AX.X, ALU.max)
                if n_c == 1:
                    ins = dve.tensor_tensor(won[:, :, :], logits[:, :, :], spread(top[:, c, :]), ALU.is_equal)
                if n_c == 2:
                    ins = dve.tensor_tensor(won[:, :, :], won[:, :, :], ranks, ALU.mult)
                if n_c == 3:
                    ins = dve.tensor_reduce(pick[:, :], won[:, :, :], AX.X, ALU.max)
                if n_c == 4:
                    ins = dve.tensor_tensor(chosen[:, c, :, :], ranks, spread(pick[:, :]), ALU.is_equal)
                if n_c == 5:
                    ins = dve.scalar_tensor_tensor(out=logits[:, :, :], in0=chosen[:, 0, :, :], scalar=-3e38,
                                                   in1=logits[:, :, :], op0=ALU.mult, op1=ALU.add)
                ins.then_inc(chosen_step, 1)

            def early_routing(i, j):
                if 20 <= j < 26:
                    choose_experts(i, 2 * (j - 20))

            def routing(i, j):
                if j == 3:
                    dve.wait_ge(pair_added, i + 1)
                    if not first(i, 1):
                        dve.wait_ge(rows_ready, i)
                    dve.sem_inc(carried, 1)
                    for t in (0,):
                        dve.bn_stats(halves[:, t, :], xs[:, bass.ds(2 * i + t, 1), :].squeeze(1)).then_inc(stats_taken, 1)
                if j == 4:
                    dve.sem_inc(carried, 1)
                    dve.bn_stats(halves[:, 1, :], xs[:, bass.ds(2 * i + 1, 1), :].squeeze(1)).then_inc(stats_taken, 1)
                if j == 5:
                    dve.wait_ge(stats_taken, 2 * i + 2)
                    dve.sem_inc(carried, 1)
                    for t in range(2):
                        ins = dve.bn_aggr(mean_var[:, t, :], halves[:, t, :])
                    ins.then_inc(stats_ready, 1)
                if 20 <= j < 25:
                    choose_experts(i, 2 * (j - 20) + 1)
                if j == 26:
                    dve.wait_ge(chosen_step, 11 * i + 11)
                    dve.tensor_tensor(both[:, :, :], chosen[:, 0, :, :], chosen[:, 1, :, :], ALU.add).then_inc(both_ready, 1)
                    dve.tensor_tensor(gap[:, 0, :], top[:, 1, :], top[:, 0, :], ALU.subtract).then_inc(gap_ready, 1)
                if j == 27:
                    dve.wait_ge(exp_gap_ready, i + 1)
                    dve.tensor_scalar(gap[:, 2, :], gap[:, 1, :], 1.0, None, ALU.add).then_inc(denom_ready, 1)
                if j == 28:
                    dve.wait_ge(denom_ready, i + 1)
                    dve.reciprocal(gap[:, 2, :], gap[:, 2, :]).then_inc(weigher_ready, 1)

            for b in range(4):
                for odd in range(2):
                    q_low_parts(b, b, odd, [ps_a, ps_b][b % 2])
                if b == 1:
                    dve.wait_ge(flag_sum, 1)
                    dve.tensor_scalar(plainflag[:, :], ps_o[0][0:1, 0:1], float(P), None, ALU.is_equal)\
                       .then_inc(flag_ready, 1)

            def fast_attention():
                def mask_and_max(i, k):
                    n = UNITS * i + k
                    if k % H == 0:
                        dve.wait_ge(bias_in[k % UNITS // H], 16 * (i + k // UNITS) + 16)
                    dve.wait_ge(scores_ready, n + 1)
                    if not first(n, 2):
                        dve.wait_ge(probs_ready, n - 1)
                    if not isinstance(n, int):
                        dve.sem_inc(carried, 1)
                    dve.tensor_tensor_reduce(masked[:, k % 2, :], ps_s[k % 2][:, 0:LASTK],
                                             bias_cur[:, k % UNITS // H, k % 2, :], HD ** -0.5, 3e38, ALU.add, ALU.min,
                                             neg_max[:, k % 2:k % 2 + 1]).then_inc(masked_ready, 1)

                def inverses(i, g):
                    dve.wait_ge(probs_ready, UNITS * i + 8 * g + 8)
                    if not first(4 * i + g, 1):
                        dve.wait_ge(invT_ps, 4 * i + g)
                    dve.reciprocal(inv_sum[:, :, :], sum_exp[:, g % 2, :, :]).then_inc(inv_ready, 1)

                def low_inverses(i, g):
                    dve.wait_ge(invT_hi, 4 * i + g + 1)
                    dve.tensor_tensor(invT[LOW0:LOW0 + 4, :], ps_b[0:4, 0:PAIR], invT[0:4, :], ALU.subtract)\
                       .then_inc(invT_lo, 1)

                def normalise(i, g):
                    dve.wait_ge(inv_spread, 4 * i + g + 1)
                    dve.wait_ge(oT_ready, H * i + 4 * g + 4)
                    four = oT[:, g % 2 * 2:g % 2 * 2 + 2, :]
                    dve.tensor_tensor(four, ps_b[:, :].rearrange("p (c n) -> p c n", c=2), four, ALU.mult)\
                       .then_inc(normed, 1)

                def low_probs(i, k):
                    dve.wait_ge(probsT_hi, UNITS * i + k + 1)
                    unit = probsT[:, k // 2 % 2, :, :, k % 2 * P:(k % 2 + 1) * P]
                    dve.tensor_tensor(unit[:, :, 1, :], ps_t[k % 2][0:STRIP, :].rearrange("p (s n) -> p s n", s=NS),
                                      unit[:, :, 0, :], ALU.subtract).then_inc(probsT_lo, 1)

                def output(i, h):
                    dve.wait_ge(o_low, H * i + h + 1)
                    p0 = h % 2 * HD
                    dst = oT[p0:p0 + HD, h // 2 % 4, :]
                    dve.tensor_tensor(dst, ps_o[h % 2][0:HD, 0:PAIR], dst, ALU.add).then_inc(oT_ready, 1)

                def residual(i, g):
                    dve.wait_ge(wo_ps, 4 * i + g + 1)
                    two = xs[:, bass.ds(2 * i, 2), :]
                    dve.scalar_tensor_tensor(out=two, in0=ps_b[:, :].rearrange("p (t d) -> p t d", t=2),
                                             scalar=tanh_g[:, 0:1], in1=two, op0=ALU.mult, op1=ALU.add)\
                       .then_inc(x2_ready, 1)

                def step(i, j, last=False):
                    if not (last and j + 6 >= UNITS):
                        mask_and_max(i, j + 6)
                    if j >= 10 and j % 8 == 2:
                        residual(i, j // 8 - 1)
                    if j == 2 and not first(i, 1):
                        residual(i - 1, 3)
                        dve.wait_ge(x2_ready, 4 * i)
                        dve.sem_inc(pair_added, 1)
                    if j >= 0 and j % 8 == 5:
                        low_inverses(i, j // 8)
                    if j >= 0 and not first(i, 1):
                        early_routing(i - 1, j)
                    if j >= 0 and j % 8 == 3:
                        inverses(i, j // 8)
                    if j + 4 >= 0 and not (last and j + 4 >= UNITS):
                        low_probs(i, j + 4)
                    if j >= 0 and j % 2 == 1:
                        output(i, j // 2)
                    if j >= 0 and j % 8 == 7:
                        normalise(i, j // 8)
                    if j >= 0 and j % 8 == 6 and not last:
                        q_low_parts(j // 8, 4 * i + 4 + j // 8, 0)
                    if j >= 8 and j % 8 == 0 and not last:
                        q_low_parts(j // 8 - 1, 4 * i + 3 + j // 8, 1)
                    if j >= 0 and not first(i, 1):
                        routing(i - 1, j)
                    if j == 0 and not first(i, 1):
                        q_low_parts(3, 4 * i + 3, 1)

                dve.wait_ge(tanh_ready, 1)
                for j in range(-6, UNITS):
                    step(0, j)
                with dve.Fori(1, NI - 1) as i:
                    for j in range(UNITS):
                        step(i, j)
                for j in range(UNITS):
                    step(NI - 1, j, last=True)
                residual(NI - 1, 3)
                dve.wait_ge(x2_ready, 4 * NI)
                dve.sem_inc(pair_added, 1)
                dve.nop().then_inc(attention_done, 1)

            with dve.If(last_block_only(dve)):
                fast_attention()
            def full_attention():
                settled(dve)
                for free in (g_klo_ready, g_masked_ready, g_o_ready, g_x2_ready, g_bias_ready):
                    dve.sem_inc(free, 1)
                dve.wait_ge(g_w_in, 48)
                with dve.Fori(0, NT) as i:
                    dve.wait_ge(g_mask_in, 16 * i + 16)
                    dve.tensor_scalar(g_bias[:, :], g_mask8[:, :], -MASKED, MASKED, ALU.mult, ALU.add)\
                       .then_inc(g_bias_ready, 1)
                    for half in range(2):
                        dve.wait_ge(q_hi, 4 * i + 2 * half + 10)
                        src = ps_a[:, :].rearrange("p (c n) -> p c n", c=4)
                        even = q_parts[:, 8 * half:8 * half + 8:2, 0:P]
                        odd = q_parts[:, 8 * half + 1:8 * half + 8:2, 0:P]
                        dve.tensor_tensor(even[HD:P], src[0:HD], even[0:HD], ALU.subtract)
                        dve.tensor_tensor(odd[0:HD], src[HD:P], odd[HD:P], ALU.subtract).then_inc(q_split, 1)
                    dve.wait_ge(q_split, 2 * i + 10)
                    dve.wait_ge(g_bias_ready, i + 2)
                    dve.sem_inc(carried, 1)
                    with dve.Fori(0, H) as h:
                        n = H * i + h
                        dve.wait_ge(g_pv_block, NB * n + 1)
                        dve.tensor_copy(g_q[:, :], q_parts[:, bass.ds(h, 1), 0:P].squeeze(1)).then_inc(g_staged, 1)
                        for copy in range(2):
                            dve.tensor_copy(g_wk2[:, :, copy, :], g_wk[:, :, bass.ds(h * HD, HD)]).then_inc(g_staged, 1)
                        for b in range(NB):
                            k0, keys, even, _ = block_of(b)
                            dve.wait_ge(g_khi_ready, NB * n + b + 1)
                            dve.scalar_tensor_tensor(out=g_klo[:, 0:even], in0=ps_a[:, 0:even], scalar=-1.0,
                                                     in1=g_khi[:, 0:even], op0=ALU.mult, op1=ALU.subtract)\
                               .then_inc(g_klo_ready, 1)
                            dve.wait_ge(g_scores_ready, NB * n + b + 1)
                            dve.sem_inc(carried, 1)
                            dve.tensor_tensor_reduce(g_probs[:, k0:k0 + keys], ps_s[0][:, 0:keys],
                                                     g_bias[:, k0:k0 + keys], HD ** -0.5, 3e38, ALU.add, ALU.min,
                                                     g_min[:, b:b + 1]).then_inc(g_masked_ready, 1)
                        dve.wait_ge(g_masked_ready, NB * n + NB + 1)
                        dve.tensor_reduce(g_min[:, 4:5], g_min[:, 0:NB], AX.X, ALU.min).then_inc(g_min_ready, 1)
                        dve.wait_ge(g_pv_block, NB * n + NB + 1)
                        dve.reciprocal(g_min[:, 5:6], ps_o[0][:, HD:VW]).then_inc(g_inv_ready, 1)
                        dve.wait_ge(g_inv_ready, n + 1)
                        dve.tensor_scalar(o_rows[:, bass.ds(h * HD, HD)], ps_o[0][:, 0:HD], g_min[:, 5:6], None,
                                          ALU.mult).then_inc(g_o_ready, 1)
                    dve.wait_ge(g_wo_ps, i + 1)
                    dve.scalar_tensor_tensor(out=xs[:, i, :], in0=ps_b[:, 0:D], scalar=tanh_g[:, 0:1],
                                             in1=xs[:, i, :], op0=ALU.mult, op1=ALU.add).then_inc(g_x2_ready, 1)
                dve.wait_ge(g_x2_ready, NT + 1)
                dve.sem_inc(pair_added, NI)
                dve.nop().then_inc(attention_done, 1)

            with dve.Else():
                full_attention()

            with dve.If(last_block_only(dve)):
                for j in range(UNITS):
                    early_routing(NI - 1, j)
                    routing(NI - 1, j)
            with dve.Else():
                with dve.Fori(0, NI) as i:
                    for j in range(UNITS):
                        early_routing(i, j)
                        routing(i, j)
            dve.wait_ge(attention_done, ENGINES)
            steps = [0]

            def step(ins):
                steps[0] += 1
                ins.then_inc(route, 1)
                dve.wait_ge(route, steps[0])

            dve.wait_ge(routed, NI)
            dve.tensor_copy(pad_row[:, :], taken[0:1, :]).then_inc(pad_rows_ready, 1)
            step(dve.tensor_scalar(tiles[:, 3, :], number[:, :], float(REGION), None, ALU.mult))
            step(dve.tensor_tensor(total[:, :], taken[:, :], tiles[:, 3, :], ALU.subtract))
            step(dve.tensor_tensor(has_tile[:, :, :], total[:, :].unsqueeze(2).to_broadcast([P, NE, NT]),
                                   fill[:, :].unsqueeze(1).to_broadcast([P, NE, NT]), ALU.is_gt))
            step(dve.tensor_reduce(tiles[:, 0, :], has_tile[:, :, :], AX.X, ALU.add))
            dve.tensor_scalar(leap[:, :], tiles[0:1, 0, :], -float(P), float(REGION), ALU.mult, ALU.add).then_inc(leap_ready, 1)
            dve.wait_ge(leap_ready, 1)
            src = 0
            for shift in (1, 2, 4):
                a, b = tiles[:, src, :], tiles[:, (src + 1) % 3, :]
                step(dve.tensor_copy(b[:, 0:shift], a[:, 0:shift]))
                step(dve.tensor_tensor(b[:, shift:], a[:, shift:], a[:, 0:NE - shift], ALU.add))
                src = (src + 1) % 3
            ends = tiles[0:1, src, :]
            step(dve.tensor_copy(n_tiles[:, :], ends[:, NE - 1:]))
            turns = turn[0:1, :].unsqueeze(2).to_broadcast([1, NSCHED, NE])
            past_end, leaps = sched_f[:, 0, :, :], sched_f[:, 1, :, :]
            step(dve.tensor_tensor(past_end, turns, ends.unsqueeze(1).to_broadcast([1, NSCHED, NE]), ALU.is_ge))
            dve.tensor_tensor(leaps, past_end, leap[:, :].unsqueeze(1).to_broadcast([1, NSCHED, NE]), ALU.mult)\
               .then_inc(leap_ready, 1)
            step(dve.tensor_reduce(sched_s[:, 1, :], past_end, AX.X, ALU.add))
            dve.wait_ge(leap_ready, 2)
            step(dve.tensor_reduce(sched_s[:, 0, :], leaps, AX.X, ALU.add))
            step(dve.scalar_tensor_tensor(out=sched_s[:, 0, :], in0=turn[0:1, :], scalar=float(P), in1=sched_s[:, 0, :],
                                          op0=ALU.mult, op1=ALU.add))
            dve.tensor_scalar(sched[:, 1, :], sched_s[:, 1, :], float(NE - 1), None, ALU.min).then_inc(sched_ready, 1)
            dve.tensor_scalar(sched[:, 0, :], sched_s[:, 0, :], float(NOWHERE), None, ALU.min).then_inc(sched_ready, 1)

            def gate(s):
                dve.wait_ge(silu_ready, s + 1)
                dve.wait_ge(h2_ps, s + 1)
                if not (isinstance(s, int) and s == 0):
                    dve.wait_ge(gatedT_ps, s)
                dve.tensor_tensor(gated[:, :], ps_s[1][:, :], silu[:, :], ALU.mult).then_inc(gated_ready, 1)

            def weigh(i, k):
                s = RING * i + k
                dve.wait_ge(xg_in[k % RING], 16 * (i + k // RING + 1))
                if not first(s, RING):
                    dve.wait_ge(added, 16 * (s - RING + 1))
                dve.tensor_copy(ids[:, k % RING:k % RING + 1], xg[:, k % RING, ID_COL:]).then_inc(ids_ready, 1)
                dve.wait_ge(y_ps, s + 2)
                if not first(s, 2):
                    dve.wait_ge(added, 16 * (s - 1))
                dve.tensor_scalar(yg[:, k % 2, :], ps_o[0][:, 0:D], xg[:, k % RING, W_COL:W_COL + 1], None, ALU.mult)\
                   .then_inc(y_ready, 1)

            def ffn_tile(i, k):
                s = RING * i + k
                if not (isinstance(s, int) and s + 1 >= NG):
                    gate(s + 1)
                weigh(i, k)

            dve.sem_inc(y_ready, 1)
            gate(0)
            for k in range(RING):
                ffn_tile(0, k)
            with dve.Fori(1, FULL // RING) as i:
                for k in range(RING):
                    ffn_tile(i, k)
            there = tiles_there(dve)
            for s in range(FULL, NG):
                with dve.If(there > s):
                    ffn_tile(s // RING, s % RING)

        @block.tensor
        def _(pe):
            pe.wait_ge(const_ready, CONSTS)
            pe.wait_ge(pads_ready, PADS)
            pe.wait_ge(wk2_act, 2)
            pe.wait_ge(wk2_dve, 2)
            for h in range(H):
                if h >= 2:
                    pe.wait_ge(k_lo_ready, h - 1)
                for k in range(KT):
                    mm = pe.matmul([ps_a, ps_b][h % 2][:, 0:EVEN],
                                   wk2_sb[:, k, h, :, :].rearrange("p c d -> p (c d)"),
                                   ctx_last[:, k, 0:EVEN], start=(k == 0), stop=(k == KT - 1))
                mm.then_inc(k_ps, 1)
            for c in range(8):
                s, half, k, t0 = c // 2, c % 2, c % 2, 4 * (c // 2)
                pe.wait_ge(xn_ready, t0 + 4)
                if c >= 2:
                    pe.wait_ge([xnT_act, xnT_dve][c % 2], c // 2)
                    pe.wait_ge(v_lo_ready, c - 1)
                if c == 0:
                    pe.wait_ge(wv_in, 16)
                for t in range(4):
                    last = pe.transpose(ps_t[c % 2][:, t * P:(t + 1) * P], xn[:, t0 + t, k * P:(k + 1) * P],
                                        ident[:, :])
                last.then_inc(xnT_ps, 1)
                for k in range(KT):
                    mm = pe.matmul(ps_s[c % 2][0:STRIP, :], ctx_last[:, k, s * STRIP:(s + 1) * STRIP],
                                   wv_sb[:, k, half * 512:(half + 1) * 512], start=(k == 0), stop=(k == KT - 1))
                mm.then_inc(v_ps, 1)
            def project_q(pair, k, i, bank=ps_a):
                return pe.matmul(bank[:, pair % 2 * PAIR:(pair % 2 + 1) * PAIR], wq_sb[:, k, pair * P:(pair + 1) * P],
                                 xnT[:, k, bass.ts(i, PAIR)], start=(k == 0), stop=(k == KT - 1))

            pe.wait_ge(wg_in, 16)
            pe.wait_ge(w_in, W_ALL)
            pe.wait_ge(k_lo_ready, H)
            pe.wait_ge(xnT_act, 4)
            pe.wait_ge(xnT_dve, 4)
            for b in range(4):
                if b >= 2:
                    pe.wait_ge(q_split, 2 * b - 2)
                for pair in (2 * b, 2 * b + 1):
                    for k in range(KT):
                        mm = project_q(pair, k, 0, [ps_a, ps_b][b % 2])
                mm.then_inc(q_ps, 1)
                if b == 1:
                    pe.wait_ge(flag_step, 5)
                    pe.matmul(ps_o[0][0:1, 0:1], ones[:, 0:1], rowflag[:, 0:1], start=True, stop=True)\
                      .then_inc(flag_sum, 1)
            def routing(i, j):
                if j == 11:
                    pe.wait_ge(rows_ready, i + 1)
                    for t in range(2):
                        for k in range(KT):
                            mm = pe.transpose(ps_b[:, (KT * t + k) * P:(KT * t + k + 1) * P],
                                              rows[:, 0, t, k * P:(k + 1) * P], ident[:, :])
                    mm.then_inc(rowsT_ps, 1)
                if j == 19:
                    pe.wait_ge(rowsT_ready, i + 1)
                    for t in range(2):
                        for k in range(KT):
                            mm = pe.matmul(ps_b[:, t * NE:(t + 1) * NE], rowsT[:, t, k, :], wg_sb[:, k, :],
                                           start=(k == 0), stop=(k == KT - 1))
                    mm.then_inc(logits_ps, 1)
                if j == 27:
                    pe.wait_ge(both_ready, i + 1)
                    pe.wait_ge(logits_ready, i + 1)
                    flat = both[:, :, :].rearrange("p t e -> p (t e)")
                    pe.matmul(ps_b[:, 0:2 * NE], before[:, :], flat, start=True, stop=True)
                    pe.matmul(ps_b[:, 2 * NE:4 * NE], ones[:, :], flat, start=True, stop=True).then_inc(counts_ps, 1)

            def fast_attention():
                pe.wait_ge(v_lo_ready, 2 * NS)
                pe.wait_ge(pads_set, 1)
                pe.wait_ge(head_of_set, 5)

                def scores(i, k):
                    n, h, t = UNITS * i + k, k // 2 % H, k % 2
                    if k % 8 == 0:
                        pe.wait_ge(q_split, 2 * (4 * i + k // 8 + 1))
                    if not first(n, 2):
                        pe.wait_ge(masked_ready, n - 1)
                    q = q_parts[:, h, t * P:(t + 1) * P]
                    pe.matmul(ps_s[t][:, 0:EVEN], q, k_hi[:, h, :], start=True, stop=False)
                    pe.matmul(ps_s[t][:, 0:EVEN], q, k_lo[:, h, :], start=False, stop=True).then_inc(scores_ready, 1)

                def transposes(i, k):
                    n, t = UNITS * i + k, k % 2
                    pe.wait_ge(probs_ready, n + 1)
                    if not first(n, 2):
                        pe.wait_ge(probsT_lo, n - 1)
                    for s in range(NS):
                        mm = pe.transpose(ps_t[t][0:STRIP, s * P:(s + 1) * P],
                                          probs[:, t, s * STRIP:(s + 1) * STRIP], ident[:, :])
                    mm.then_inc(probsT_ps, 1)

                def probs_v(i, h, part):
                    if part == 0:
                        pe.wait_ge(probsT_lo, UNITS * i + 2 * h + 2)
                        if not first(H * i + h, 2):
                            pe.wait_ge(oT_ready, H * i + h - 1)
                    for s in range(part * NS // 2, (part + 1) * NS // 2):
                        for c in range(2):
                            mm = pe.matmul(ps_o[h % 2][:, 0:PAIR],
                                           v_parts[:, s, h % H, :, :].rearrange("p c d -> p (c d)"),
                                           probsT[:, h % 2, s, c, :], start=(s == 0 and c == 0),
                                           stop=(s == NS - 1 and c == 1))
                    if part == 1:
                        mm.then_inc(pv_ready, 1)

                def transpose_inverses(i, g):
                    pe.wait_ge(inv_ready, 4 * i + g + 1)
                    if g > 0 and not first(i, 1):
                        pe.wait_ge([None, rowsT_ready, logits_ready, counts_ready][g], i)
                    if not first(4 * i + g, 1):
                        pe.wait_ge(x2_ready, 4 * i + g)
                    for t in range(2):
                        mm = pe.transpose(ps_b[0:4, t * P:(t + 1) * P], inv_sum[:, t, :], ident[:, :])
                    mm.then_inc(invT_ps, 1)

                def spread_inverses(i, g):
                    pe.wait_ge(invT_lo, 4 * i + g + 1)
                    for c in range(2):
                        mm = pe.matmul(ps_b[:, c * PAIR:(c + 1) * PAIR], head_of[:, c, :, :].rearrange("p h d -> p (h d)"),
                                       invT[:, :], start=True, stop=True)
                    mm.then_inc(inv_spread, 1)

                def out_projection(i, g):
                    pe.wait_ge(normed, 4 * i + g + 1)
                    for t in range(2):
                        for p in (2 * g, 2 * g + 1):
                            mm = pe.matmul(ps_b[:, t * D:(t + 1) * D], oT[:, p % 4, t * P:(t + 1) * P], wo_sb[:, p, :],
                                           start=(p == 2 * g), stop=(p == 2 * g + 1))
                    mm.then_inc(wo_ps, 1)

                def next_queries(i, j):
                    b, part = j // 8, j % 8 - 2
                    if part == 0:
                        pe.wait_ge(q_split, 2 * (4 * i + 4 + b))
                    if 0 <= part < 4:
                        mm = project_q(2 * b + part // 2, part % 2, i + 1)
                        if part == 3:
                            mm.then_inc(q_ps, 1)

                def step(i, j, last=False):
                    if not (last and j + 6 >= UNITS):
                        scores(i, j + 6)
                    if j + 4 >= 0 and not (last and j + 4 >= UNITS):
                        transposes(i, j + 4)
                    if j >= 0 and j % 2 == 0:
                        probs_v(i, j // 2, 1)
                    if j >= -1 and j % 2 == 1 and not (last and j == UNITS - 1):
                        probs_v(i, (j + 1) // 2, 0)
                    if j >= 0 and j % 8 == 4:
                        transpose_inverses(i, j // 8)
                    if j >= 0 and j % 8 == 6:
                        spread_inverses(i, j // 8)
                    if j >= 9 and j % 8 == 1:
                        out_projection(i, j // 8 - 1)
                    if j == 1 and not first(i, 1):
                        out_projection(i - 1, 3)
                    if j >= 0 and not last:
                        next_queries(i, j)
                    if j in (11, 19, 27) and not first(i, 1):
                        pe.wait_ge(x2_ready, 4 * i + j // 8)
                        routing(i - 1, j)

                for j in range(-6, UNITS):
                    step(0, j)
                with pe.Fori(1, NI - 1) as i:
                    for j in range(UNITS):
                        step(i, j)
                for j in range(UNITS):
                    step(NI - 1, j, last=True)
                out_projection(NI - 1, 3)
                pe.wait_ge(wo_ps, 4 * NI)
                pe.nop().then_inc(attention_done, 1)

            with pe.If(last_block_only(pe)):
                fast_attention()
            def full_attention():
                settled(pe)
                pe.wait_ge(g_pads, 3)
                pe.wait_ge(g_w_in, 48)
                pe.sem_inc(g_pv_block, 1)
                for c in range(2 * NB * NS):
                    half, s, (k0, _, _, w) = c % 2, c // 2 % NS, block_of(c // 2 // NS)
                    if c >= 2:
                        pe.wait_ge(g_v_ready, c - 1)
                    for k in range(KT):
                        mm = pe.matmul(ps_s[half][0:w, :], g_ctxT[:, k, k0 + s * w:k0 + (s + 1) * w],
                                       g_wv[:, k, half * 512:(half + 1) * 512], start=(k == 0), stop=(k == KT - 1))
                    mm.then_inc(g_v_ps, 1)
                pe.wait_ge(g_v_ready, 2 * NB * NS)
                with pe.Fori(0, NT) as i:
                    pe.wait_ge(g_x2_ready, i + 1)
                    for half in range(2):
                        pe.wait_ge(q_split, 2 * i + half + 8)
                        for pair in range(4):
                            for k in range(KT):
                                mm = pe.matmul(ps_a[:, pair * P:(pair + 1) * P],
                                               wq_sb[:, k, (4 * half + pair) * P:(4 * half + pair + 1) * P],
                                               xnT[:, k, bass.ts(i, P)], start=(k == 0), stop=(k == KT - 1))
                        mm.then_inc(q_ps, 1)
                    pe.wait_ge(q_split, 2 * i + 10)
                    pe.sem_inc(carried, 1)
                    with pe.Fori(0, H) as h:
                        n = H * i + h
                        pe.wait_ge(g_staged, 3 * n + 3)
                        for b in range(NB):
                            k0, keys, even, _ = block_of(b)
                            pe.wait_ge(g_klo_ready, NB * n + b + 1)
                            for k in range(KT):
                                mm = pe.matmul(ps_a[:, 0:even], g_wk2[:, k, :, :].rearrange("p c d -> p (c d)"),
                                               g_ctxT[:, k, k0:k0 + even], start=(k == 0), stop=(k == KT - 1))
                            mm.then_inc(g_k_ps, 1)
                            pe.wait_ge(g_klo_ready, NB * n + b + 2)
                            pe.wait_ge(g_masked_ready, NB * n + b + 1)
                            pe.matmul(ps_s[0][:, 0:even], g_q[:, :], g_khi[:, 0:even], start=True, stop=False)
                            pe.matmul(ps_s[0][:, 0:even], g_q[:, :], g_klo[:, 0:even], start=False, stop=True)\
                              .then_inc(g_scores_ready, 1)
                        pe.wait_ge(g_probs_ready, n + 1)
                        pe.wait_ge(g_o_ready, n + 1)
                        for b in range(NB):
                            k0, _, _, w = block_of(b)
                            pe.wait_ge(g_probsT_ready, NB * n + b + 1)
                            for s in range(NS):
                                mm = pe.transpose(ps_t[0][0:w, s * P:(s + 1) * P],
                                                  g_probs[:, k0 + s * w:k0 + (s + 1) * w], ident[:, :])
                            mm.then_inc(g_probsT_ps, 1)
                            pe.wait_ge(g_probsT_ready, NB * n + b + 2)
                            for s in range(NS):
                                mm = pe.matmul(ps_o[0][:, 0:VW], g_probsT[0:w, s * P:(s + 1) * P],
                                               g_v[0:w, b * NS + s, bass.ds(h, 1), :].squeeze(1),
                                               start=(b == 0 and s == 0), stop=(b == NB - 1 and s == NS - 1))
                            mm.then_inc(g_pv_block, 1)
                    pe.wait_ge(g_o_ready, H * i + H + 1)
                    for half in range(2):
                        for p in range(4):
                            mm = pe.transpose([ps_b, ps_a][half][:, p * P:(p + 1) * P],
                                              o_rows[:, (4 * half + p) * P:(4 * half + p + 1) * P], ident[:, :])
                        mm.then_inc(g_oT_ps, 1)
                    pe.wait_ge(g_oT_ready, 2 * i + 2)
                    for p in range(H // 2):
                        mm = pe.matmul(ps_b[:, 0:D], g_oT[:, p, :], wo_sb[:, p, :], start=(p == 0), stop=(p == H // 2 - 1))
                    mm.then_inc(g_wo_ps, 1)
                pe.wait_ge(g_wo_ps, NT)
                pe.nop().then_inc(attention_done, 1)

            with pe.Else():
                full_attention()

            with pe.If(last_block_only(pe)):
                for j in range(UNITS):
                    routing(NI - 1, j)
            with pe.Else():
                with pe.Fori(0, NI) as i:
                    for j in range(UNITS):
                        routing(i, j)
            pe.wait_ge(attention_done, ENGINES)

            def transpose_x(i, k):
                s = RING * i + k
                pe.wait_ge(xg_in[k % RING], 16 * (i + k // RING + 1))
                if not (isinstance(s, int) and s == 0):
                    pe.wait_ge(xgT_ready, s)
                for c in range(KT):
                    mm = pe.transpose(ps_t[1][:, c * P:(c + 1) * P], xg[:, k % RING, c * P:(c + 1) * P], ident[:, :])
                mm.then_inc(xgT_ps, 1)

            def hidden(s, buf, expert, w, bank, done):
                for k in range(KT):
                    mm = pe.matmul(bank[:, :], xgT[:, buf, k, :], w[:, k, bass.ds(expert, 1), :].squeeze(1), start=(k == 0), stop=(k == KT - 1))
                mm.then_inc(done, 1)

            def first_hidden(s, buf, expert):
                pe.wait_ge(xgT_ready, s + 1)
                pe.wait_ge(experts_ready, expert + 1)
                if not (isinstance(s, int) and s == 0):
                    pe.wait_ge(silu_ready, s)
                hidden(s, buf, expert, w1_sb, ps_s[0], h1_ps)

            def second_hidden(s, buf, expert):
                if not (isinstance(s, int) and s == 0):
                    pe.wait_ge(gated_ready, s)
                hidden(s, buf, expert, w2_sb, ps_s[1], h2_ps)

            def transpose_gated(s):
                pe.wait_ge(gated_ready, s + 1)
                pe.wait_ge(gatedT_ready, s + 1)
                for k in range(HT):
                    mm = pe.transpose(ps_t[0][:, k * P:(k + 1) * P], gated[:, k * P:(k + 1) * P], ident[:, :])
                mm.then_inc(gatedT_ps, 1)

            def project_down(s, expert):
                pe.wait_ge(gatedT_ready, s + 2)
                pe.wait_ge(y_ready, s + 1)
                for k in range(HT):
                    mm = pe.matmul(ps_o[0][:, 0:D], gatedT[:, k, :], w3_sb[:, k, bass.ds(expert, 1), :].squeeze(1), start=(k == 0), stop=(k == HT - 1))
                mm.then_inc(y_ps, 1)

            pe.sem_inc(y_ps, 1)
            pe.wait_ge(sched_ready, 2)
            transpose_x(0, 0)
            expert = table(pe, 1, 0, NE - 1)
            first_hidden(0, 0, expert)
            second_hidden(0, 0, expert)
            transpose_x(0, 1)

            def ffn_tile(i, k):
                s = RING * i + k
                last = isinstance(s, int)
                if not (last and s + 1 >= NG):
                    ahead = table(pe, 1, s + 1, NE - 1)
                    first_hidden(s + 1, (k + 1) % 2, ahead)
                transpose_gated(s)
                if not (last and s + 1 >= NG):
                    second_hidden(s + 1, (k + 1) % 2, ahead)
                now = table(pe, 1, s, NE - 1)
                if not (last and s + 2 >= NG):
                    transpose_x(i, k + 2)
                project_down(s, now)

            with pe.Fori(0, FULL // RING) as i:
                for k in range(RING):
                    ffn_tile(i, k)
            there = tiles_there(pe)
            for s in range(FULL, NG):
                with pe.If(there > s):
                    ffn_tile(s // RING, s % RING)


_INS = ["x", "ctx_1024", "mask_1x1xSxS2_bk0", "g_xattn", "g_ffn", "L0_xattn_Wq", "L0_xattn_Wk", "L0_xattn_Wv",
        "L0_xattn_Wo", "L0_ffn_Wg", "L0_ffn_W1", "L0_ffn_W2", "L0_ffn_W3"]


def kernel(**inputs):
    import numpy as np
    import concourse.bacc as bacc
    from concourse.bass_utils import run_bass_kernel_spmd

    a = {name: np.asarray(inputs[name]) for name in _INS}
    laid_out = {
        "x": a["x"][0],
        "ctxT": a["ctx_1024"][0].T,
        "mask": a["mask_1x1xSxS2_bk0"][0, 0],
        "g_xattn": a["g_xattn"],
        "g_ffn": a["g_ffn"],
        "Wq": a["L0_xattn_Wq"],
        "Wk": a["L0_xattn_Wk"],
        "Wv": a["L0_xattn_Wv"],
        "Wo": a["L0_xattn_Wo"],
        "WgT": a["L0_ffn_Wg"].T,
        "W1T": a["L0_ffn_W1"].transpose(0, 2, 1),
        "W2T": a["L0_ffn_W2"].transpose(0, 2, 1),
        "W3T": a["L0_ffn_W3"].transpose(0, 2, 1),
    }
    nc = bacc.Bacc("TRN2", target_bir_lowering=False, num_devices=1)
    arrays, args = {}, []
    for name, v in laid_out.items():
        v = np.ascontiguousarray(v)
        arrays[name + "_dram"] = v
        args.append(nc.dram_tensor(name + "_dram", v.shape, mybir.dt.from_np(v.dtype), kind="ExternalInput").ap())
    args.append(nc.dram_tensor("out_dram", (S + P, D), F32, kind="ExternalOutput").ap())
    build(nc, *args)
    r = run_bass_kernel_spmd(nc, [arrays], core_ids=[0])
    return r.results[0]["out_dram"][:S].reshape(1, S, D)
```
